# Optimizing a Trainium2 kernel written in Bass

```python
import numpy as np
import jax
import jax.numpy as jnp

def _softmax(x, axis=-1):
    return jax.nn.softmax(x, axis=axis)

def _gelu(x):
    return jax.nn.gelu(x, approximate=True)

def _silu(x):
    return jax.nn.silu(x)

def _sigmoid(x):
    return jax.nn.sigmoid(x)

def _layernorm(x, axis=-1, eps=1e-05):
    m = jnp.mean(x, axis=axis, keepdims=True)
    v = jnp.var(x, axis=axis, keepdims=True)
    return (x - m) / jnp.sqrt(v + eps)

def _scatter_add(tgt, idx, src, axis=0):
    return tgt.at[idx].add(src)

def _segment_sum(src, seg, n):
    return jax.ops.segment_sum(src, seg, n)
kernel_name = 'mk_gnn_resnorm_d4_gnn_r32_88ebed'

def setup_inputs(seed: int=0):
    np.random.seed(seed)
    _w = jnp.asarray

    def _rec_inputs():
        import jax
        import jax.numpy as jnp
        _gk = jax.random.key(seed)
        x = -0.0005121 + 1.001 * jax.random.normal(jax.random.fold_in(_gk, 1), (3125, 32), jnp.float32)
        src = jax.random.randint(jax.random.fold_in(_gk, 2), (100000,), 0, 3125, jnp.int32)
        dst = jax.random.randint(jax.random.fold_in(_gk, 3), (100000,), 0, 3125, jnp.int32)
        _o = jnp.argsort(dst, stable=True)
        src = src[_o]
        dst = dst[_o]
        edge_attr_4 = 0.000398945 + 1.00003 * jax.random.normal(jax.random.fold_in(_gk, 12), (100000, 4), jnp.float32)
        return (x, src, dst, edge_attr_4)
    x, src, dst, edge_attr_4 = _rec_inputs()

    def _L0_gnn_setup():
        import jax, jax.numpy as jnp
        import numpy as np
        N_NODES = 3125
        N_EDGES = 50000
        IN_DIM = 32
        HID = 64
        OUT_DIM = 32
        EDGE_DIM = 4
        key = jax.random.key(seed)
        ks = jax.random.split(key, 12)
        x = jax.random.normal(ks[0], (N_NODES, IN_DIM), dtype=jnp.float32)
        edge_index = jax.random.randint(ks[1], (2, N_EDGES), 0, N_NODES, dtype=jnp.int32)
        edge_attr = jax.random.normal(ks[2], (N_EDGES, EDGE_DIM), dtype=jnp.float32)

        def lin(k, fan_in, fan_out):
            kw, kb = jax.random.split(k)
            bound = 1.0 / np.sqrt(fan_in)
            W = jax.random.uniform(kw, (fan_in, fan_out), minval=-bound, maxval=bound, dtype=jnp.float32)
            b = jax.random.uniform(kb, (fan_out,), minval=-bound, maxval=bound, dtype=jnp.float32)
            return (W, b)
        W1, b1 = lin(ks[3], 2 * IN_DIM, HID)
        W2, b2 = lin(ks[4], HID, 2 * HID)
        W3, b3 = lin(ks[5], 2 * HID, HID)
        W4, b4 = lin(ks[6], HID, OUT_DIM)
        return {'x': x, 'edge_index': edge_index, 'edge_attr': edge_attr, 'W1': W1, 'b1': b1, 'W2': W2, 'b2': b2, 'W3': W3, 'b3': b3, 'W4': W4, 'b4': b4}
    _L0_gnn_all = _L0_gnn_setup()
    _L0_gnn_in = {k: v for k, v in _L0_gnn_all.items() if k in ('W1', 'b1', 'W2', 'b2', 'W3', 'b3', 'W4', 'b4')}
    del _L0_gnn_all

    def _L1_gnn_setup():
        import jax, jax.numpy as jnp
        import numpy as np
        NUM_NODES = 3125
        EMB_DIM = 32
        NUM_EDGES = 50000
        key = jax.random.key(seed)
        k1, k2 = jax.random.split(key)
        edge_index = jax.random.randint(k1, (2, NUM_EDGES), 0, NUM_NODES, dtype=jnp.int64)
        embedding_weight = jax.random.normal(k2, (NUM_NODES, EMB_DIM), dtype=jnp.float32)
        return {'edge_index': edge_index, 'embedding_weight': embedding_weight}
    _L1_gnn_all = _L1_gnn_setup()
    _L1_gnn_in = {k: v for k, v in _L1_gnn_all.items() if k in ()}
    del _L1_gnn_all

    def _L2_gnn_setup():
        import jax, jax.numpy as jnp
        import numpy as np
        N_NODES = 3125
        key = jax.random.key(seed)
        k1, k2, k3, k4 = jax.random.split(key, 4)
        features = jax.random.normal(k1, (N_NODES, 32), dtype=jnp.float32)
        src = jax.random.randint(k2, (50000,), 0, N_NODES, dtype=jnp.int64)
        dst = jax.random.randint(k3, (50000,), 0, N_NODES, dtype=jnp.int64)
        weight = jax.random.normal(k4, (32, 32), dtype=jnp.float32) * (1.0 / np.sqrt(32.0))
        bias = jnp.zeros((32,), dtype=jnp.float32)
        return {'features': features, 'src': src, 'dst': dst, 'weight': weight, 'bias': bias}
    _L2_gnn_all = _L2_gnn_setup()
    _L2_gnn_in = {k: v for k, v in _L2_gnn_all.items() if k in ('weight', 'bias')}
    del _L2_gnn_all

    def _L3_gnn_setup():
        import jax, jax.numpy as jnp
        import numpy as np
        N_NODES = 3125
        N_EDGES = 50000
        HEADS = 8
        CH = 32

        def _gatv2(x, src, dst, Wl, Wr, att, bias):
            H, C = att.shape
            xl = (x @ Wl).reshape(-1, H, C)
            xr = (x @ Wr).reshape(-1, H, C)
            e = jax.nn.leaky_relu(xl[src] + xr[dst], 0.2)
            logits = jnp.einsum('ehc,hc->eh', e, att)
            m = jax.ops.segment_max(logits, dst, num_segments=N_NODES)
            p = jnp.exp(logits - m[dst])
            denom = jax.ops.segment_sum(p, dst, num_segments=N_NODES)
            alpha = p / denom[dst]
            out = jax.ops.segment_sum(alpha[:, :, None] * xl[src], dst, num_segments=N_NODES)
            return out.mean(axis=1) + bias

        def _bn(x, gamma, beta):
            mu = x.mean(axis=0)
            var = jnp.mean((x - mu) ** 2, axis=0)
            return (x - mu) * jax.lax.rsqrt(var + 1e-05) * gamma + beta
        key = jax.random.key(seed)
        ks = jax.random.split(key, 32)
        d = {'patch_embs': jax.random.normal(ks[0], (N_NODES, CH), dtype=jnp.float32), 'edge_index': jax.random.randint(ks[1], (2, N_EDGES), 0, N_NODES, dtype=jnp.int64 if jax.config.read('jax_enable_x64') else jnp.int32), 'edge_attr': jax.random.normal(ks[2], (N_EDGES, 4), dtype=jnp.float32)}
        s = 1.0 / np.sqrt(CH)
        for i, k0 in zip((1, 2, 3), (3, 10, 17)):
            d[f'Wl{i}'] = jax.random.normal(ks[k0 + 0], (CH, HEADS * CH), dtype=jnp.float32) * s
            d[f'Wr{i}'] = jax.random.normal(ks[k0 + 1], (CH, HEADS * CH), dtype=jnp.float32) * s
            d[f'att{i}'] = jax.random.normal(ks[k0 + 2], (HEADS, CH), dtype=jnp.float32) * s
            d[f'b{i}'] = jnp.zeros((CH,), dtype=jnp.float32)
            d[f'g{i}'] = jnp.ones((CH,), dtype=jnp.float32)
            d[f'be{i}'] = jnp.zeros((CH,), dtype=jnp.float32)
        return d
    _L3_gnn_all = _L3_gnn_setup()
    _L3_gnn_in = {k: v for k, v in _L3_gnn_all.items() if k in ('Wl1', 'Wr1', 'att1', 'b1', 'g1', 'be1', 'Wl2', 'Wr2', 'att2', 'b2', 'g2', 'be2', 'Wl3', 'Wr3', 'att3', 'b3', 'g3', 'be3')}
    del _L3_gnn_all
    return {'x': x, 'src': src, 'dst': dst, 'edge_attr_4': edge_attr_4, 'L0_gnn_W1': _L0_gnn_in['W1'], 'L0_gnn_b1': _L0_gnn_in['b1'], 'L0_gnn_W2': _L0_gnn_in['W2'], 'L0_gnn_b2': _L0_gnn_in['b2'], 'L0_gnn_W3': _L0_gnn_in['W3'], 'L0_gnn_b3': _L0_gnn_in['b3'], 'L0_gnn_W4': _L0_gnn_in['W4'], 'L0_gnn_b4': _L0_gnn_in['b4'], 'L2_gnn_weight': _L2_gnn_in['weight'], 'L2_gnn_bias': _L2_gnn_in['bias'], 'L3_gnn_Wl1': _L3_gnn_in['Wl1'], 'L3_gnn_Wr1': _L3_gnn_in['Wr1'], 'L3_gnn_att1': _L3_gnn_in['att1'], 'L3_gnn_b1': _L3_gnn_in['b1'], 'L3_gnn_g1': _L3_gnn_in['g1'], 'L3_gnn_be1': _L3_gnn_in['be1'], 'L3_gnn_Wl2': _L3_gnn_in['Wl2'], 'L3_gnn_Wr2': _L3_gnn_in['Wr2'], 'L3_gnn_att2': _L3_gnn_in['att2'], 'L3_gnn_b2': _L3_gnn_in['b2'], 'L3_gnn_g2': _L3_gnn_in['g2'], 'L3_gnn_be2': _L3_gnn_in['be2'], 'L3_gnn_Wl3': _L3_gnn_in['Wl3'], 'L3_gnn_Wr3': _L3_gnn_in['Wr3'], 'L3_gnn_att3': _L3_gnn_in['att3'], 'L3_gnn_b3': _L3_gnn_in['b3'], 'L3_gnn_g3': _L3_gnn_in['g3'], 'L3_gnn_be3': _L3_gnn_in['be3']}

def reference(x, src, dst, edge_attr_4, L0_gnn_W1, L0_gnn_b1, L0_gnn_W2, L0_gnn_b2, L0_gnn_W3, L0_gnn_b3, L0_gnn_W4, L0_gnn_b4, L2_gnn_weight, L2_gnn_bias, L3_gnn_Wl1, L3_gnn_Wr1, L3_gnn_att1, L3_gnn_b1, L3_gnn_g1, L3_gnn_be1, L3_gnn_Wl2, L3_gnn_Wr2, L3_gnn_att2, L3_gnn_b2, L3_gnn_g2, L3_gnn_be2, L3_gnn_Wl3, L3_gnn_Wr3, L3_gnn_att3, L3_gnn_b3, L3_gnn_g3, L3_gnn_be3):
    import jax
    import jax.numpy as jnp

    def _L0_gnn_ref(x, edge_index, edge_attr, W1, b1, W2, b2, W3, b3, W4, b4):
        import jax, jax.numpy as jnp
        import numpy as np
        N_NODES = 3125
        N_EDGES = 50000
        IN_DIM = 32
        HID = 64
        OUT_DIM = 32
        EDGE_DIM = 4
        j_idx = edge_index[0]
        i_idx = edge_index[1]
        x_j = x[j_idx]
        x_i = x[i_idx]
        msg = jnp.concatenate([x_i, x_j - x_i], axis=-1)
        h = jax.nn.relu(msg @ W1 + b1)
        h = jax.nn.relu(h @ W2 + b2)
        h = jax.nn.relu(h @ W3 + b3)
        m = h @ W4 + b4
        s = jax.ops.segment_sum(m, i_idx, num_segments=N_NODES)
        cnt = jax.ops.segment_sum(jnp.ones((m.shape[0],), m.dtype), i_idx, num_segments=N_NODES)
        return s / jnp.maximum(cnt, 1.0)[:, None]

    def _L1_gnn_ref(edge_index, embedding_weight):
        import jax, jax.numpy as jnp
        import numpy as np
        NUM_NODES = 3125
        EMB_DIM = 32
        NUM_EDGES = 50000
        row, col = (edge_index[0], edge_index[1])
        n = embedding_weight.shape[0]
        ones = jnp.ones(row.shape[0], dtype=embedding_weight.dtype)
        deg = jax.ops.segment_sum(ones, col, num_segments=n)
        deg_inv_sqrt = jnp.where(deg > 0, jax.lax.rsqrt(jnp.maximum(deg, 1.0)), 0.0)
        norm = deg_inv_sqrt[row] * deg_inv_sqrt[col]
        msgs = embedding_weight[row] * norm[:, None]
        out = jax.ops.segment_sum(msgs, col, num_segments=n)
        return out

    def _L2_gnn_ref(features, src, dst, weight, bias):
        import jax, jax.numpy as jnp
        import numpy as np
        N_NODES = 3125
        n = features.shape[0]
        ones = jnp.ones(src.shape[0], dtype=features.dtype)
        deg_out = jax.ops.segment_sum(ones, src, num_segments=n)
        deg_in = jax.ops.segment_sum(ones, dst, num_segments=n)
        norm_src = jax.lax.rsqrt(jnp.maximum(deg_out, 1.0))
        norm_dst = jax.lax.rsqrt(jnp.maximum(deg_in, 1.0))
        h = features * norm_src[:, None]
        msgs = h[src]
        agg = jax.ops.segment_sum(msgs, dst, num_segments=n)
        agg = agg * norm_dst[:, None]
        out = agg @ weight + bias
        return jax.nn.relu(out)

    def _L3_gnn_ref(patch_embs, edge_index, edge_attr, Wl1, Wr1, att1, b1, g1, be1, Wl2, Wr2, att2, b2, g2, be2, Wl3, Wr3, att3, b3, g3, be3):
        import jax, jax.numpy as jnp
        import numpy as np
        N_NODES = 3125
        N_EDGES = 50000
        HEADS = 8
        CH = 32

        def _gatv2(x, src, dst, Wl, Wr, att, bias):
            H, C = att.shape
            xl = (x @ Wl).reshape(-1, H, C)
            xr = (x @ Wr).reshape(-1, H, C)
            e = jax.nn.leaky_relu(xl[src] + xr[dst], 0.2)
            logits = jnp.einsum('ehc,hc->eh', e, att)
            m = jax.ops.segment_max(logits, dst, num_segments=N_NODES)
            p = jnp.exp(logits - m[dst])
            denom = jax.ops.segment_sum(p, dst, num_segments=N_NODES)
            alpha = p / denom[dst]
            out = jax.ops.segment_sum(alpha[:, :, None] * xl[src], dst, num_segments=N_NODES)
            return out.mean(axis=1) + bias

        def _bn(x, gamma, beta):
            mu = x.mean(axis=0)
            var = jnp.mean((x - mu) ** 2, axis=0)
            return (x - mu) * jax.lax.rsqrt(var + 1e-05) * gamma + beta
        loop = jnp.arange(N_NODES, dtype=edge_index.dtype)
        src = jnp.concatenate([edge_index[0], loop])
        dst = jnp.concatenate([edge_index[1], loop])
        x = patch_embs
        x = _bn(jax.nn.leaky_relu(_gatv2(x, src, dst, Wl1, Wr1, att1, b1), 0.01) + x, g1, be1)
        x = _bn(jax.nn.leaky_relu(_gatv2(x, src, dst, Wl2, Wr2, att2, b2), 0.01) + x, g2, be2)
        x = _bn(_gatv2(x, src, dst, Wl3, Wr3, att3, b3) + x, g3, be3)
        return x
    edge_index = jnp.stack([src, dst])
    x = _layernorm(x + _L0_gnn_ref(x, edge_index, edge_attr_4, L0_gnn_W1, L0_gnn_b1, L0_gnn_W2, L0_gnn_b2, L0_gnn_W3, L0_gnn_b3, L0_gnn_W4, L0_gnn_b4), axis=-1)
    x = _layernorm(x + _L1_gnn_ref(edge_index, x), axis=-1)
    x = _layernorm(x + _L2_gnn_ref(x, src, dst, L2_gnn_weight, L2_gnn_bias), axis=-1)
    x = _layernorm(x + _L3_gnn_ref(x, edge_index, edge_attr_4, L3_gnn_Wl1, L3_gnn_Wr1, L3_gnn_att1, L3_gnn_b1, L3_gnn_g1, L3_gnn_be1, L3_gnn_Wl2, L3_gnn_Wr2, L3_gnn_att2, L3_gnn_b2, L3_gnn_g2, L3_gnn_be2, L3_gnn_Wl3, L3_gnn_Wr3, L3_gnn_att3, L3_gnn_b3, L3_gnn_g3, L3_gnn_be3), axis=-1)
    return x

_drawn_inputs = setup_inputs


def setup_inputs(seed=0):
    import zlib

    import numpy as np

    out = dict(_drawn_inputs(seed))
    spreads = {'L2_gnn_bias': (0.0, 0.1),
     'L3_gnn_b1': (0.0, 0.504),
     'L3_gnn_g1': (1.0, 0.6),
     'L3_gnn_be1': (0.0, 0.8),
     'L3_gnn_b2': (0.0, 0.518),
     'L3_gnn_g2': (1.0, 0.6),
     'L3_gnn_be2': (0.0, 0.8),
     'L3_gnn_b3': (0.0, 0.8),
     'L3_gnn_g3': (1.0, 0.2),
     'L3_gnn_be3': (0.0, 0.1)}
    factors = {'L0_gnn_W1': 2.904,
     'L0_gnn_b1': 8.0,
     'L0_gnn_b2': 4.197,
     'L3_gnn_Wr1': 5.673,
     'L3_gnn_att1': 3.201,
     'L3_gnn_Wr2': 5.974,
     'L3_gnn_att2': 2.978,
     'L3_gnn_Wr3': 3.621}
    for name, (base, spread) in spreads.items():
        noise = np.random.default_rng([zlib.crc32(name.encode()), seed]).standard_normal(out[name].shape)
        drawn = base * np.exp(spread * noise) if base else spread * noise
        out[name] = jnp.asarray(drawn.astype(out[name].dtype))
    for name, factor in factors.items():
        out[name] = (out[name] * factor).astype(out[name].dtype)
    return out
```

```python
from contextlib import ExitStack

import numpy as np

import concourse.bass as bass
from concourse import mybir

ALU = mybir.AluOpType
ACT = mybir.ActivationFunctionType
AX = mybir.AxisListType
F32 = mybir.dt.float32
BF16 = mybir.dt.bfloat16
I32 = mybir.dt.int32

P = 128
N = 3125
C = 32
E = 100000
W = -(-N // P)
LAST = N - (W - 1) * P
BLOCK = 256
BLOCKS = -(-E // BLOCK)
STEPS = -(-(BLOCKS + W - 1) // 8) * 8
SLOTS = 2 * STEPS
G = SLOTS // 8
HALF = G // 2
ROWS = 4
NO_NODE = 8191
HID = 64
H = 8
HC = H * C
LAYERS = 3
JB = 16
SG = SLOTS // JB
BIG = 1e30
EPS = 1e-5
DVE_SLOTS = 5
NT = -(-(W * P) // 512)
YT = -(-2 * W // 4)
assert G % 2 == 0 and SLOTS % JB == 0 and SG % 4 == 0


def build(nc, x, edge_blocks, L0, W_gcn, b_gcn, gat, out):
    with ExitStack() as ctx:
        def sb(name, shape, dt=F32):
            return ctx.enter_context(nc.sbuf_tensor(name, shape, dt))

        def sem(name):
            return ctx.enter_context(nc.semaphore(name))

        ps = ctx.enter_context(nc.psum_tensor("ps", [P, 8, 512], F32))

        table = nc.dram_tensor("table", [W * P, C], F32).ap()
        parts_dram = nc.dram_tensor("parts_dram", [W, P, 3 * C], BF16).ap()
        turned_dram = nc.dram_tensor("turned_dram", [G, P, 8 * P], BF16).ap()
        xs_dram = nc.dram_tensor("xs_dram", [G, P, 16 * C], F32).ap()

        X = sb("X", [P, W, C])
        T1 = sb("T1", [P, W, C])
        T2 = sb("T2", [P, W, C])
        parts = sb("parts", [P, W, 3, C], BF16)
        nodecol = sb("nodecol", [P, 12, W])
        acc = sb("acc", [P, W, 272])
        src = sb("src", [P, SLOTS + 16])
        dloc = sb("dloc", [P, SLOTS])
        gone = sb("gone", [P, SLOTS])
        last = sb("last", [P, SLOTS])
        logit = sb("logit", [P, SLOTS, H])
        order1 = sb("order1", [P, SG, P])
        order2 = sb("order2", [P, SG, P])
        newF = sb("newF", [P, SG, P], BF16)
        newR = sb("newR", [P, SG, P], BF16)
        packed = sb("packed", [1, G], I32)
        idx = sb("idx", [P, 2, 8], I32)
        rows = sb("rows", [P, 2, 8, 2, C])
        hot = sb("hot", [P, 2, 8, P])
        turned = sb("turned", [P, 2, 8 * P], BF16)
        xwin = sb("xwin", [P, 2, 4, 3 * C], BF16)
        xT = sb("xT", [P, 2, 512])
        ident = sb("ident", [P, P])
        iota = sb("iota", [P, P])
        ones = sb("ones", [P, P])
        w1 = sb("w1", [P, HID])
        w2 = sb("w2", [P, 2 * HID])
        w3 = sb("w3", [P, HID])
        w4 = sb("w4", [HID, C])
        bcol = sb("bcol", [P, 2])
        b3row = sb("b3row", [P, HID])
        b4row = sb("b4row", [P, C])
        wg = sb("wg", [C, C])
        bgrow = sb("bgrow", [P, C])
        wcat = [sb(f"wcat{l}", [P, HC]) for l in range(LAYERS)]
        wsum = [sb(f"wsum{l}", [C, HC]) for l in range(LAYERS)]
        wstk = [sb(f"wstk{l}", [P, 2, C]) for l in range(LAYERS)]
        attrow = [sb(f"attrow{l}", [P, HC]) for l in range(LAYERS)]
        attcol = [sb(f"attcol{l}", [P, 2]) for l in range(LAYERS)]
        abd = [sb(f"abd{l}", [P, 2, H]) for l in range(LAYERS)]
        wlin = [sb(f"wlin{l}", [P, H]) for l in range(LAYERS)]
        wlinsum = [sb(f"wlinsum{l}", [C, H]) for l in range(LAYERS)]
        brow = [sb(f"brow{l}", [P, 3, C]) for l in range(LAYERS)]
        w1less = sb("w1less", [P, HID])
        zeros = sb("zeros", [P, P], BF16)
        headmask = sb("headmask", [P, 2, H])
        lself = sb("lself", [P, W, H])
        bn = sb("bn", [P, 3, C])
        carry = sb("carry", [1, 4, P])
        carrycol = sb("carrycol", [P, 4])

        X0 = sb("X0", [P, W, C])
        root = sb("root", [P, 2 * C])
        lastmask = sb("lastmask", [P, 1])
        empty = sb("empty", [P, W])
        block_no = sb("block_no", [P, 4], I32)
        win = sb("win", [P, 16, W + 1])
        win_i = sb("win_i", [P, 2, W + 1], I32)
        anyreset = sb("anyreset", [P, 2])
        resetrow = sb("resetrow", [1, 2, P])
        powers = [nodecol[:, 2, :], nodecol[:, 4, :], nodecol[:, 2, :], nodecol[:, 7, :], nodecol[:, 2, :]] \
            + [bn[:, 1, :]] * LAYERS + [nodecol[:, 2, :]]

        hotf = hot[:, :, :, :].rearrange("p b j n -> p (b j n)")
        selfcol = hotf[:, 0:4 * W * H].rearrange("p (k w h) -> p k w h", k=4, w=W)
        rest = hotf[:, 4 * W * H:4 * W * H + W * C].rearrange("p (w c) -> p w c", w=W)
        accf = acc[:, :, :].rearrange("p w c -> p (w c)")
        dst_i = accf[:, 0:1024].bitcast(I32)
        dst_all = accf[:, 1024:2048]
        junk = accf[:, 2048:3072]
        step_no = accf[:, 3072:3072 + STEPS + 4]
        step_win = accf[:, 3500:3500 + STEPS + 4]
        step_blk = accf[:, 3930:3930 + STEPS + 4]
        step_tmp = accf[:, 4360:4360 + STEPS + 4]
        spreads = [t.rearrange("p (g j h) -> p g j h", g=SG, j=JB)
                   for t in (logit[:, :, :].rearrange("p s h -> p (s h)"), accf[:, 0:SLOTS * H])]
        staged = hotf[:, 0:1024].rearrange("p (k c) -> p k c", k=2)
        o1 = order1[:, :, :].rearrange("p a b -> p (a b)")
        o2 = order2[:, :, :].rearrange("p a b -> p (a b)")
        blocks_i = order1[:, :, :].rearrange("p a b -> p (a b)")[:, 0:4 * 1024].bitcast(I32) \
            .rearrange("p (g r) -> p g r", g=4)
        blocks_f = o2[:, 0:4 * 1024].rearrange("p (g r) -> p g r", g=4)
        dstf = hot[:, 0, :, :].rearrange("p j n -> p (j n)")[:, 0:SLOTS]
        prevf = hot[:, 1, :, :].rearrange("p j n -> p (j n)")[:, 0:SLOTS]
        nodeslots = o1[:, 4 * 1024:4 * 1024 + 2 * SLOTS].rearrange("p (k s) -> p k s", k=2)
        nextf = nodeslots[:, 0, :]
        valid = nodeslots[:, 1, :]
        src_a, src_b = nodeslots[:, 0, :], nodeslots[:, 1, :]
        srchot = o1[:, 0:8 * (P + W)].bitcast(BF16).rearrange("p (r j c) -> p r j c", r=2, j=8)
        sltmp = xT[:, :, :].rearrange("p a b -> p (a b)")[:, 0:SLOTS]
        nodeT = o2[0:HID, 0:W * P]
        h1 = o1[:, 0:512]
        h2 = o1[:, 512:1536]
        h3 = o1[:, 1536:1536 + 8 * (HID + 1)].rearrange("p (j c) -> p j c", j=8)
        zed = o1[:, 0:2048].rearrange("p (k c) -> p k c", k=4)
        px = [o1[:, k * 2176:(k + 1) * 2176].rearrange("p (j c) -> p j c", j=8) for k in range(2)]
        endmax = order2[:, :, :].rearrange("p a b -> p (a b)").rearrange("p (s h) -> p s h", h=H)
        ysum = order2[:, :, :].rearrange("p a b -> p (a b)")[:, 0:W * HC].rearrange("p (w k) -> p w k", w=W)
        yself = order1[:, :, :].rearrange("p a b -> p (a b)")[:, 0:W * HC].rearrange("p (w k) -> p w k", w=W)
        yT = logit[:, :, :].rearrange("p s h -> p (s h)")
        znode = logit[:, :, :].rearrange("p s h -> p (s h)")

        x_in, x_zeroed, zeros_made = sem("x_in"), sem("x_zeroed"), sem("zeros_made")
        exp_asked, exp_done = sem("exp_asked"), sem("exp_done")
        weights_in = sem("weights_in")
        edges_in = sem("edges_in")
        consts_made = sem("consts_made")
        weights_made = sem("weights_made")
        counts_made = sem("counts_made")
        counts_summed = sem("counts_summed")
        steps_made = sem("steps_made")
        blocks_in = sem("blocks_in")
        blocks_floated = sem("blocks_floated")
        slots_turned = sem("slots_turned")
        slots_copied = sem("slots_copied")
        flags_spread = sem("flags_spread")
        flags_turned = sem("flags_turned")
        flags_copied = sem("flags_copied")
        table_ready = sem("table_ready")
        table_stored = sem("table_stored")
        parts_ready = sem("parts_ready")
        parts_stored = sem("parts_stored")
        begun, begun_pe = sem("begun"), sem("begun_pe")
        idx_ready = sem("idx_ready")
        gathered = [sem(f"gathered{b}") for b in range(2)]
        hot_made = sem("hot_made")
        px_made_pool = sem("px_made_pool")
        hot_turned = sem("hot_turned")
        turned_made = sem("turned_made")
        turned_stored = [sem(f"turned_stored{b}") for b in range(2)]
        turned_in = [sem(f"turned_in{b}") for b in range(2)]
        xwin_in = [sem(f"xwin_in{b}") for b in range(2)]
        xd_summed = sem("xd_summed")
        xd_copied = sem("xd_copied")
        x_turned = sem("x_turned")
        xT_copied = sem("xT_copied")
        h1_summed, h1_made = sem("h1_summed"), sem("h1_made")
        h2_summed, h2_made = sem("h2_summed"), sem("h2_made")
        h3_summed, h3_made = sem("h3_summed"), sem("h3_made")
        agg_summed = sem("agg_summed")
        acc_added = sem("acc_added")
        srchot_made, degree_summed = sem("srchot_made"), sem("degree_summed")
        z_summed, z_made = sem("z_summed"), sem("z_made")
        logit_summed, logit_made = sem("logit_summed"), sem("logit_made")
        xs_stored = [sem(f"xs_stored{b}") for b in range(2)]
        xs_in = [sem(f"xs_in{b}") for b in range(2)]
        px_made, p_made = sem("px_made"), sem("p_made")
        root_asked, root_done = sem("root_asked"), sem("root_done")
        order_staged = sem("order_staged")
        order_turned, order_copied = sem("order_turned"), sem("order_copied")
        back_asked, back_turned, back_copied = sem("back_asked"), sem("back_turned"), sem("back_copied")
        carry_asked, carry_turned = sem("carry_asked"), sem("carry_turned")
        small_asked, small_turned, small_copied = sem("small_asked"), sem("small_turned"), sem("small_copied")
        small_summed = sem("small_summed")
        zn_summed, zn_made, self_summed = sem("zn_summed"), sem("zn_made"), sem("self_summed")
        y_asked, y_turned, y_copied, y_summed = sem("y_asked"), sem("y_turned"), sem("y_copied"), sem("y_summed")
        bn_asked, bn_summed = sem("bn_asked"), sem("bn_summed")
        h3_biased, linked = sem("h3_biased"), sem("linked")
        out_stored = sem("out_stored")

        block = ctx.enter_context(nc.Block())

        def pipelined(eng, both, front, back):
            front(0, 0)
            with eng.Fori(0, HALF - 1) as i:
                both((i, 1), (i, 0))
                both((i + 1, 0), (i, 1))
            both((HALF - 1, 1), (HALF - 1, 0))
            back(HALF - 1, 1)

        n_gat = {3 + l: l for l in range(LAYERS)}

        def pool_gathers(pool, pas):
            def group(i, b):
                done = pas * G + 2 * i + b
                pool.wait_ge(table_stored, 16 * (pas + 1))
                pool.wait_ge(idx_ready, done + 1)
                if pas == 0:
                    pool.wait_ge(x_turned, 2 * i + b + 1)
                elif pas < 3:
                    pool.wait_ge(agg_summed, done - 1)
                else:
                    pool.wait_ge(x_turned, (pas - 2) * G + 2 * i + b + 1)
                    pool.wait_ge(xs_stored[b], 16 * ((pas - 3) * HALF + i))
                pool.sem_inc(begun, 1)
                for j in range(8):
                    pool.indirect_dma_start(
                        rows[:, b, j, 0, :], None, table,
                        bass.IndirectOffsetOnAxis(ap=idx[:, b, j:j + 1], axis=0)).then_inc(gathered[b], 16)
            with pool.Fori(0, HALF) as i:
                group(i, 0)
                group(i, 1)

        def weigh(eng, b, lo, hi):
            return eng.tensor_tensor(
                px[b][:, lo:hi, 0:HC].rearrange("p j (h c) -> p j h c", h=H),
                px[b][:, lo:hi, HC:HC + H].unsqueeze(3).broadcast_to([P, hi - lo, H, C]),
                rows[:, b, lo:hi, 0, :].unsqueeze(2).broadcast_to([P, hi - lo, H, C]), ALU.mult)

        def pool_weighs(pool, l):
            def group(i, b):
                g = l * G + 2 * i + b
                pool.wait_ge(p_made, 2 * g + 2)
                pool.wait_ge(xs_in[b], 16 * (l * HALF + i + 1))
                weigh(pool, b, DVE_SLOTS, 8).then_inc(px_made_pool, 1)
            with pool.Fori(0, HALF) as i:
                group(i, 0)
                group(i, 1)

        @block.gpsimd
        def _(pool):
            pool.iota(iota[:, :], [[1, P]], 0, 0, allow_small_or_imprecise_dtypes=True).then_inc(consts_made, 1)
            pool.memset(ones[:, :], 1.0).then_inc(consts_made, 1)
            pool.wait_ge(consts_made, 2)
            pool.affine_select(ident[:, :], ones[:, :], [[-1, P]], ALU.is_equal, 0.0, 0, 1).then_inc(consts_made, 1)
            pool.iota(step_no[:, 0:STEPS], [[1, STEPS]], 0, 0, allow_small_or_imprecise_dtypes=True).then_inc(consts_made, 1)
            pool.iota(step_no[:, STEPS:STEPS + 4], [[P, 4]], 0, 1, allow_small_or_imprecise_dtypes=True
                      ).then_inc(consts_made, 1)
            pool.iota(headmask[:, :, :], [[P, 2], [-C, H]], 0, 1, allow_small_or_imprecise_dtypes=True
                      ).then_inc(consts_made, 1)
            pool.iota(lastmask[:, :], [[0, 1]], 0, 1, allow_small_or_imprecise_dtypes=True).then_inc(consts_made, 1)
            pool.wait_ge(steps_made, 1)
            for g in range(4):
                pool.indirect_dma_start(
                    blocks_i[:, g, :], None, edge_blocks,
                    bass.IndirectOffsetOnAxis(ap=block_no[:, g:g + 1], axis=0)).then_inc(blocks_in, 16)
            pool_gathers(pool, 0)
            pool_gathers(pool, 1)
            pool_gathers(pool, 2)
            for l in range(LAYERS):
                pool_gathers(pool, 3 + l)
                pool_weighs(pool, l)

        def window_of(eng, code, k):
            return nc.s_assert_within(eng.snap((code >> (5 * k)) & 31), 0, W - 1,
                                      skip_runtime_bounds_check_because="DVE clamps the windows that it packs")

        def load_windows(sp, which, i, b):
            done = which * G + 2 * i + b
            sp.wait_ge(xd_summed, done + 1)
            code = sp.value_load(packed[0:1, bass.ds(2 * i + b, 1)], min_val=0, max_val=(1 << 20) - 1)
            for k in range(4):
                w = window_of(sp, code, k)
                sp.dma_start(xwin[:, b, k, :], parts_dram[bass.ds(w, 1), :, :].rearrange("a p c -> (a p) c")
                             ).then_inc(xwin_in[b], 16)

        def sp_pass0(sp):
            sp.wait_ge(parts_stored, 16)
            def group(i, b):
                load_windows(sp, 0, i, b)
                sp.wait_ge(turned_made, 2 * i + b + 1)
                sp.dma_start(turned_dram[bass.ds(2 * i + b, 1), :, :].rearrange("a p c -> (a p) c"),
                             turned[:, b, :]).then_inc(turned_stored[b], 16)
            with sp.Fori(0, HALF) as i:
                group(i, 0)
                group(i, 1)
            for b in range(2):
                sp.wait_ge(turned_stored[b], 16 * HALF)

        def sp_gather_side(sp, l):
            sp.wait_ge(parts_stored, 16 * (l + 2))
            def group(i, b):
                load_windows(sp, l + 1, i, b)
                sp.dma_start(turned[:, b, :], turned_dram[bass.ds(2 * i + b, 1), :, :].rearrange("a p c -> (a p) c")
                             ).then_inc(turned_in[b], 16)
                sp.wait_ge(xd_copied, (l + 1) * G + 2 * i + b + 1)
                sp.wait_ge(gathered[b], 128 * ((3 + l) * HALF + i + 1))
                sp.dma_start(xs_dram[bass.ds(2 * i + b, 1), :, :].rearrange("a p c -> (a p) c"),
                             rows[:, b, :, :, :].rearrange("p j s c -> p (j s c)")).then_inc(xs_stored[b], 16)
            with sp.Fori(0, HALF) as i:
                group(i, 0)
                group(i, 1)
            for b in range(2):
                sp.wait_ge(xs_stored[b], 16 * (l + 1) * HALF)

        def sp_sum_side(sp, l):
            sp.wait_ge(x_turned, (l + 2) * G + 2)
            def group(i, b):
                sp.wait_ge(px_made, l * G + 2 * i + b + 1)
                sp.wait_ge(px_made_pool, l * G + 2 * i + b + 1)
                sp.dma_start(rows[:, b, :, :, :].rearrange("p j s c -> p (j s c)"),
                             xs_dram[bass.ds(2 * i + b, 1), :, :].rearrange("a p c -> (a p) c")
                             ).then_inc(xs_in[b], 16)
            with sp.Fori(0, HALF) as i:
                group(i, 0)
                group(i, 1)

        def store_table(sp, n):
            sp.wait_ge(table_ready, n + 1)
            sp.dma_start(table.rearrange("(w p) c -> p w c", p=P), T1[:, :, :]).then_inc(table_stored, 16)

        def store_parts(sp, n):
            sp.wait_ge(parts_ready, n + 1)
            sp.dma_start(parts_dram.rearrange("w p c -> p w c"),
                         parts[:, :, :, :].rearrange("p w s c -> p w (s c)")).then_inc(parts_stored, 16)

        @block.sync
        def _(sp):
            full = BLOCKS // P
            sp.dma_start(dst_i[:, 0:full * BLOCK].rearrange("p (g r) -> p g r", g=full),
                         edge_blocks[0:full * P, BLOCK:2 * BLOCK].rearrange("(p g) r -> p g r", g=full)
                         ).then_inc(edges_in, 16)
            sp.wait_ge(x_zeroed, 2)
            sp.dma_start(dst_i[0:BLOCKS - full * P, full * BLOCK:(full + 1) * BLOCK],
                         edge_blocks[full * P:BLOCKS, BLOCK:2 * BLOCK]).then_inc(edges_in, 16)
            sp.dma_start(X[:, 0:W - 1, :], x[0:(W - 1) * P, :].rearrange("(w p) c -> p w c", p=P)).then_inc(x_in, 16)
            sp.dma_start(X[0:LAST, W - 1, :], x[(W - 1) * P:N, :]).then_inc(x_in, 16)
            store_table(sp, 0)
            store_parts(sp, 0)
            sp_pass0(sp)
            store_table(sp, 1)
            store_table(sp, 2)
            for l in range(LAYERS):
                store_table(sp, 3 + l)
                store_parts(sp, 1 + l)
                sp_gather_side(sp, l)
                sp_sum_side(sp, l)
            sp.wait_ge(table_ready, 4 + LAYERS)
            sp.dma_start(out[0:(W - 1) * P, :].rearrange("(w p) c -> p w c", p=P), X[:, 0:W - 1, :]).then_inc(out_stored, 16)
            sp.dma_start(out[(W - 1) * P:N, :], X[0:LAST, W - 1, :]).then_inc(out_stored, 16)
            sp.wait_ge(out_stored, 32)

        weights = [
            (w1[0:C, :], L0[0][C:2 * C, :]), (w1[2 * C:3 * C, :], L0[0][C:2 * C, :]),
            (w1[C:2 * C, :], L0[0][0:C, :]), (w1[3 * C:4 * C, :], L0[0][0:C, :]),
            (w1less[C:2 * C, :], L0[0][C:2 * C, :]), (w1less[3 * C:4 * C, :], L0[0][C:2 * C, :]),
            (w2[0:HID, :], L0[2]), (w2[HID:P, :], L0[2]), (w3[:, :], L0[4]), (w4[:, :], L0[6]),
            (bcol[0:HID, 0:1], L0[1].rearrange("(p a) -> p a", a=1)),
            (bcol[HID:P, 0:1], L0[1].rearrange("(p a) -> p a", a=1)),
            (bcol[:, 1:2], L0[3].rearrange("(p a) -> p a", a=1)),
            (b3row[:, :], L0[5].partition_broadcast(P)), (b4row[:, :], L0[7].partition_broadcast(P)),
            (wg[:, :], W_gcn), (bgrow[:, :], b_gcn.partition_broadcast(P)),
        ]
        for l, (Wl, Wr, att, bias, gamma, beta) in enumerate(gat):
            flat = att.rearrange("h c -> (h c)")
            weights += [(wcat[l][k * C:(k + 1) * C, :], (Wl, Wr)[k % 2]) for k in range(4)]
            weights += [(wsum[l][:, :], Wr), (attrow[l][:, :], flat.partition_broadcast(P)),
                        (attcol[l][:, 0:1], flat[0:P].rearrange("(p a) -> p a", a=1)),
                        (attcol[l][:, 1:2], flat[P:2 * P].rearrange("(p a) -> p a", a=1))]
            weights += [(brow[l][:, k, :], v.partition_broadcast(P)) for k, v in enumerate((bias, gamma, beta))]
            weights += [(wstk[l][q * C:(q + 1) * C, t, :], Wl[:, (4 * t + q) * C:(4 * t + q + 1) * C])
                        for q in range(4) for t in range(2)]

        def act_pass0(act):
            def front(i, b):
                g = 2 * i + b
                act.wait_ge(hot_turned, g + 1)
                act.wait_ge(turned_stored[b], 16 * i)
                act.activation(turned[:, b, :], ps[:, 0:2, :].rearrange("p k c -> p (k c)"), ACT.Copy
                               ).then_inc(turned_made, 1)

            def front2(i, b):
                act.wait_ge(x_turned, 2 * i + b + 3)
                act.activation(xT[:, b, :], ps[:, 3, :], ACT.Copy).then_inc(xT_copied, 1)

            def back(i, b):
                g = 2 * i + b
                act.wait_ge(h1_summed, g + 1)
                act.activation(h1, ps[:, 4, :], ACT.Relu, bias=bcol[:, 0:1]).then_inc(h1_made, 1)

            def back2(i, b):
                g = 2 * i + b
                act.wait_ge(h2_summed, g + 1)
                act.activation(h2, ps[:, 5:7, :].rearrange("p k c -> p (k c)"), ACT.Relu, bias=bcol[:, 1:2]
                               ).then_inc(h2_made, 1)

            def both(f, k):
                front(*f)
                back(*k)
                back2(*k)
                front2(*f)
            pipelined(act, both, lambda i, b: (front(i, b), front2(i, b)), lambda i, b: (back(i, b), back2(i, b)))

        def act_gather_side(act, l):
            base = (l + 1) * G

            def front(i, b):
                act.wait_ge(x_turned, base + 2 * i + b + 3)
                act.activation(xT[:, b, :], ps[:, 1, :], ACT.Copy).then_inc(xT_copied, 1)

            def back(i, b):
                for k in range(4):
                    act.wait_ge(z_summed, l * 4 * G + 8 * i + 4 * b + k + 1)
                    act.activation(zed[:, k, :], ps[:, 2 + k, :], ACT.Relu).then_inc(z_made, 1)

            def both(f, k):
                back(*k)
                front(*f)
            pipelined(act, both, front, back)

        def act_sum_side(act, l):
            act.wait_ge(back_copied, (l + 1) * SG // 4)
            def group(i, b):
                act.wait_ge(agg_summed, (3 + l) * G + 2 * i + b - 1)
                sl = bass.ds(16 * i + 8 * b, 8)
                act.activation(px[b][:, :, HC:HC + H], logit[:, sl, :], ACT.Exp).then_inc(p_made, 1)
                act.activation(px[b][:, :, HC + H:HC + 2 * H], endmax[:, sl, :], ACT.Copy).then_inc(p_made, 1)
            with act.Fori(0, HALF) as i:
                group(i, 0)
                group(i, 1)

        def act_small(act, n, rows_):
            act.wait_ge(small_turned, n + 1)
            for k in range(NT):
                c = min(512, W * P - 512 * k)
                act.activation(nodeT[0:rows_, 512 * k:512 * k + c], ps[0:rows_, k, 0:c], ACT.Copy
                               ).then_inc(small_copied, 1)

        def act_root(act, n):
            act.wait_ge(root_asked, n + 1)
            act.activation(root[:, 0:powers[n].shape[1]], powers[n], ACT.Sqrt).then_inc(root_done, 1)

        @block.scalar
        def _(act):
            for dst, srcw in weights:
                act.dma_start(dst, srcw).then_inc(weights_in, 16)
            for n in range(2 * SG // 4):
                act.wait_ge(flags_turned, n + 1)
                tile = (newF, newR)[n // (SG // 4)]
                k = n % (SG // 4)
                act.activation(tile[:, 4 * k:4 * k + 4, :].rearrange("p g e -> p (g e)"), ps[:, n % 8, :], ACT.Copy
                               ).then_inc(flags_copied, 1)
            act_pass0(act)
            act_small(act, 0, HID)
            for n in range(4):
                act_root(act, n)
            act_small(act, 1, C)
            act_root(act, 4)
            for l in range(LAYERS):
                act_small(act, 2 + l, C)
                for n in range(2 * NT):
                    k, t = n // 2, n % 2
                    c = min(512, W * P - 512 * k)
                    act.wait_ge(zn_summed, l * 2 * NT + n + 1)
                    act.activation(znode[:, t * W * P + 512 * k:t * W * P + 512 * k + c], ps[:, n % 8, 0:c], ACT.Relu
                                   ).then_inc(zn_made, 1)
                act_gather_side(act, l)
                act.wait_ge(logit_made, (l + 1) * G)
                view = logit[:, :, :].rearrange("p (j g) h -> p g j h", j=JB)

                def stage_order(n):
                    for k in range(4):
                        ins = act.activation(staged[:, n % 2, k * P:(k + 1) * P].rearrange("p (j h) -> p j h", h=H),
                                             view[:, 4 * n + k, :, :], ACT.Copy)
                    ins.then_inc(order_staged, 1)
                stage_order(0)
                stage_order(1)
                for n in range(SG // 4):
                    act.wait_ge(order_turned, l * (SG // 4) + n + 1)
                    if n + 2 < SG // 4:
                        stage_order(n + 2)
                    act.activation(order1[:, 4 * n:4 * n + 4, :].rearrange("p g e -> p (g e)"), ps[:, n % 4, :],
                                   ACT.Copy).then_inc(order_copied, 1)
                act_sum_side(act, l)
                act.wait_ge(exp_asked, l + 1)
                act.activation(selfcol[:, 0:2, :, :], selfcol[:, 0:2, :, :], ACT.Exp).then_inc(exp_done, 1)
                for n in range(YT):
                    c = min(4, 2 * W - 4 * n) * P
                    act.wait_ge(y_turned, l * YT + n + 1)
                    act.activation(yT[:, 512 * n:512 * n + c], ps[:, 1 + n % 6, 0:c], ACT.Copy).then_inc(y_copied, 1)
                act_root(act, 5 + l)
            act_root(act, 5 + LAYERS)

        def pe_edge_rows(pe, b, bank):
            for j in range(8):
                for s in range(3):
                    mm = pe.matmul(ps[:, bank, j * C:(j + 1) * C], turned[:, b, j * P:(j + 1) * P],
                                   xwin[:, b, j // 2, s * C:(s + 1) * C], start=(s == 0), stop=(s == 2))
            mm.then_inc(xd_summed, 1)

        def pe_turn_rows(pe, b, bank):
            for q in range(4):
                mm = pe.transpose(ps[:, bank, q * P:(q + 1) * P],
                                  rows[:, b, 2 * q:2 * q + 2, :, :].rearrange("p j s c -> p (j s c)"), ident[:, :])
            mm.then_inc(x_turned, 1)

        def pe_pass0(pe):
            def front_a(i, b):
                pe.wait_ge(hot_made, 2 * i + b + 1)
                for j in range(8):
                    mm = pe.transpose(ps[:, j // 4, (j % 4) * P:(j % 4 + 1) * P], hot[:, b, j, :], ident[:, :])
                mm.then_inc(hot_turned, 1)

            def front_b(i, b):
                pe.wait_ge(turned_made, 2 * i + b + 1)
                pe.wait_ge(xwin_in[b], 64 * (i + 1))
                pe_edge_rows(pe, b, 2)

            def front_c(i, b):
                pe.wait_ge(xd_copied, 2 * i + b + 1)
                pe.wait_ge(gathered[b], 128 * (i + 1))
                pe_turn_rows(pe, b, 3)

            def back_a(i, b):
                g = 2 * i + b
                pe.wait_ge(xT_copied, g + 1)
                pe.wait_ge(acc_added, 4 * g)
                pe.sem_inc(begun_pe, 1)
                for q in range(2):
                    mm = pe.matmul(ps[64 * q:64 * q + 64, 4, :], w1[64 * q:64 * q + 64, :], xT[64 * q:64 * q + 64, b, :],
                                   start=True, stop=True)
                mm.then_inc(h1_summed, 1)

            def back_b(i, b):
                pe.wait_ge(h1_made, 2 * i + b + 1)
                for q in range(2):
                    mm = pe.matmul(ps[:, 5 + q, :], w2[64 * q:64 * q + 64, :], h1[64 * q:64 * q + 64, :],
                                   start=True, stop=True)
                mm.then_inc(h2_summed, 1)

            def back_c(i, b):
                pe.wait_ge(h2_made, 2 * i + b + 1)
                for j in range(8):
                    at = (j % 2) * 512 + (j // 2) * P
                    mm = pe.matmul(ps[:, 7, j * HID:(j + 1) * HID], h2[:, at:at + P], w3[:, :], start=True, stop=True)
                mm.then_inc(h3_summed, 1)

            def back_d(i, b):
                pe.wait_ge(h3_made, 2 * i + b + 1)
                for j in range(8):
                    k = j // 2
                    mm = pe.matmul(ps[:, 4, k * (HID + 1):(k + 1) * (HID + 1)], hot[:, b, j, :], h3[:, j, :],
                                   start=(j % 2 == 0), stop=(j % 2 == 1))
                mm.then_inc(agg_summed, 1)

            def both(f, k):
                front_a(*f)
                back_a(*k)
                front_b(*f)
                back_b(*k)
                front_c(*f)
                back_c(*k)
                back_d(*k)
            pipelined(pe, both, lambda i, b: (front_a(i, b), front_b(i, b), front_c(i, b)),
                      lambda i, b: (back_a(i, b), back_b(i, b), back_c(i, b), back_d(i, b)))

        def pe_gcn(pe, pas):
            base = pas * G

            def group(i, b):
                g = base + 2 * i + b
                if pas == 1:
                    pe.wait_ge(srchot_made, 4 * i + 2 * b + 2)
                    for j in range(8):
                        pe.matmul(ps[:, 7, 0:W], srchot[:, b, j, 0:P], srchot[:, b, j, P:P + W],
                                  start=False, stop=False, skip_group_check=True)
                pe.wait_ge(hot_made, g + 1)
                pe.wait_ge(gathered[b], 128 * (pas * HALF + i + 1))
                pe.wait_ge(acc_added, 4 * g - 4)
                for j in range(8):
                    k = j // 2
                    mm = pe.matmul(ps[:, b, k * C:(k + 1) * C], hot[:, b, j, :], rows[:, b, j, 0, :],
                                   start=(j % 2 == 0), stop=(j % 2 == 1))
                mm.then_inc(agg_summed, 1)
            if pas == 1:
                pe.wait_ge(zeros_made, 1)
                pe.wait_ge(srchot_made, 2)
                pe.matmul(ps[:, 7, 0:W], zeros[:, 0:P], zeros[:, 0:W], start=True, stop=False, skip_group_check=True)
            with pe.Fori(0, HALF) as i:
                group(i, 0)
                group(i, 1)
            if pas == 1:
                pe.matmul(ps[:, 7, 0:W], zeros[:, 0:P], zeros[:, 0:W], start=False, stop=True,
                          skip_group_check=True).then_inc(degree_summed, 1)

        def pe_gather_side(pe, l):
            base = (l + 1) * G

            def front_a(i, b):
                pe.wait_ge(turned_in[b], 16 * (l * HALF + i + 1))
                pe.wait_ge(xwin_in[b], 64 * ((l + 1) * HALF + i + 1))
                pe_edge_rows(pe, b, 0)

            def front_b(i, b):
                pe.wait_ge(xd_copied, base + 2 * i + b + 1)
                pe.wait_ge(gathered[b], 128 * ((3 + l) * HALF + i + 1))
                pe_turn_rows(pe, b, 1)

            def back_a(i, b):
                pe.wait_ge(xT_copied, base + 2 * i + b + 1)
                for k in range(4):
                    q, t = k // 2, k % 2
                    pe.matmul(ps[:, 2 + k, :], wcat[l][64 * q:64 * q + 64, t * P:(t + 1) * P],
                              xT[64 * q:64 * q + 64, b, :], start=True, stop=True).then_inc(z_summed, 1)

            def back_b(i, b):
                g = l * G + 2 * i + b
                pe.wait_ge(z_made, 4 * g + 4)
                pe.wait_ge(logit_made, g)
                for j in range(8):
                    q, at = j % 2, (j // 2) * P
                    o = ps[:, 6 + q, (j // 2) * H:(j // 2 + 1) * H]
                    pe.matmul(o, xT[64 * q:64 * q + 64, b, at:at + P], wlin[l][64 * q:64 * q + 64, :],
                              start=True, stop=False)
                    for t in range(2):
                        mm = pe.matmul(o, zed[:, 2 * q + t, at:at + P], abd[l][:, t, :], start=False, stop=(t == 1))
                mm.then_inc(logit_summed, 1)

            def both(f, k):
                front_a(*f)
                back_a(*k)
                front_b(*f)
                back_b(*k)
            pipelined(pe, both, lambda i, b: (front_a(i, b), front_b(i, b)),
                      lambda i, b: (back_a(i, b), back_b(i, b)))

        def pe_order(pe, l):
            for n in range(SG // 4):
                if n >= 4:
                    pe.wait_ge(order_copied, l * (SG // 4) + n - 3)
                pe.wait_ge(order_staged, l * (SG // 4) + n + 1)
                for k in range(4):
                    mm = pe.transpose(ps[:, n % 4, k * P:(k + 1) * P], staged[:, n % 2, k * P:(k + 1) * P], ident[:, :])
                mm.then_inc(order_turned, 1)
            for k in range(2):
                pe.wait_ge(carry_asked, 4 * l + 2 * k + 1 + 2)
                pe.transpose(ps[0:1, 4, 0:P], carrycol[:, 2 * k:2 * k + 1], ident[:, :]).then_inc(carry_turned, 1)
                pe.wait_ge(carry_asked, 4 * l + 2 * k + 2 + 2)
                pe.transpose(ps[:, 5, 0:1], carry[0:1, 2 * k + 1, :], ident[0:1, 0:1]).then_inc(carry_turned, 1)
            pe.wait_ge(back_asked, l + 1)
            for n in range(SG // 4):
                if n >= 4:
                    pe.wait_ge(back_copied, l * (SG // 4) + n - 3)
                for k in range(4):
                    mm = pe.transpose(ps[:, n % 4, k * P:(k + 1) * P], order1[:, 4 * n + k, :], ident[:, :])
                mm.then_inc(back_turned, 1)

        def pe_sum_side(pe, l):
            def group(i, b):
                g = l * G + 2 * i + b
                pe.wait_ge(hot_made, 3 * G + g + 1)
                pe.wait_ge(px_made, g + 3)
                pe.wait_ge(px_made_pool, g + 3)
                pe.wait_ge(acc_added, 12 * G + 4 * g - 4)
                for j in range(8):
                    mm = pe.matmul(ps[:, 4 * b + j // 2, 0:HC + 2 * H], hot[:, b, j, :], px[b][:, j, :],
                                   start=(j % 2 == 0), stop=(j % 2 == 1))
                mm.then_inc(agg_summed, 1)
            with pe.Fori(0, HALF) as i:
                group(i, 0)
                group(i, 1)

        def pe_small(pe, n, src_, cols, weight):
            pe.wait_ge(small_asked, n + 1)
            for w in range(W):
                mm = pe.transpose(ps[0:cols, w // 4, (w % 4) * P:(w % 4 + 1) * P], src_[:, w, 0:cols], ident[:, :])
            mm.then_inc(small_turned, 1)
            pe.wait_ge(small_copied, NT * (n + 1))
            if weight is not None:
                for w in range(W):
                    mm = pe.matmul(out_at(w), nodeT[0:cols, w * P:(w + 1) * P], weight, start=True, stop=True)
                mm.then_inc(small_summed, 1)

        def out_at(w):
            return ps[:, 7, w * C:(w + 1) * C] if w < 16 else ps[:, 0, (w - 16) * C:(w - 15) * C]

        def pe_self_logits(pe, l):
            for n in range(2 * NT):
                k, t = n // 2, n % 2
                c = min(512, W * P - 512 * k)
                if n >= 8:
                    pe.wait_ge(zn_made, l * 2 * NT + n - 7)
                pe.matmul(ps[:, n % 8, 0:c], wsum[l][:, t * P:(t + 1) * P], nodeT[0:C, 512 * k:512 * k + c],
                          start=True, stop=True).then_inc(zn_summed, 1)
            pe.wait_ge(zn_made, (l + 1) * 2 * NT)
            for w in range(W):
                o = ps[:, 7, w * H:(w + 1) * H]
                pe.matmul(o, nodeT[0:C, w * P:(w + 1) * P], wlinsum[l][:, :], start=True, stop=False)
                for t in range(2):
                    mm = pe.matmul(o, znode[:, (t * W + w) * P:(t * W + w + 1) * P], abd[l][:, t, :],
                                   start=False, stop=(t == 1))
            mm.then_inc(self_summed, 1)

        def pe_attention_out(pe, l):
            pe.wait_ge(y_asked, l + 1)
            for n in range(YT):
                if n >= 6:
                    pe.wait_ge(y_copied, l * YT + n - 5)
                for k in range(4 * n, min(4 * n + 4, 2 * W)):
                    w, t = k // 2, k % 2
                    mm = pe.transpose(ps[:, 1 + n % 6, (k % 4) * P:(k % 4 + 1) * P], ysum[:, w, t * P:(t + 1) * P],
                                      ident[:, :])
                mm.then_inc(y_turned, 1)
            pe.wait_ge(y_copied, (l + 1) * YT)
            for w in range(W):
                for t in range(2):
                    mm = pe.matmul(out_at(w), yT[:, (2 * w + t) * P:(2 * w + t + 1) * P], wstk[l][:, t, :],
                                   start=(t == 0), stop=(t == 1))
            mm.then_inc(y_summed, 1)
            for s in range(2):
                pe.wait_ge(bn_asked, 2 * l + s + 1)
                for w in range(W):
                    mm = pe.matmul(ps[:, 1 + s, 0:C], ones[:, :], rest[:, w, :], start=(w == 0), stop=(w == W - 1))
                mm.then_inc(bn_summed, 1)

        @block.tensor
        def _(pe):
            pe.sem_inc(xd_summed, 2)
            pe.sem_inc(x_turned, 2)
            pe.wait_ge(consts_made, 7)
            pe.wait_ge(counts_made, 1)
            pe.matmul(ps[:, 0, 0:W - 1], ones[:, :], win[:, 0, 1:W], start=True, stop=True).then_inc(counts_summed, 1)
            pe.wait_ge(blocks_floated, 1)
            for g in range(4):
                for rp in range(2):
                    for k in range(4):
                        r, hf = 2 * rp + k // 2, k % 2
                        at = r * BLOCK + hf * P
                        mm = pe.transpose(ps[:, 2 * g + rp, k * P:(k + 1) * P], blocks_f[:, g, at:at + P], ident[:, :])
                    mm.then_inc(slots_turned, 1)
            pe.wait_ge(flags_spread, 1)
            for n in range(2 * SG // 4):
                spread = spreads[n // (SG // 4)].rearrange("p g j h -> p g (j h)")
                if n >= 8:
                    pe.wait_ge(flags_copied, n - 7)
                for k in range(4):
                    mm = pe.transpose(ps[:, n % 8, k * P:(k + 1) * P], spread[:, 4 * (n % (SG // 4)) + k, :], ident[:, :])
                mm.then_inc(flags_turned, 1)
            pe.wait_ge(flags_copied, 2 * SG // 4)
            for k in range(2):
                pe.wait_ge(carry_asked, 1)
                pe.transpose(ps[0:1, k, 0:P], anyreset[:, k:k + 1], ident[:, :]).then_inc(carry_turned, 1)
            pe.wait_ge(carry_asked, 2)
            pe.wait_ge(weights_made, 1)
            pe_pass0(pe)
            pe_small(pe, 0, acc, HID, w4[:, :])
            pe_gcn(pe, 1)
            pe_gcn(pe, 2)
            pe_small(pe, 1, T1, C, wg[:, :])
            for l in range(LAYERS):
                pe_small(pe, 2 + l, X, C, None)
                pe_self_logits(pe, l)
                pe_gather_side(pe, l)
                pe_order(pe, l)
                pe_sum_side(pe, l)
                pe_attention_out(pe, l)

        def wide(ap, cols):
            return ap.unsqueeze(2).broadcast_to([ap.shape[0], ap.shape[1], cols])

        def down(ap, k):
            return ap.unsqueeze(1).broadcast_to([ap.shape[0], k, ap.shape[1]])

        @block.vector
        def _(v):
            chain = [0]

            def link(ins):
                chain[0] += 1
                ins.then_inc(linked, 1)
                v.wait_ge(linked, chain[0])

            def tt(o, a, b, op):
                link(v.tensor_tensor(o, a, b, op))

            def ts(o, a, s1, s2, op0, op1=ALU.bypass):
                link(v.tensor_scalar(o, a, s1, s2, op0, op1))

            def stt(o, a, s_, b, op0, op1):
                link(v.scalar_tensor_tensor(o, a, s_, b, op0, op1))

            def cp(o, a):
                link(v.tensor_copy(o, a))

            asked = [0]

            def rsqrt():
                x_ = powers[asked[0]]
                asked[0] += 1
                v.sem_inc(root_asked, 1)
                v.wait_ge(root_done, asked[0])
                r_, t_ = root[:, 0:x_.shape[1]], root[:, C:C + x_.shape[1]]
                link(v.reciprocal(r_, r_))
                tt(t_, x_, r_, ALU.mult)
                tt(t_, t_, r_, ALU.mult)
                ts(t_, t_, -0.5, 1.5, ALU.mult, ALU.add)
                tt(x_, r_, t_, ALU.mult)

            def layernorm(of):
                mean, var = nodecol[:, 1, :], nodecol[:, 2, :]
                link(v.tensor_reduce(mean, of, AX.X, ALU.add))
                ts(mean, mean, 1.0 / C, None, ALU.mult)
                tt(T2[:, :, :], of, wide(mean, C), ALU.subtract)
                tt(rest[:, :, :], T2[:, :, :], T2[:, :, :], ALU.mult)
                link(v.tensor_reduce(var, rest[:, :, :], AX.X, ALU.add))
                ts(var, var, 1.0 / C, EPS, ALU.mult, ALU.add)
                rsqrt()
                tt(X[:, :, :], T2[:, :, :], wide(var, C), ALU.mult)

            def give_table(n):
                v.sem_inc(table_ready, 1)

            def give_parts():
                cp(parts[:, :, 0, :], X[:, :, :])
                tt(T2[:, :, :], X[:, :, :], parts[:, :, 0, :], ALU.subtract)
                cp(parts[:, :, 1, :], T2[:, :, :])
                tt(T2[:, :, :], T2[:, :, :], parts[:, :, 1, :], ALU.subtract)
                cp(parts[:, :, 2, :], T2[:, :, :])
                v.sem_inc(parts_ready, 1)

            def out_parts():
                return [(slice(0, 16), ps[:, 7, :].rearrange("p (w c) -> p w c", c=C)),
                        (slice(16, W), ps[:, 0, 0:(W - 16) * C].rearrange("p (w c) -> p w c", c=C))]

            def make_hot(i, b):
                v.tensor_tensor(hot[:, b, :, :], wide(dloc[:, bass.ds(16 * i + 8 * b, 8)], P),
                                down(iota[:, :], 8), ALU.is_equal).then_inc(hot_made, 1)

            def stage(pas, i, b):
                v.wait_ge(gathered[b], 128 * (pas * HALF + i + 1))
                v.tensor_copy(idx[:, b, :], src[:, bass.ds(16 * i + 8 * b + 16, 8)]).then_inc(idx_ready, 1)

            def add_steps(pas, i, b, banks, cols):
                g = pas * G + 2 * i + b
                v.wait_ge(agg_summed, g + 1)
                code = v.value_load(packed[0:1, bass.ds(2 * i + b, 1)], min_val=0, max_val=(1 << 20) - 1)
                for k in range(4):
                    w = window_of(v, code, k)
                    at = acc[:, bass.ds(w, 1), 0:cols].rearrange("p a c -> p (a c)")
                    v.wait_ge(acc_added, 4 * g + k)
                    v.tensor_tensor(at, at, banks[k], ALU.add).then_inc(acc_added, 1)

            v.sem_inc(px_made_pool, 2)
            v.sem_inc(px_made, 2)
            v.memset(dst_i[:, (BLOCKS // P) * BLOCK:], NO_NODE).then_inc(x_zeroed, 1)
            v.memset(X[:, W - 1, :], 0.0).then_inc(x_zeroed, 1)
            v.memset(zeros[:, :], 0.0).then_inc(zeros_made, 1)
            v.wait_ge(edges_in, 32)
            v.wait_ge(x_zeroed, 2)
            cp(dst_all, dst_i)
            for w in range(1, W):
                link(v.tensor_scalar(junk, dst_all, float(P * w), 0.0, ALU.is_lt, ALU.add, accum_out=win[:, 0, w:w + 1]))
            v.sem_inc(counts_made, 1)
            before, blk0, blk1, steps, some = (win[:, k, :] for k in range(1, 6))
            ends, starts, shift, incr = (win[:, k, :] for k in range(6, 10))
            link(v.memset(before[:, 0:1], 0.0))
            link(v.memset(before[:, W:W + 1], float(E)))
            v.wait_ge(counts_summed, 1)
            cp(before[:, 1:W], ps[:, 0, 0:W - 1])
            cp(win_i[:, 0, :], before)
            ts(win_i[:, 0, :], win_i[:, 0, :], 8, None, ALU.arith_shift_right)
            cp(blk0, win_i[:, 0, :])
            ts(win_i[:, 1, :], before, float(BLOCK - 1), None, ALU.add)
            ts(win_i[:, 1, :], win_i[:, 1, :], 8, None, ALU.arith_shift_right)
            cp(blk1, win_i[:, 1, :])
            tt(steps[:, 0:W], blk1[:, 1:W + 1], blk0[:, 0:W], ALU.subtract)
            tt(some[:, 0:W], before[:, 1:W + 1], before[:, 0:W], ALU.is_gt)
            tt(steps[:, 0:W], steps[:, 0:W], some[:, 0:W], ALU.mult)
            v.wait_ge(consts_made, 7)
            link(v.tensor_tensor_scan(ends[:, 0:W], ones[:, 0:W], steps[:, 0:W], 0.0, ALU.mult, ALU.add))
            link(v.memset(starts[:, 0:1], 0.0))
            cp(starts[:, 1:W + 1], ends[:, 0:W])
            tt(shift, blk0, starts, ALU.subtract)
            tt(incr[:, 0:W], shift[:, 1:W + 1], shift[:, 0:W], ALU.subtract)
            link(v.memset(step_win, 0.0))
            cp(step_blk, step_no)
            for w in range(W):
                ts(step_tmp, step_no, ends[:, w:w + 1], None, ALU.is_ge)
                tt(step_win, step_win, step_tmp, ALU.add)
                stt(step_blk, step_tmp, incr[:, w:w + 1], step_blk, ALU.mult, ALU.add)
            ts(step_blk, step_blk, float(BLOCKS - 1), 0.0, ALU.min, ALU.max)
            cp(block_no[:, :], step_blk[:, STEPS:STEPS + 4])
            v.sem_inc(steps_made, 1)
            ts(step_tmp, step_win, float(W - 1), None, ALU.min)
            quad = step_tmp[0:1, 0:STEPS].rearrange("p (g k) -> p g k", k=4)
            code = win[0:1, :, :].rearrange("p a b -> p (a b)")[:, 0:G]
            stt(code, quad[:, :, 3], 32.0, quad[:, :, 2], ALU.mult, ALU.add)
            stt(code, code, 32.0, quad[:, :, 1], ALU.mult, ALU.add)
            stt(code, code, 32.0, quad[:, :, 0], ALU.mult, ALU.add)
            cp(packed[:, :], code)

            v.wait_ge(blocks_in, 64)
            for g in range(4):
                cp(blocks_f[:, g, :], blocks_i[:, g, :])
            v.sem_inc(blocks_floated, 1)
            for g in range(4):
                ns = min(P, STEPS - P * g)
                for r, to in enumerate((src[:, 0:SLOTS], dstf, prevf, nextf)):
                    v.wait_ge(slots_turned, 2 * g + r // 2 + 1)
                    for hf in range(2):
                        k = (r % 2) * 2 + hf
                        cp(to.rearrange("p (s f) -> p s f", f=2)[:, P * g:P * g + ns, hf],
                           ps[:, 2 * g + r // 2, k * P:k * P + ns])
            stt(dloc[:, :].rearrange("p (s f) -> p s f", f=2), wide(step_win[:, 0:STEPS], 2), -float(P),
                dstf.rearrange("p (s f) -> p s f", f=2), ALU.mult, ALU.add)
            ts(sltmp, dloc[:, :], 0.0, None, ALU.is_ge)
            stt(valid, dloc[:, :], float(P - 1), sltmp, ALU.is_le, ALU.mult)
            ts(gone[:, :], valid, 1.0, BIG, ALU.subtract, ALU.mult)
            tt(sltmp, dstf, prevf, ALU.not_equal)
            stt(prevf, sltmp, -BIG, valid, ALU.mult, ALU.mult)
            tt(sltmp, dstf, nextf, ALU.not_equal)
            tt(last[:, :], sltmp, valid, ALU.mult)
            def in_order(ap):
                return ap.rearrange("p (j g) -> p g j", j=JB).unsqueeze(3).broadcast_to([P, SG, JB, H])
            cp(spreads[0], in_order(prevf))
            ts(spreads[1], in_order(last[:, :]), -BIG, None, ALU.mult)
            v.sem_inc(flags_spread, 1)
            cp(src[:, SLOTS:SLOTS + 16], src[:, 0:16])
            slint = sltmp.bitcast(I32)
            cp(slint, src[:, 0:SLOTS])
            ts(slint, slint, 7, None, ALU.arith_shift_right)
            cp(src_a, slint)
            stt(src_b, src_a, -float(P), src[:, 0:SLOTS], ALU.mult, ALU.add)
            tt(src_a, src_a, gone[:, :], ALU.add)

            v.wait_ge(weights_in, 16 * len(weights))
            for q in (1, 3):
                tt(w1[q * C:(q + 1) * C, :], w1[q * C:(q + 1) * C, :], w1less[q * C:(q + 1) * C, :], ALU.subtract)
            ts(abd[0][:, :, :], headmask[:, :, :], 0.0, None, ALU.is_ge)
            stt(headmask[:, :, :], headmask[:, :, :], float(C), abd[0][:, :, :], ALU.is_lt, ALU.mult)
            ts(lastmask[:, :], lastmask[:, :], float(LAST), None, ALU.is_lt)
            tmp = o2[:, 0:HC]
            for l in range(LAYERS):
                stt(abd[l][:, :, :], headmask[:, :, :], 0.8, wide(attcol[l][:, :], H), ALU.mult, ALU.mult)
                stt(tmp, wcat[l][:, :], 0.2, attrow[l][:, :], ALU.mult, ALU.mult)
                link(v.tensor_reduce(wlin[l][:, :], tmp.rearrange("p (h c) -> p h c", h=H), AX.X, ALU.add))
                tt(wsum[l][:, :], wsum[l][:, :], wcat[l][0:C, :], ALU.add)
                stt(tmp[0:C, :], wsum[l][:, :], 0.2, attrow[l][0:C, :], ALU.mult, ALU.mult)
                link(v.tensor_reduce(wlinsum[l][:, :], tmp[0:C, :].rearrange("p (h c) -> p h c", h=H), AX.X, ALU.add))
            v.sem_inc(weights_made, 1)
            v.wait_ge(x_in, 32)
            cp(T1[:, :, :], X[:, :, :])
            give_table(0)
            give_parts()
            v.wait_ge(flags_copied, 2 * SG // 4)
            for k, f in enumerate((newF, newR)):
                link(v.tensor_reduce(anyreset[:, k:k + 1], f[:, :, :], AX.XY, ALU.min))
            v.sem_inc(carry_asked, 1)
            v.wait_ge(carry_turned, 2)
            for k in range(2):
                cp(resetrow[0:1, k, :], ps[0:1, k, 0:P])
            v.sem_inc(carry_asked, 1)

            link(v.memset(acc[:, :, 0:HID + 1], 0.0))
            link(v.memset(h3[:, :, HID:HID + 1], 1.0))
            for b in range(2):
                v.tensor_copy(idx[:, b, :], src[:, 8 * b:8 * b + 8]).then_inc(idx_ready, 1)

            def front0(i, b):
                make_hot(i, b)
                stage(0, i, b)
                v.wait_ge(xd_summed, 2 * i + b + 3)
                v.tensor_copy(rows[:, b, :, 1, :], ps[:, 2, 0:8 * C].rearrange("p (j c) -> p j c", j=8)).then_inc(xd_copied, 1)

            def back0(i, b):
                g = 2 * i + b
                v.wait_ge(h3_summed, g + 1)
                v.tensor_tensor(h3[:, :, 0:HID], ps[:, 7, :].rearrange("p (j c) -> p j c", j=8),
                                down(b3row[:, :], 8), ALU.add).then_inc(h3_biased, 1)
                v.wait_ge(h3_biased, g + 1)
                v.tensor_scalar(h3[:, :, 0:HID], h3[:, :, 0:HID], 0.0, None, ALU.max).then_inc(h3_made, 1)
                add_steps(0, i, b, [ps[:, 4, k * (HID + 1):(k + 1) * (HID + 1)] for k in range(4)], HID + 1)

            pipelined(v, lambda f, k: (front0(*f), back0(*k)), front0, back0)
            v.wait_ge(acc_added, 4 * G)
            v.sem_inc(small_asked, 1)
            count, most, inv, rs, dis, out_rs = (nodecol[:, k, :] for k in (0, 1, 3, 4, 5, 7))
            cp(count, acc[:, :, HID])
            ts(most, count, 1.0, None, ALU.max)
            link(v.reciprocal(inv, most))
            cp(rs, most)
            ts(empty[:, :], count, 0.0, -BIG, ALU.is_equal, ALU.mult)
            v.wait_ge(table_stored, 16)
            v.wait_ge(small_summed, 1)
            tt(T1[:, :, :], wide(count, C), down(b4row[:, :], W), ALU.mult)
            for w, o in out_parts():
                tt(T1[:, w, :], T1[:, w, :], o, ALU.add)
            tt(T1[:, :, :], T1[:, :, :], wide(inv, C), ALU.mult)
            tt(T1[:, :, :], T1[:, :, :], X[:, :, :], ALU.add)
            layernorm(T1[:, :, :])
            rsqrt()
            ts(dis, count, 0.0, None, ALU.is_gt)
            tt(dis, dis, rs, ALU.mult)

            def gcn(pas):
                def front(i, b):
                    if pas == 1:
                        sl = bass.ds(16 * i + 8 * b, 8)
                        v.tensor_tensor(srchot[:, b, :, 0:P], wide(src_b[:, sl], P), down(iota[:, :], 8), ALU.is_equal
                                        ).then_inc(srchot_made, 1)
                        v.tensor_tensor(srchot[:, b, :, P:P + W], wide(src_a[:, sl], W), down(iota[:, 0:W], 8),
                                        ALU.is_equal).then_inc(srchot_made, 1)
                    make_hot(i, b)
                    stage(pas, i, b)

                def back(i, b):
                    add_steps(pas, i, b, [ps[:, b, k * C:(k + 1) * C] for k in range(4)], C)
                link(v.memset(acc[:, :, 0:C], 0.0))
                pipelined(v, lambda f, k: (front(*f), back(*k)), front, back)
                v.wait_ge(acc_added, 4 * G * (pas + 1))
                v.wait_ge(table_stored, 16 * (pas + 1))

            tt(T1[:, :, :], X[:, :, :], wide(dis, C), ALU.mult)
            give_table(1)
            gcn(1)
            tt(T1[:, :, :], acc[:, :, 0:C], wide(dis, C), ALU.mult)
            tt(T1[:, :, :], T1[:, :, :], X[:, :, :], ALU.add)
            layernorm(T1[:, :, :])
            v.wait_ge(degree_summed, 1)
            ts(out_rs, ps[:, 7, 0:W], 1.0, None, ALU.max)
            rsqrt()

            tt(T1[:, :, :], X[:, :, :], wide(out_rs, C), ALU.mult)
            give_table(2)
            gcn(2)
            tt(T1[:, :, :], acc[:, :, 0:C], wide(rs, C), ALU.mult)
            v.sem_inc(small_asked, 1)
            v.wait_ge(small_summed, 2)
            for w, o in out_parts():
                tt(T2[:, w, :], o, down(bgrow[:, :], w.stop - w.start), ALU.add)
            stt(T1[:, :, :], T2[:, :, :], 0.0, X[:, :, :], ALU.max, ALU.add)
            layernorm(T1[:, :, :])
            cp(X0[:, :, :], X[:, :, :])

            stretch = [(JB - 1) * H + h for h in range(H)]

            def scans(l):
                begin = newF[:, :, :].rearrange("p a b -> p (a b)")
                end = newR[:, :, :].rearrange("p a b -> p (a b)")
                L = SG * P

                def carries(k, column, resets):
                    cp(carrycol[:, 2 * k:2 * k + 1], column)
                    v.sem_inc(carry_asked, 1)
                    v.wait_ge(carry_turned, 2 + 4 * l + 2 * k + 1)
                    cp(carry[0:1, 2 * k, :], ps[0:1, 4, 0:P])
                    link(v.memset(carry[0:1, 2 * k + 1, :], -BIG))
                    got = carry[0:1, 2 * k, :].rearrange("p (j h) -> p h j", h=H)
                    res = resets.rearrange("p (j h) -> p h j", h=H)
                    to = carry[0:1, 2 * k + 1, :].rearrange("p (j h) -> p h j", h=H)
                    for h in range(H):
                        if k == 0:
                            o, a, c = to[:, h, 1:JB], res[:, h, 0:JB - 1], got[:, h, 0:JB - 1]
                        else:
                            o, a, c = to[:, h, JB - 2::-1], res[:, h, JB - 1:0:-1], got[:, h, JB - 1:0:-1]
                        link(v.tensor_tensor_scan(o, a, c, -BIG, ALU.add, ALU.max))
                    v.sem_inc(carry_asked, 1)
                    v.wait_ge(carry_turned, 2 + 4 * l + 2 * k + 2)
                    cp(carrycol[:, 2 * k + 1:2 * k + 2], ps[:, 5, 0:1])
                    return carrycol[:, 2 * k + 1:2 * k + 2]

                v.wait_ge(order_copied, (l + 1) * (SG // 4))
                link(v.tensor_tensor_scan(o2, begin, o1, -BIG, ALU.add, ALU.max))
                c = carries(0, o2[:, L - 1:L], resetrow[0:1, 0, :])
                link(v.tensor_tensor_scan(o2, begin, o1, c, ALU.add, ALU.max))
                link(v.tensor_tensor_scan(o1[:, ::-1], end[:, ::-1], o2[:, ::-1], -BIG, ALU.add, ALU.max))
                c = carries(1, o1[:, 0:1], resetrow[0:1, 1, :])
                link(v.tensor_tensor_scan(o1[:, ::-1], end[:, ::-1], o2[:, ::-1], c, ALU.add, ALU.max))
                v.sem_inc(back_asked, 1)
                for n in range(SG // 4):
                    v.wait_ge(back_turned, l * (SG // 4) + n + 1)
                    m = ps[:, n % 4, :].rearrange("p (g j h) -> p g j h", g=4, j=JB)
                    for k in range(4):
                        lg = logit[:, 4 * n + k::SG, :]
                        tt(lg, lg, m[:, k, :, :], ALU.subtract)
                        ins = v.tensor_tensor(endmax[:, 4 * n + k::SG, :], m[:, k, :, :],
                                              wide(last[:, 4 * n + k::SG], H), ALU.mult)
                        if k == 3:
                            ins.then_inc(back_copied, 1)
                        else:
                            link(ins)

            for l in range(LAYERS):
                cp(T1[:, :, :], X[:, :, :])
                give_table(3 + l)
                v.sem_inc(small_asked, 1)
                give_parts()
                v.wait_ge(self_summed, l + 1)
                cp(lself[:, :, :].rearrange("p w h -> p (w h)"), ps[:, 7, 0:W * H])

                def front(i, b):
                    stage(3 + l, i, b)
                    v.wait_ge(xd_summed, (l + 1) * G + 2 * i + b + 3)
                    v.tensor_copy(rows[:, b, :, 1, :], ps[:, 0, 0:8 * C].rearrange("p (j c) -> p j c", j=8)
                                  ).then_inc(xd_copied, 1)

                def back(i, b):
                    v.wait_ge(logit_summed, l * G + 2 * i + b + 1)
                    sl = bass.ds(16 * i + 8 * b, 8)
                    v.tensor_tensor(logit[:, sl, :].rearrange("p (j q) h -> p j q h", q=2),
                                    ps[:, 6:8, 0:4 * H].rearrange("p q (j h) -> p j q h", h=H),
                                    wide(gone[:, sl], H).rearrange("p (j q) h -> p j q h", q=2), ALU.add
                                    ).then_inc(logit_made, 1)
                pipelined(v, lambda f, k: (front(*f), back(*k)), front, back)
                link(v.memset(acc[:, :, :], 0.0))
                scans(l)

                def front(i, b):
                    g = l * G + 2 * i + b
                    make_hot(i, b)
                    v.wait_ge(p_made, 2 * g + 2)
                    v.wait_ge(xs_in[b], 16 * (l * HALF + i + 1))
                    weigh(v, b, 0, DVE_SLOTS).then_inc(px_made, 1)

                def back(i, b):
                    add_steps(3 + l, i, b, [ps[:, 4 * b + k, 0:HC + 2 * H] for k in range(4)], HC + 2 * H)
                pipelined(v, lambda f, k: (front(*f), back(*k)), front, back)
                v.wait_ge(acc_added, 4 * G * (4 + l))

                a, s0, s1, m = (selfcol[:, k, :, :] for k in (2, 0, 1, 3))
                tt(a, acc[:, :, HC + H:HC + 2 * H], wide(empty[:, :], H), ALU.add)
                tt(m, a, lself[:, :, :], ALU.max)
                tt(s0, a, m, ALU.subtract)
                tt(s1, lself[:, :, :], m, ALU.subtract)
                v.sem_inc(exp_asked, 1)
                v.wait_ge(exp_done, l + 1)
                tt(a, acc[:, :, HC:HC + H], s0, ALU.mult)
                tt(a, a, s1, ALU.add)
                link(v.reciprocal(m, a))
                stt(s0, m, 1.0 / H, s0, ALU.mult, ALU.mult)
                stt(s1, m, 1.0 / H, s1, ALU.mult, ALU.mult)
                y4 = ysum.rearrange("p w (h c) -> p w h c", h=H)
                z4 = yself.rearrange("p w (h c) -> p w h c", h=H)
                tt(y4, acc[:, :, 0:HC].rearrange("p w (h c) -> p w h c", h=H),
                   s0.unsqueeze(3).broadcast_to([P, W, H, C]), ALU.mult)
                tt(z4, X[:, :, :].unsqueeze(2).broadcast_to([P, W, H, C]),
                   s1.unsqueeze(3).broadcast_to([P, W, H, C]), ALU.mult)
                tt(ysum, ysum, yself, ALU.add)
                v.sem_inc(y_asked, 1)
                v.wait_ge(table_stored, 16 * (4 + l))
                v.wait_ge(y_summed, l + 1)
                for w, o in out_parts():
                    tt(T1[:, w, :], o, down(brow[l][:, 0, :], w.stop - w.start), ALU.add)
                if l < LAYERS - 1:
                    stt(T1[:, :, :], T1[:, :, :], 0.01, T1[:, :, :], ALU.mult, ALU.max)
                tt(T1[:, :, :], T1[:, :, :], X[:, :, :], ALU.add)
                ts(T1[:, W - 1, :], T1[:, W - 1, :], lastmask[:, 0:1], None, ALU.mult)
                cp(rest[:, :, :], T1[:, :, :])
                v.sem_inc(bn_asked, 1)
                v.wait_ge(bn_summed, 2 * l + 1)
                ts(bn[:, 0, :], ps[:, 1, 0:C], 1.0 / N, None, ALU.mult)
                tt(T2[:, :, :], T1[:, :, :], down(bn[:, 0, :], W), ALU.subtract)
                ts(T2[:, W - 1, :], T2[:, W - 1, :], lastmask[:, 0:1], None, ALU.mult)
                tt(rest[:, :, :], T2[:, :, :], T2[:, :, :], ALU.mult)
                v.sem_inc(bn_asked, 1)
                v.wait_ge(bn_summed, 2 * l + 2)
                ts(bn[:, 1, :], ps[:, 2, 0:C], 1.0 / N, EPS, ALU.mult, ALU.add)
                rsqrt()
                tt(bn[:, 2, :], bn[:, 1, :], brow[l][:, 1, :], ALU.mult)
                tt(T2[:, :, :], T2[:, :, :], down(bn[:, 2, :], W), ALU.mult)
                tt(X[:, :, :], T2[:, :, :], down(brow[l][:, 2, :], W), ALU.add)

            tt(T1[:, :, :], X[:, :, :], X0[:, :, :], ALU.add)
            layernorm(T1[:, :, :])
            v.sem_inc(table_ready, 1)


def kernel(**inputs):
    import numpy as _np
    import concourse.bacc as _bacc
    from concourse import mybir as _mybir
    from concourse.bass_utils import run_bass_kernel_spmd as _run

    nc = _bacc.Bacc("TRN2", target_bir_lowering=False, num_devices=1)
    arrays = {}

    def given(name, a):
        a = _np.ascontiguousarray(a)
        arrays[f"in_{name}"] = a
        return nc.dram_tensor(f"in_{name}", a.shape, _mybir.dt.from_np(a.dtype), kind="ExternalInput").ap()

    src, dst = _np.asarray(inputs["src"]), _np.asarray(inputs["dst"])
    pad = BLOCKS * BLOCK - E
    none = _np.full(pad + 1, NO_NODE, dst.dtype)
    rows = [_np.concatenate([src, _np.zeros(pad, src.dtype)]), _np.concatenate([dst, none[1:]]),
            _np.concatenate([none[:1], dst, none[1:]])[:-1], _np.concatenate([dst[1:], none])]
    blocks = _np.stack([r.reshape(BLOCKS, BLOCK) for r in rows], axis=1).reshape(BLOCKS, ROWS * BLOCK)

    x = given("x", inputs["x"])
    edge_blocks = given("edge_blocks", blocks)
    L0 = [given(f"L0_{k}", inputs[f"L0_gnn_{k}"]) for k in ("W1", "b1", "W2", "b2", "W3", "b3", "W4", "b4")]
    W_gcn, b_gcn = given("W_gcn", inputs["L2_gnn_weight"]), given("b_gcn", inputs["L2_gnn_bias"])
    gat = [[given(f"{k}{l}", inputs[f"L3_gnn_{k}{l}"]) for k in ("Wl", "Wr", "att", "b", "g", "be")]
           for l in range(1, LAYERS + 1)]
    out = nc.dram_tensor("out_0", (N, C), _mybir.dt.from_np(_np.dtype("float32")), kind="ExternalOutput").ap()
    build(nc, x, edge_blocks, L0, W_gcn, b_gcn, gat, out)
    r = _run(nc, [arrays], core_ids=[0])
    return r.results[0]["out_0"]
```

```python
from contextlib import ExitStack

import numpy as np

import concourse.bass as bass
from concourse import mybir

ALU = mybir.AluOpType
ACT = mybir.ActivationFunctionType
AX = mybir.AxisListType
F32 = mybir.dt.float32
BF16 = mybir.dt.bfloat16
I32 = mybir.dt.int32

P = 128
N = 3125
C = 32
E = 100000
W = -(-N // P)
LAST = N - (W - 1) * P
BLOCK = 256
BLOCKS = -(-E // BLOCK)
STEPS = -(-(BLOCKS + W - 1) // 8) * 8
SLOTS = 2 * STEPS
G = SLOTS // 8
HALF = G // 2
ROWS = 4
NO_NODE = 8191
HID = 64
H = 8
HC = H * C
LAYERS = 3
JB = 16
SG = SLOTS // JB
BIG = 1e30
EPS = 1e-5
TAB = C + 3 * C // 2
ZC = HC + H
DVE_SLOTS = 5
NT = -(-(W * P) // 512)
YT = -(-2 * W // 4)
assert G % 2 == 0 and SLOTS % JB == 0 and SG % 4 == 0


def build(nc, x, edge_blocks, L0, W_gcn, b_gcn, gat, out):
    with ExitStack() as ctx:
        def sb(name, shape, dt=F32):
            return ctx.enter_context(nc.sbuf_tensor(name, shape, dt))

        def sem(name):
            return ctx.enter_context(nc.semaphore(name))

        ps = ctx.enter_context(nc.psum_tensor("ps", [P, 8, 512], F32))

        table = nc.dram_tensor("table", [W * P, TAB], F32).ap()
        turned_dram = nc.dram_tensor("turned_dram", [G, P, 8 * P], BF16).ap()
        xs_dram = nc.dram_tensor("xs_dram", [G, P, 8 * C], F32).ap()

        X = sb("X", [P, W, C])
        T1 = sb("T1", [P, W, C])
        T2 = sb("T2", [P, W, C])
        nodecol = sb("nodecol", [P, 12, W])
        acc = sb("acc", [P, W, 272])
        src = sb("src", [P, SLOTS + 16])
        dloc = sb("dloc", [P, SLOTS])
        gone = sb("gone", [P, SLOTS])
        last = sb("last", [P, SLOTS])
        logit = sb("logit", [P, SLOTS, H])
        order1 = sb("order1", [P, SG, P])
        order2 = sb("order2", [P, SG, P])
        newF = sb("newF", [P, SG, P], BF16)
        newR = sb("newR", [P, SG, P], BF16)
        packed = sb("packed", [1, G], I32)
        idx = sb("idx", [P, 2, 8], I32)
        rows = sb("rows", [P, 2, 8, TAB])
        xs = sb("xs", [P, 2, 8, C])
        lin = sb("lin", [P, 2, 8, H])
        hot = sb("hot", [P, 2, 8, P])
        turned = sb("turned", [P, 2, 8 * P], BF16)
        xwin = sb("xwin", [P, 2, 4, 3 * C], BF16)
        xT = sb("xT", [P, 2, 512])
        ident = sb("ident", [P, P])
        identb = sb("identb", [P, P], BF16)
        iota = sb("iota", [P, P])
        ones = sb("ones", [P, P])
        w1 = sb("w1", [P, HID])
        w2 = sb("w2", [P, 2 * HID])
        w3 = sb("w3", [P, HID])
        w4 = sb("w4", [HID, C])
        bcol = sb("bcol", [P, 2])
        b3row = sb("b3row", [P, HID])
        b4row = sb("b4row", [P, C])
        wg = sb("wg", [C, C])
        bgrow = sb("bgrow", [P, C])
        wcat = [sb(f"wcat{l}", [P, ZC]) for l in range(LAYERS)]
        wsum = [sb(f"wsum{l}", [C, ZC]) for l in range(LAYERS)]
        wstk = [sb(f"wstk{l}", [P, 2, C]) for l in range(LAYERS)]
        attrow = [sb(f"attrow{l}", [P, HC]) for l in range(LAYERS)]
        brow = [sb(f"brow{l}", [P, 3, C]) for l in range(LAYERS)]
        w1less = sb("w1less", [P, HID])
        zeros = sb("zeros", [P, P], BF16)
        lself = sb("lself", [P, W, H])
        bn = sb("bn", [P, 3, C])
        carry = sb("carry", [1, 4, P])
        carrycol = sb("carrycol", [P, 4])

        X0 = sb("X0", [P, W, C])
        zsum = sb("zsum", [P, 2, 8 * H])
        root = sb("root", [P, 2 * C])
        lastmask = sb("lastmask", [P, 1])
        empty = sb("empty", [P, W])
        block_no = sb("block_no", [P, 4], I32)
        win = sb("win", [P, 16, W + 1])
        win_i = sb("win_i", [P, 2, W + 1], I32)
        anyreset = sb("anyreset", [P, 2])
        resetrow = sb("resetrow", [1, 2, P])
        powers = [nodecol[:, 2, :], nodecol[:, 4, :], nodecol[:, 2, :], nodecol[:, 7, :], nodecol[:, 2, :]] \
            + [bn[:, 1, :]] * LAYERS + [nodecol[:, 2, :]]

        hotf = hot[:, :, :, :].rearrange("p b j n -> p (b j n)")
        selfcol = hotf[:, 0:4 * W * H].rearrange("p (k w h) -> p k w h", k=4, w=W)
        rest = hotf[:, 4 * W * H:4 * W * H + W * C].rearrange("p (w c) -> p w c", w=W)
        tabf = hotf[:, 0:W * TAB]
        tab = tabf.rearrange("p (w c) -> p w c", w=W)
        tabparts = tabf.bitcast(BF16).rearrange("p (w c) -> p w c", w=W)
        accf = acc[:, :, :].rearrange("p w c -> p (w c)")
        dst_i = accf[:, 0:1024].bitcast(I32)
        dst_all = accf[:, 1024:2048]
        junk = accf[:, 2048:3072]
        step_no = accf[:, 3072:3072 + STEPS + 4]
        step_win = accf[:, 3500:3500 + STEPS + 4]
        step_blk = accf[:, 3930:3930 + STEPS + 4]
        step_tmp = accf[:, 4360:4360 + STEPS + 4]
        spreads = [t.rearrange("p (g j h) -> p g j h", g=SG, j=JB)
                   for t in (logit[:, :, :].rearrange("p s h -> p (s h)"), accf[:, 0:SLOTS * H])]
        staged = hotf[:, 0:1024].rearrange("p (k c) -> p k c", k=2)
        o1 = order1[:, :, :].rearrange("p a b -> p (a b)")
        o2 = order2[:, :, :].rearrange("p a b -> p (a b)")
        blocks_i = order1[:, :, :].rearrange("p a b -> p (a b)")[:, 0:4 * 1024].bitcast(I32) \
            .rearrange("p (g r) -> p g r", g=4)
        blocks_f = o2[:, 0:4 * 1024].rearrange("p (g r) -> p g r", g=4)
        dstf = hot[:, 0, :, :].rearrange("p j n -> p (j n)")[:, 0:SLOTS]
        prevf = hot[:, 1, :, :].rearrange("p j n -> p (j n)")[:, 0:SLOTS]
        nodeslots = o1[:, 4 * 1024:4 * 1024 + 2 * SLOTS].rearrange("p (k s) -> p k s", k=2)
        nextf = nodeslots[:, 0, :]
        valid = nodeslots[:, 1, :]
        src_a, src_b = nodeslots[:, 0, :], nodeslots[:, 1, :]
        srchot = o1[:, 0:8 * (P + W)].bitcast(BF16).rearrange("p (r j c) -> p r j c", r=2, j=8)
        sltmp = xT[:, :, :].rearrange("p a b -> p (a b)")[:, 0:SLOTS]
        nodeT = o2[0:HID, 0:W * P]
        h1 = o1[:, 0:512]
        h2 = o1[:, 512:1536]
        h3 = o1[:, 1536:1536 + 8 * (HID + 1)].rearrange("p (j c) -> p j c", j=8)
        prod = [o1[:, k * 2048:(k + 1) * 2048].rearrange("p (j c) -> p j c", j=8) for k in range(2)]
        prodself = o1[:, 0:W * HC].rearrange("p (w c) -> p w c", w=W)
        hotb = hotf[:, 0:1024].bitcast(BF16).rearrange("p (b j n) -> p b j n", b=2, j=8)
        rowparts = [rows[:, b, :, :].rearrange("p j c -> p (j c)").bitcast(BF16).rearrange("p (j c) -> p j c", j=8)
                    for b in range(2)]
        px = [o1[:, k * 2176:(k + 1) * 2176].rearrange("p (j c) -> p j c", j=8) for k in range(2)]
        endmax = order2[:, :, :].rearrange("p a b -> p (a b)").rearrange("p (s h) -> p s h", h=H)
        ysum = order2[:, :, :].rearrange("p a b -> p (a b)")[:, 0:W * HC].rearrange("p (w k) -> p w k", w=W)
        yself = order1[:, :, :].rearrange("p a b -> p (a b)")[:, 0:W * HC].rearrange("p (w k) -> p w k", w=W)
        yT = logit[:, :, :].rearrange("p s h -> p (s h)")

        x_in, x_zeroed, zeros_made = sem("x_in"), sem("x_zeroed"), sem("zeros_made")
        exp_asked, exp_done = sem("exp_asked"), sem("exp_done")
        weights_in = sem("weights_in")
        edges_in = sem("edges_in")
        consts_made = sem("consts_made")
        weights_made = sem("weights_made")
        counts_made = sem("counts_made")
        counts_summed = sem("counts_summed")
        steps_made = sem("steps_made")
        blocks_in = sem("blocks_in")
        blocks_floated = sem("blocks_floated")
        slots_turned = sem("slots_turned")
        slots_copied = sem("slots_copied")
        flags_spread = sem("flags_spread")
        flags_turned = sem("flags_turned")
        flags_copied = sem("flags_copied")
        table_ready = sem("table_ready")
        table_stored = sem("table_stored")
        begun, begun_pe = sem("begun"), sem("begun_pe")
        idx_ready = sem("idx_ready")
        gathered = [sem(f"gathered{b}") for b in range(2)]
        hot_made = sem("hot_made")
        px_made_pool = sem("px_made_pool")
        hot_turned = sem("hot_turned")
        turned_made = sem("turned_made")
        turned_stored = [sem(f"turned_stored{b}") for b in range(2)]
        turned_in = [sem(f"turned_in{b}") for b in range(2)]
        xwin_in = [sem(f"xwin_in{b}") for b in range(2)]
        xd_summed = sem("xd_summed")
        xs_copied = sem("xs_copied")
        lin_copied, prod_made, prod_summed = sem("lin_copied"), sem("prod_made"), sem("prod_summed")
        x_turned = sem("x_turned")
        xT_copied = sem("xT_copied")
        h1_summed, h1_made = sem("h1_summed"), sem("h1_made")
        h2_summed, h2_made = sem("h2_summed"), sem("h2_made")
        h3_summed, h3_made = sem("h3_summed"), sem("h3_made")
        agg_summed = sem("agg_summed")
        acc_added = sem("acc_added")
        srchot_made, degree_summed = sem("srchot_made"), sem("degree_summed")
        z_summed, logit_made = sem("z_summed"), sem("logit_made")
        xs_stored = [sem(f"xs_stored{b}") for b in range(2)]
        xs_in = [sem(f"xs_in{b}") for b in range(2)]
        px_made, p_made = sem("px_made"), sem("p_made")
        root_asked, root_done = sem("root_asked"), sem("root_done")
        order_staged = sem("order_staged")
        order_turned, order_copied = sem("order_turned"), sem("order_copied")
        back_asked, back_turned, back_copied = sem("back_asked"), sem("back_turned"), sem("back_copied")
        carry_asked, carry_turned = sem("carry_asked"), sem("carry_turned")
        small_asked, small_turned, small_copied = sem("small_asked"), sem("small_turned"), sem("small_copied")
        small_summed = sem("small_summed")
        zn_summed, zn_read = sem("zn_summed"), sem("zn_read")
        y_asked, y_turned, y_copied, y_summed = sem("y_asked"), sem("y_turned"), sem("y_copied"), sem("y_summed")
        bn_asked, bn_summed = sem("bn_asked"), sem("bn_summed")
        h3_biased, linked = sem("h3_biased"), sem("linked")
        out_stored = sem("out_stored")

        block = ctx.enter_context(nc.Block())

        def pipelined(eng, both, front, back):
            front(0, 0)
            with eng.Fori(0, HALF - 1) as i:
                both((i, 1), (i, 0))
                both((i + 1, 0), (i, 1))
            both((HALF - 1, 1), (HALF - 1, 0))
            back(HALF - 1, 1)

        n_gat = {3 + l: l for l in range(LAYERS)}

        def pool_gathers(pool, pas):
            def group(i, b):
                done = pas * G + 2 * i + b
                pool.wait_ge(table_stored, 16 * (pas + 1))
                pool.wait_ge(idx_ready, done + 1)
                if pas == 0:
                    pool.wait_ge(x_turned, 2 * i + b + 1)
                elif pas < 3:
                    pool.wait_ge(agg_summed, done - 1)
                else:
                    pool.wait_ge(x_turned, (pas - 2) * G + 2 * i + b + 1)
                    pool.wait_ge(xs_copied, (pas - 3) * G + 2 * i + b + 1)
                pool.sem_inc(begun, 1)
                for j in range(8):
                    pool.indirect_dma_start(
                        rows[:, b, j, :], None, table,
                        bass.IndirectOffsetOnAxis(ap=idx[:, b, j:j + 1], axis=0)).then_inc(gathered[b], 16)
            with pool.Fori(0, HALF) as i:
                group(i, 0)
                group(i, 1)

        def weigh(eng, b, lo, hi):
            return eng.tensor_tensor(
                px[b][:, lo:hi, 0:HC].rearrange("p j (h c) -> p j h c", h=H),
                px[b][:, lo:hi, HC:HC + H].unsqueeze(3).broadcast_to([P, hi - lo, H, C]),
                xs[:, b, lo:hi, :].unsqueeze(2).broadcast_to([P, hi - lo, H, C]), ALU.mult)

        def pool_weighs(pool, l):
            def group(i, b):
                g = l * G + 2 * i + b
                pool.wait_ge(p_made, 2 * g + 2)
                pool.wait_ge(xs_in[b], 16 * (l * HALF + i + 1))
                weigh(pool, b, DVE_SLOTS, 8).then_inc(px_made_pool, 1)
            with pool.Fori(0, HALF) as i:
                group(i, 0)
                group(i, 1)

        @block.gpsimd
        def _(pool):
            pool.iota(iota[:, :], [[1, P]], 0, 0, allow_small_or_imprecise_dtypes=True).then_inc(consts_made, 1)
            pool.memset(ones[:, :], 1.0).then_inc(consts_made, 1)
            pool.wait_ge(consts_made, 2)
            pool.affine_select(ident[:, :], ones[:, :], [[-1, P]], ALU.is_equal, 0.0, 0, 1).then_inc(consts_made, 1)
            pool.iota(step_no[:, 0:STEPS], [[1, STEPS]], 0, 0, allow_small_or_imprecise_dtypes=True).then_inc(consts_made, 1)
            pool.iota(step_no[:, STEPS:STEPS + 4], [[P, 4]], 0, 1, allow_small_or_imprecise_dtypes=True
                      ).then_inc(consts_made, 1)
            pool.iota(lastmask[:, :], [[0, 1]], 0, 1, allow_small_or_imprecise_dtypes=True).then_inc(consts_made, 1)
            pool.wait_ge(steps_made, 1)
            for g in range(4):
                pool.indirect_dma_start(
                    blocks_i[:, g, :], None, edge_blocks,
                    bass.IndirectOffsetOnAxis(ap=block_no[:, g:g + 1], axis=0)).then_inc(blocks_in, 16)
            pool_gathers(pool, 0)
            pool_gathers(pool, 1)
            pool_gathers(pool, 2)
            for l in range(LAYERS):
                pool_gathers(pool, 3 + l)
                pool_weighs(pool, l)

        def window_of(eng, code, k):
            return nc.s_assert_within(eng.snap((code >> (5 * k)) & 31), 0, W - 1,
                                      skip_runtime_bounds_check_because="DVE clamps the windows that it packs")

        def load_windows(sp, which, i, b):
            done = which * G + 2 * i + b
            sp.wait_ge(xd_summed, done + 1)
            code = sp.value_load(packed[0:1, bass.ds(2 * i + b, 1)], min_val=0, max_val=(1 << 20) - 1)
            for k in range(4):
                w = window_of(sp, code, k)
                sp.dma_start(xwin[:, b, k, :], table[bass.ds(w * P, P), C:TAB].bitcast(BF16)
                             ).then_inc(xwin_in[b], 16)

        def sp_pass0(sp):
            sp.wait_ge(table_stored, 16)

            def front(i, b):
                load_windows(sp, 0, i, b)

            def back(i, b):
                sp.wait_ge(turned_made, 2 * i + b + 1)
                sp.dma_start(turned_dram[bass.ds(2 * i + b, 1), :, :].rearrange("a p c -> (a p) c"),
                             turned[:, b, :]).then_inc(turned_stored[b], 16)
            pipelined(sp, lambda f, k: (front(*f), back(*k)), front, back)
            for b in range(2):
                sp.wait_ge(turned_stored[b], 16 * (HALF + 1))

        def sp_gather_side(sp, l):
            sp.wait_ge(table_stored, 16 * (l + 4))

            def front(i, b):
                load_windows(sp, l + 1, i, b)
                sp.dma_start(turned[:, b, :], turned_dram[bass.ds(2 * i + b, 1), :, :].rearrange("a p c -> (a p) c")
                             ).then_inc(turned_in[b], 16)

            def back(i, b):
                sp.wait_ge(xs_copied, l * G + 2 * i + b + 3)
                sp.dma_start(xs_dram[bass.ds(2 * i + b, 1), :, :].rearrange("a p c -> (a p) c"),
                             xs[:, b, :, :].rearrange("p j c -> p (j c)")).then_inc(xs_stored[b], 16)
            pipelined(sp, lambda f, k: (front(*f), back(*k)), front, back)
            for b in range(2):
                sp.wait_ge(xs_stored[b], 16 * ((l + 1) * HALF + 1))

        def sp_sum_side(sp, l):
            sp.wait_ge(x_turned, (l + 2) * G + 2)
            def group(i, b):
                sp.wait_ge(px_made, l * G + 2 * i + b + 1)
                sp.wait_ge(px_made_pool, l * G + 2 * i + b + 1)
                sp.dma_start(xs[:, b, :, :].rearrange("p j c -> p (j c)"),
                             xs_dram[bass.ds(2 * i + b, 1), :, :].rearrange("a p c -> (a p) c")
                             ).then_inc(xs_in[b], 16)
            with sp.Fori(0, HALF) as i:
                group(i, 0)
                group(i, 1)

        def store_table(sp, n):
            sp.wait_ge(table_ready, n + 1)
            sp.dma_start(table.rearrange("(w p) c -> p w c", p=P), tab[:, :, :]).then_inc(table_stored, 16)

        @block.sync
        def _(sp):
            full = BLOCKS // P
            sp.dma_start(dst_i[:, 0:full * BLOCK].rearrange("p (g r) -> p g r", g=full),
                         edge_blocks[0:full * P, BLOCK:2 * BLOCK].rearrange("(p g) r -> p g r", g=full)
                         ).then_inc(edges_in, 16)
            sp.wait_ge(x_zeroed, 2)
            sp.dma_start(dst_i[0:BLOCKS - full * P, full * BLOCK:(full + 1) * BLOCK],
                         edge_blocks[full * P:BLOCKS, BLOCK:2 * BLOCK]).then_inc(edges_in, 16)
            sp.dma_start(X[:, 0:W - 1, :], x[0:(W - 1) * P, :].rearrange("(w p) c -> p w c", p=P)).then_inc(x_in, 16)
            sp.dma_start(X[0:LAST, W - 1, :], x[(W - 1) * P:N, :]).then_inc(x_in, 16)
            store_table(sp, 0)
            sp_pass0(sp)
            store_table(sp, 1)
            store_table(sp, 2)
            for l in range(LAYERS):
                store_table(sp, 3 + l)
                sp_gather_side(sp, l)
                sp_sum_side(sp, l)
            sp.wait_ge(table_ready, 4 + LAYERS)
            sp.dma_start(out[0:(W - 1) * P, :].rearrange("(w p) c -> p w c", p=P), X[:, 0:W - 1, :]).then_inc(out_stored, 16)
            sp.dma_start(out[(W - 1) * P:N, :], X[0:LAST, W - 1, :]).then_inc(out_stored, 16)
            sp.wait_ge(out_stored, 32)

        weights = [
            (w1[0:C, :], L0[0][C:2 * C, :]), (w1[2 * C:3 * C, :], L0[0][C:2 * C, :]),
            (w1[C:2 * C, :], L0[0][0:C, :]), (w1[3 * C:4 * C, :], L0[0][0:C, :]),
            (w1less[C:2 * C, :], L0[0][C:2 * C, :]), (w1less[3 * C:4 * C, :], L0[0][C:2 * C, :]),
            (w2[0:HID, :], L0[2]), (w2[HID:P, :], L0[2]), (w3[:, :], L0[4]), (w4[:, :], L0[6]),
            (bcol[0:HID, 0:1], L0[1].rearrange("(p a) -> p a", a=1)),
            (bcol[HID:P, 0:1], L0[1].rearrange("(p a) -> p a", a=1)),
            (bcol[:, 1:2], L0[3].rearrange("(p a) -> p a", a=1)),
            (b3row[:, :], L0[5].partition_broadcast(P)), (b4row[:, :], L0[7].partition_broadcast(P)),
            (wg[:, :], W_gcn), (bgrow[:, :], b_gcn.partition_broadcast(P)),
        ]
        for l, (Wl, Wr, att, bias, gamma, beta) in enumerate(gat):
            flat = att.rearrange("h c -> (h c)")
            weights += [(wcat[l][k * C:(k + 1) * C, 0:HC], (Wl, Wr)[k % 2]) for k in range(4)]
            weights += [(wsum[l][:, 0:HC], Wr), (attrow[l][:, :], flat.partition_broadcast(P))]
            weights += [(brow[l][:, k, :], v.partition_broadcast(P)) for k, v in enumerate((bias, gamma, beta))]
            weights += [(wstk[l][q * C:(q + 1) * C, t, :], Wl[:, (4 * t + q) * C:(4 * t + q + 1) * C])
                        for q in range(4) for t in range(2)]

        def act_pass0(act):
            def front(i, b):
                g = 2 * i + b
                act.wait_ge(hot_turned, g + 1)
                act.wait_ge(turned_stored[b], 16 * (i + 1))
                act.activation(turned[:, b, :], ps[:, 0:2, :].rearrange("p k c -> p (k c)"), ACT.Copy
                               ).then_inc(turned_made, 1)

            def front2(i, b):
                act.wait_ge(x_turned, 2 * i + b + 3)
                act.activation(xT[:, b, :], ps[:, 3, :], ACT.Copy).then_inc(xT_copied, 1)

            def back(i, b):
                g = 2 * i + b
                act.wait_ge(h1_summed, g + 1)
                act.activation(h1, ps[:, 4, :], ACT.Relu, bias=bcol[:, 0:1]).then_inc(h1_made, 1)

            def back2(i, b):
                g = 2 * i + b
                act.wait_ge(h2_summed, g + 1)
                act.activation(h2, ps[:, 5:7, :].rearrange("p k c -> p (k c)"), ACT.Relu, bias=bcol[:, 1:2]
                               ).then_inc(h2_made, 1)

            def both(f, k):
                front(*f)
                back(*k)
                back2(*k)
                front2(*f)
            pipelined(act, both, lambda i, b: (front(i, b), front2(i, b)), lambda i, b: (back(i, b), back2(i, b)))

        def pair(b, k):
            n = 2 + 2 * ((4 * b + k) % 3)
            return ps[:, n:n + 2, :]

        def act_gather_side(act, l):
            base = (l + 1) * G

            def front(i, b):
                g = 2 * i + b
                act.wait_ge(gathered[b], 128 * ((3 + l) * HALF + i + 1))
                act.wait_ge(xs_stored[b], 16 * (l * HALF + i + 1))
                act.activation(xs[:, b, :, :], rows[:, b, :, 0:C], ACT.Copy).then_inc(xs_copied, 1)
                act.wait_ge(x_turned, base + g + 3)
                act.activation(xT[:, b, :], ps[:, b, :], ACT.Copy).then_inc(xT_copied, 1)

            def back(i, b):
                for k in range(4):
                    act.wait_ge(z_summed, l * 4 * G + 8 * i + 4 * b + k + 1)
                    act.activation(lin[:, b, 2 * k:2 * k + 2, :], pair(b, k)[:, :, HC:ZC], ACT.Copy
                                   ).then_inc(lin_copied, 1)

            def both(f, k):
                back(*k)
                front(*f)
            pipelined(act, both, front, back)

        def act_sum_side(act, l):
            act.wait_ge(back_copied, (l + 1) * SG // 4)
            def group(i, b):
                act.wait_ge(agg_summed, (3 + l) * G + 2 * i + b - 1)
                sl = bass.ds(16 * i + 8 * b, 8)
                act.activation(px[b][:, :, HC:HC + H], logit[:, sl, :], ACT.Exp).then_inc(p_made, 1)
                act.activation(px[b][:, :, HC + H:HC + 2 * H], endmax[:, sl, :], ACT.Copy).then_inc(p_made, 1)
            with act.Fori(0, HALF) as i:
                group(i, 0)
                group(i, 1)

        def act_small(act, n, rows_):
            act.wait_ge(small_turned, n + 1)
            for k in range(NT):
                c = min(512, W * P - 512 * k)
                act.activation(nodeT[0:rows_, 512 * k:512 * k + c], ps[0:rows_, k, 0:c], ACT.Copy
                               ).then_inc(small_copied, 1)

        def act_root(act, n):
            act.wait_ge(root_asked, n + 1)
            act.activation(root[:, 0:powers[n].shape[1]], powers[n], ACT.Sqrt).then_inc(root_done, 1)

        @block.scalar
        def _(act):
            for dst, srcw in weights:
                act.dma_start(dst, srcw).then_inc(weights_in, 16)
            for n in range(2 * SG // 4):
                act.wait_ge(flags_turned, n + 1)
                tile = (newF, newR)[n // (SG // 4)]
                k = n % (SG // 4)
                act.activation(tile[:, 4 * k:4 * k + 4, :].rearrange("p g e -> p (g e)"), ps[:, n % 8, :], ACT.Copy
                               ).then_inc(flags_copied, 1)
            act_pass0(act)
            act_small(act, 0, HID)
            for n in range(4):
                act_root(act, n)
            act_small(act, 1, C)
            act_root(act, 4)
            for l in range(LAYERS):
                act_small(act, 2 + l, C)
                act_gather_side(act, l)
                act.wait_ge(logit_made, (l + 1) * G)
                view = logit[:, :, :].rearrange("p (j g) h -> p g j h", j=JB)

                def stage_order(n):
                    for k in range(4):
                        ins = act.activation(staged[:, n % 2, k * P:(k + 1) * P].rearrange("p (j h) -> p j h", h=H),
                                             view[:, 4 * n + k, :, :], ACT.Copy)
                    ins.then_inc(order_staged, 1)
                stage_order(0)
                stage_order(1)
                for n in range(SG // 4):
                    act.wait_ge(order_turned, l * (SG // 4) + n + 1)
                    if n + 2 < SG // 4:
                        stage_order(n + 2)
                    act.activation(order1[:, 4 * n:4 * n + 4, :].rearrange("p g e -> p (g e)"), ps[:, n % 4, :],
                                   ACT.Copy).then_inc(order_copied, 1)
                act_sum_side(act, l)
                act.wait_ge(exp_asked, l + 1)
                act.activation(selfcol[:, 0:2, :, :], selfcol[:, 0:2, :, :], ACT.Exp).then_inc(exp_done, 1)
                for n in range(YT):
                    c = min(4, 2 * W - 4 * n) * P
                    act.wait_ge(y_turned, l * YT + n + 1)
                    act.activation(yT[:, 512 * n:512 * n + c], ps[:, 1 + n % 6, 0:c], ACT.Copy).then_inc(y_copied, 1)
                act_root(act, 5 + l)
            act_root(act, 5 + LAYERS)

        def pe_dst_rows(pe, b, bank):
            for j in range(8):
                q = 64 * (j % 2) + C
                for s in range(3):
                    mm = pe.matmul(ps[q:q + C, bank, (j // 2) * P:(j // 2 + 1) * P],
                                   xwin[:, b, j // 2, s * C:(s + 1) * C], turned[:, b, j * P:(j + 1) * P],
                                   start=(s == 0), stop=(s == 2))
            mm.then_inc(xd_summed, 1)

        def pe_src_rows(pe, b, bank):
            for j in range(8):
                q = 64 * (j % 2)
                for s in range(3):
                    mm = pe.matmul(ps[q:q + C, bank, (j // 2) * P:(j // 2 + 1) * P],
                                   rowparts[b][:, j, 2 * C + s * C:2 * C + (s + 1) * C], identb[:, :],
                                   start=(s == 0), stop=(s == 2))
            mm.then_inc(x_turned, 1)

        def pe_pass0(pe):
            def front_a(i, b):
                pe.wait_ge(hot_made, 2 * i + b + 1)
                for j in range(8):
                    mm = pe.transpose(ps[:, j // 4, (j % 4) * P:(j % 4 + 1) * P], hot[:, b, j, :], ident[:, :])
                mm.then_inc(hot_turned, 1)

            def front_b(i, b):
                pe.wait_ge(turned_made, 2 * i + b + 1)
                pe.wait_ge(xwin_in[b], 64 * (i + 1))
                pe_dst_rows(pe, b, 3)

            def front_c(i, b):
                pe.wait_ge(gathered[b], 128 * (i + 1))
                pe_src_rows(pe, b, 3)

            def back_a(i, b):
                g = 2 * i + b
                pe.wait_ge(xT_copied, g + 1)
                pe.sem_inc(begun_pe, 1)
                for q in range(2):
                    mm = pe.matmul(ps[64 * q:64 * q + 64, 4, :], w1[64 * q:64 * q + 64, :], xT[64 * q:64 * q + 64, b, :],
                                   start=True, stop=True)
                mm.then_inc(h1_summed, 1)

            def back_b(i, b):
                pe.wait_ge(h1_made, 2 * i + b + 1)
                for q in range(2):
                    mm = pe.matmul(ps[:, 5 + q, :], w2[64 * q:64 * q + 64, :], h1[64 * q:64 * q + 64, :],
                                   start=True, stop=True)
                mm.then_inc(h2_summed, 1)

            def back_c(i, b):
                pe.wait_ge(h2_made, 2 * i + b + 1)
                for j in range(8):
                    at = (j % 2) * 512 + (j // 2) * P
                    mm = pe.matmul(ps[:, 7, j * HID:(j + 1) * HID], h2[:, at:at + P], w3[:, :], start=True, stop=True)
                mm.then_inc(h3_summed, 1)

            def back_d(i, b):
                pe.wait_ge(h3_made, 2 * i + b + 1)
                pe.wait_ge(acc_added, 8 * i + 4 * b + 1)
                for j in range(8):
                    k = j // 2
                    mm = pe.matmul(ps[:, 2, k * (HID + 1):(k + 1) * (HID + 1)], hot[:, b, j, :], h3[:, j, :],
                                   start=(j % 2 == 0), stop=(j % 2 == 1))
                mm.then_inc(agg_summed, 1)

            def both(f, k):
                front_a(*f)
                back_a(*k)
                front_b(*f)
                back_b(*k)
                front_c(*f)
                back_c(*k)
                back_d(*k)
            pipelined(pe, both, lambda i, b: (front_a(i, b), front_b(i, b), front_c(i, b)),
                      lambda i, b: (back_a(i, b), back_b(i, b), back_c(i, b), back_d(i, b)))

        def pe_gcn(pe, pas):
            base = pas * G

            def group(i, b):
                g = base + 2 * i + b
                if pas == 1:
                    pe.wait_ge(srchot_made, 4 * i + 2 * b + 2)
                    for j in range(8):
                        pe.matmul(ps[:, 7, 0:W], srchot[:, b, j, 0:P], srchot[:, b, j, P:P + W],
                                  start=False, stop=False, skip_group_check=True)
                pe.wait_ge(hot_made, g + 1)
                pe.wait_ge(gathered[b], 128 * (pas * HALF + i + 1))
                pe.wait_ge(acc_added, 4 * g - 3)
                for j in range(8):
                    k = j // 2
                    mm = pe.matmul(ps[:, b, k * 3 * C:(k + 1) * 3 * C], hotb[:, b, j, :],
                                   rowparts[b][:, j, 2 * C:5 * C],
                                   start=(j % 2 == 0), stop=(j % 2 == 1))
                mm.then_inc(agg_summed, 1)
            if pas == 1:
                pe.wait_ge(zeros_made, 1)
                pe.wait_ge(srchot_made, 2)
                pe.matmul(ps[:, 7, 0:W], zeros[:, 0:P], zeros[:, 0:W], start=True, stop=False, skip_group_check=True)
            with pe.Fori(0, HALF) as i:
                group(i, 0)
                group(i, 1)
            if pas == 1:
                pe.matmul(ps[:, 7, 0:W], zeros[:, 0:P], zeros[:, 0:W], start=False, stop=True,
                          skip_group_check=True).then_inc(degree_summed, 1)

        def pe_gather_side(pe, l):
            base = (l + 1) * G

            def front_a(i, b):
                pe.wait_ge(turned_in[b], 16 * (l * HALF + i + 1))
                pe.wait_ge(xwin_in[b], 64 * ((l + 1) * HALF + i + 1))
                pe_dst_rows(pe, b, b)

            def front_b(i, b):
                pe.wait_ge(gathered[b], 128 * ((3 + l) * HALF + i + 1))
                pe_src_rows(pe, b, b)

            def back(i, b):
                pe.wait_ge(xT_copied, base + 2 * i + b + 1)
                for k in range(4):
                    n = l * 4 * G + 8 * i + 4 * b + k
                    pe.wait_ge(prod_made, n + 1 + (b == 0 and k < 2))
                    for q in range(2):
                        mm = pe.matmul(pair(b, k)[:, q, 0:ZC], xT[64 * q:64 * q + 64, b, k * P:(k + 1) * P],
                                       wcat[l][64 * q:64 * q + 64, :], start=True, stop=True)
                    mm.then_inc(z_summed, 1)

            def both(f, k):
                front_a(*f)
                back(*k)
                front_b(*f)
            pe.wait_ge(zn_read, (l + 1) * W)
            pipelined(pe, both, lambda i, b: (front_a(i, b), front_b(i, b)), back)

        def pe_order(pe, l):
            for n in range(SG // 4):
                if n >= 4:
                    pe.wait_ge(order_copied, l * (SG // 4) + n - 3)
                pe.wait_ge(order_staged, l * (SG // 4) + n + 1)
                for k in range(4):
                    mm = pe.transpose(ps[:, n % 4, k * P:(k + 1) * P], staged[:, n % 2, k * P:(k + 1) * P], ident[:, :])
                mm.then_inc(order_turned, 1)
            for k in range(2):
                pe.wait_ge(carry_asked, 4 * l + 2 * k + 1 + 2)
                pe.transpose(ps[0:1, 4, 0:P], carrycol[:, 2 * k:2 * k + 1], ident[:, :]).then_inc(carry_turned, 1)
                pe.wait_ge(carry_asked, 4 * l + 2 * k + 2 + 2)
                pe.transpose(ps[:, 5, 0:1], carry[0:1, 2 * k + 1, :], ident[0:1, 0:1]).then_inc(carry_turned, 1)
            pe.wait_ge(back_asked, l + 1)
            for n in range(SG // 4):
                if n >= 4:
                    pe.wait_ge(back_copied, l * (SG // 4) + n - 3)
                for k in range(4):
                    mm = pe.transpose(ps[:, n % 4, k * P:(k + 1) * P], order1[:, 4 * n + k, :], ident[:, :])
                mm.then_inc(back_turned, 1)

        def pe_sum_side(pe, l):
            def group(i, b):
                g = l * G + 2 * i + b
                pe.wait_ge(hot_made, 3 * G + g + 1)
                pe.wait_ge(px_made, g + 3)
                pe.wait_ge(px_made_pool, g + 3)
                pe.wait_ge(acc_added, 12 * G + 4 * g - 3)
                for j in range(8):
                    mm = pe.matmul(ps[:, 4 * b + j // 2, 0:HC + 2 * H], hot[:, b, j, :], px[b][:, j, :],
                                   start=(j % 2 == 0), stop=(j % 2 == 1))
                mm.then_inc(agg_summed, 1)
            with pe.Fori(0, HALF) as i:
                group(i, 0)
                group(i, 1)

        def pe_small(pe, n, src_, cols, weight):
            pe.wait_ge(small_asked, n + 1)
            for w in range(W):
                mm = pe.transpose(ps[0:cols, w // 4, (w % 4) * P:(w % 4 + 1) * P], src_[:, w, 0:cols], ident[:, :])
            mm.then_inc(small_turned, 1)
            pe.wait_ge(small_copied, NT * (n + 1))
            if weight is not None:
                for w in range(W):
                    mm = pe.matmul(out_at(w), nodeT[0:cols, w * P:(w + 1) * P], weight, start=True, stop=True)
                mm.then_inc(small_summed, 1)

        def out_at(w):
            return ps[:, 7, w * C:(w + 1) * C] if w < 16 else ps[:, 0, (w - 16) * C:(w - 15) * C]

        def pe_self_sums(pe, l):
            for w in range(W):
                if w >= 8:
                    pe.wait_ge(zn_read, l * W + w - 7)
                pe.matmul(ps[:, w % 8, 0:ZC], nodeT[0:C, w * P:(w + 1) * P], wsum[l][:, :],
                          start=True, stop=True).then_inc(zn_summed, 1)

        def pe_attention_out(pe, l):
            pe.wait_ge(y_asked, l + 1)
            for n in range(YT):
                if n >= 6:
                    pe.wait_ge(y_copied, l * YT + n - 5)
                for k in range(4 * n, min(4 * n + 4, 2 * W)):
                    w, t = k // 2, k % 2
                    mm = pe.transpose(ps[:, 1 + n % 6, (k % 4) * P:(k % 4 + 1) * P], ysum[:, w, t * P:(t + 1) * P],
                                      ident[:, :])
                mm.then_inc(y_turned, 1)
            pe.wait_ge(y_copied, (l + 1) * YT)
            for w in range(W):
                for t in range(2):
                    mm = pe.matmul(out_at(w), yT[:, (2 * w + t) * P:(2 * w + t + 1) * P], wstk[l][:, t, :],
                                   start=(t == 0), stop=(t == 1))
            mm.then_inc(y_summed, 1)
            for s in range(2):
                pe.wait_ge(bn_asked, 2 * l + s + 1)
                for w in range(W):
                    mm = pe.matmul(ps[:, 1 + s, 0:C], ones[:, :], rest[:, w, :], start=(w == 0), stop=(w == W - 1))
                mm.then_inc(bn_summed, 1)

        @block.tensor
        def _(pe):
            pe.sem_inc(xd_summed, 2)
            pe.sem_inc(x_turned, 2)
            for b in range(2):
                pe.sem_inc(turned_stored[b], 16)
                pe.sem_inc(xs_stored[b], 16)
            pe.sem_inc(xs_copied, 2)
            pe.sem_inc(prod_made, 3)
            pe.sem_inc(acc_added, 1)
            pe.wait_ge(consts_made, 6)
            pe.wait_ge(counts_made, 1)
            pe.matmul(ps[:, 0, 0:W - 1], ones[:, :], win[:, 0, 1:W], start=True, stop=True).then_inc(counts_summed, 1)
            pe.wait_ge(blocks_floated, 1)
            for g in range(4):
                for rp in range(2):
                    for k in range(4):
                        r, hf = 2 * rp + k // 2, k % 2
                        at = r * BLOCK + hf * P
                        mm = pe.transpose(ps[:, 2 * g + rp, k * P:(k + 1) * P], blocks_f[:, g, at:at + P], ident[:, :])
                    mm.then_inc(slots_turned, 1)
            pe.wait_ge(flags_spread, 1)
            for n in range(2 * SG // 4):
                spread = spreads[n // (SG // 4)].rearrange("p g j h -> p g (j h)")
                if n >= 8:
                    pe.wait_ge(flags_copied, n - 7)
                for k in range(4):
                    mm = pe.transpose(ps[:, n % 8, k * P:(k + 1) * P], spread[:, 4 * (n % (SG // 4)) + k, :], ident[:, :])
                mm.then_inc(flags_turned, 1)
            pe.wait_ge(flags_copied, 2 * SG // 4)
            for k in range(2):
                pe.wait_ge(carry_asked, 1)
                pe.transpose(ps[0:1, k, 0:P], anyreset[:, k:k + 1], ident[:, :]).then_inc(carry_turned, 1)
            pe.wait_ge(carry_asked, 2)
            pe.wait_ge(weights_made, 1)
            pe_pass0(pe)
            pe_small(pe, 0, acc, HID, w4[:, :])
            pe_gcn(pe, 1)
            pe_gcn(pe, 2)
            pe_small(pe, 1, T1, C, wg[:, :])
            for l in range(LAYERS):
                pe_small(pe, 2 + l, X, C, None)
                pe_self_sums(pe, l)
                pe_gather_side(pe, l)
                pe_order(pe, l)
                pe_sum_side(pe, l)
                pe_attention_out(pe, l)

        def wide(ap, cols):
            return ap.unsqueeze(2).broadcast_to([ap.shape[0], ap.shape[1], cols])

        def down(ap, k):
            return ap.unsqueeze(1).broadcast_to([ap.shape[0], k, ap.shape[1]])

        @block.vector
        def _(v):
            chain = [0]

            def link(ins):
                chain[0] += 1
                ins.then_inc(linked, 1)
                v.wait_ge(linked, chain[0])

            def tt(o, a, b, op):
                link(v.tensor_tensor(o, a, b, op))

            def ts(o, a, s1, s2, op0, op1=ALU.bypass):
                link(v.tensor_scalar(o, a, s1, s2, op0, op1))

            def stt(o, a, s_, b, op0, op1):
                link(v.scalar_tensor_tensor(o, a, s_, b, op0, op1))

            def cp(o, a):
                link(v.tensor_copy(o, a))

            asked = [0]

            def rsqrt():
                x_ = powers[asked[0]]
                asked[0] += 1
                v.sem_inc(root_asked, 1)
                v.wait_ge(root_done, asked[0])
                r_, t_ = root[:, 0:x_.shape[1]], root[:, C:C + x_.shape[1]]
                link(v.reciprocal(r_, r_))
                tt(t_, x_, r_, ALU.mult)
                tt(t_, t_, r_, ALU.mult)
                ts(t_, t_, -0.5, 1.5, ALU.mult, ALU.add)
                tt(x_, r_, t_, ALU.mult)

            def layernorm(of):
                mean, var = nodecol[:, 1, :], nodecol[:, 2, :]
                link(v.tensor_reduce(mean, of, AX.X, ALU.add))
                ts(mean, mean, 1.0 / C, None, ALU.mult)
                tt(T2[:, :, :], of, wide(mean, C), ALU.subtract)
                tt(rest[:, :, :], T2[:, :, :], T2[:, :, :], ALU.mult)
                link(v.tensor_reduce(var, rest[:, :, :], AX.X, ALU.add))
                ts(var, var, 1.0 / C, EPS, ALU.mult, ALU.add)
                rsqrt()
                tt(X[:, :, :], T2[:, :, :], wide(var, C), ALU.mult)

            def give_table(of):
                hi, mid, lo = (tabparts[:, :, (2 + k) * C:(3 + k) * C] for k in range(3))
                cp(tab[:, :, 0:C], of)
                cp(hi, of)
                tt(T2[:, :, :], of, hi, ALU.subtract)
                cp(mid, T2[:, :, :])
                tt(T2[:, :, :], T2[:, :, :], mid, ALU.subtract)
                cp(lo, T2[:, :, :])
                v.sem_inc(table_ready, 1)

            def out_parts():
                return [(slice(0, 16), ps[:, 7, :].rearrange("p (w c) -> p w c", c=C)),
                        (slice(16, W), ps[:, 0, 0:(W - 16) * C].rearrange("p (w c) -> p w c", c=C))]

            def make_hot(i, b, to):
                v.tensor_tensor(to[:, b, :, :], wide(dloc[:, bass.ds(16 * i + 8 * b, 8)], P),
                                down(iota[:, :], 8), ALU.is_equal).then_inc(hot_made, 1)

            def stage(pas, i, b):
                v.wait_ge(gathered[b], 128 * (pas * HALF + i + 1))
                v.tensor_copy(idx[:, b, :], src[:, bass.ds(16 * i + 8 * b + 16, 8)]).then_inc(idx_ready, 1)

            def add_steps(pas, i, b, banks, cols):
                g = pas * G + 2 * i + b
                v.wait_ge(agg_summed, g + 1)
                code = v.value_load(packed[0:1, bass.ds(2 * i + b, 1)], min_val=0, max_val=(1 << 20) - 1)
                for k in range(4):
                    w = window_of(v, code, k)
                    at = acc[:, bass.ds(w, 1), 0:cols].rearrange("p a c -> p (a c)")
                    v.wait_ge(acc_added, 4 * g + k + 1)
                    v.tensor_tensor(at, at, banks[k], ALU.add).then_inc(acc_added, 1)

            v.sem_inc(px_made_pool, 2)
            v.sem_inc(px_made, 2)
            v.memset(dst_i[:, (BLOCKS // P) * BLOCK:], NO_NODE).then_inc(x_zeroed, 1)
            v.memset(X[:, W - 1, :], 0.0).then_inc(x_zeroed, 1)
            v.memset(zeros[:, :], 0.0).then_inc(zeros_made, 1)
            v.wait_ge(edges_in, 32)
            v.wait_ge(x_zeroed, 2)
            cp(dst_all, dst_i)
            for w in range(1, W):
                link(v.tensor_scalar(junk, dst_all, float(P * w), 0.0, ALU.is_lt, ALU.add, accum_out=win[:, 0, w:w + 1]))
            v.sem_inc(counts_made, 1)
            before, blk0, blk1, steps, some = (win[:, k, :] for k in range(1, 6))
            ends, starts, shift, incr = (win[:, k, :] for k in range(6, 10))
            link(v.memset(before[:, 0:1], 0.0))
            link(v.memset(before[:, W:W + 1], float(E)))
            v.wait_ge(counts_summed, 1)
            cp(before[:, 1:W], ps[:, 0, 0:W - 1])
            cp(win_i[:, 0, :], before)
            ts(win_i[:, 0, :], win_i[:, 0, :], 8, None, ALU.arith_shift_right)
            cp(blk0, win_i[:, 0, :])
            ts(win_i[:, 1, :], before, float(BLOCK - 1), None, ALU.add)
            ts(win_i[:, 1, :], win_i[:, 1, :], 8, None, ALU.arith_shift_right)
            cp(blk1, win_i[:, 1, :])
            tt(steps[:, 0:W], blk1[:, 1:W + 1], blk0[:, 0:W], ALU.subtract)
            tt(some[:, 0:W], before[:, 1:W + 1], before[:, 0:W], ALU.is_gt)
            tt(steps[:, 0:W], steps[:, 0:W], some[:, 0:W], ALU.mult)
            v.wait_ge(consts_made, 6)
            link(v.tensor_tensor_scan(ends[:, 0:W], ones[:, 0:W], steps[:, 0:W], 0.0, ALU.mult, ALU.add))
            link(v.memset(starts[:, 0:1], 0.0))
            cp(starts[:, 1:W + 1], ends[:, 0:W])
            tt(shift, blk0, starts, ALU.subtract)
            tt(incr[:, 0:W], shift[:, 1:W + 1], shift[:, 0:W], ALU.subtract)
            link(v.memset(step_win, 0.0))
            cp(step_blk, step_no)
            for w in range(W):
                ts(step_tmp, step_no, ends[:, w:w + 1], None, ALU.is_ge)
                tt(step_win, step_win, step_tmp, ALU.add)
                stt(step_blk, step_tmp, incr[:, w:w + 1], step_blk, ALU.mult, ALU.add)
            ts(step_blk, step_blk, float(BLOCKS - 1), 0.0, ALU.min, ALU.max)
            cp(block_no[:, :], step_blk[:, STEPS:STEPS + 4])
            v.sem_inc(steps_made, 1)
            ts(step_tmp, step_win, float(W - 1), None, ALU.min)
            quad = step_tmp[0:1, 0:STEPS].rearrange("p (g k) -> p g k", k=4)
            code = win[0:1, :, :].rearrange("p a b -> p (a b)")[:, 0:G]
            stt(code, quad[:, :, 3], 32.0, quad[:, :, 2], ALU.mult, ALU.add)
            stt(code, code, 32.0, quad[:, :, 1], ALU.mult, ALU.add)
            stt(code, code, 32.0, quad[:, :, 0], ALU.mult, ALU.add)
            cp(packed[:, :], code)

            v.wait_ge(blocks_in, 64)
            for g in range(4):
                cp(blocks_f[:, g, :], blocks_i[:, g, :])
            v.sem_inc(blocks_floated, 1)
            for g in range(4):
                ns = min(P, STEPS - P * g)
                for r, to in enumerate((src[:, 0:SLOTS], dstf, prevf, nextf)):
                    v.wait_ge(slots_turned, 2 * g + r // 2 + 1)
                    for hf in range(2):
                        k = (r % 2) * 2 + hf
                        cp(to.rearrange("p (s f) -> p s f", f=2)[:, P * g:P * g + ns, hf],
                           ps[:, 2 * g + r // 2, k * P:k * P + ns])
            stt(dloc[:, :].rearrange("p (s f) -> p s f", f=2), wide(step_win[:, 0:STEPS], 2), -float(P),
                dstf.rearrange("p (s f) -> p s f", f=2), ALU.mult, ALU.add)
            ts(sltmp, dloc[:, :], 0.0, None, ALU.is_ge)
            stt(valid, dloc[:, :], float(P - 1), sltmp, ALU.is_le, ALU.mult)
            ts(gone[:, :], valid, 1.0, BIG, ALU.subtract, ALU.mult)
            tt(sltmp, dstf, prevf, ALU.not_equal)
            stt(prevf, sltmp, -BIG, valid, ALU.mult, ALU.mult)
            tt(sltmp, dstf, nextf, ALU.not_equal)
            tt(last[:, :], sltmp, valid, ALU.mult)
            def in_order(ap):
                return ap.rearrange("p (j g) -> p g j", j=JB).unsqueeze(3).broadcast_to([P, SG, JB, H])
            cp(spreads[0], in_order(prevf))
            ts(spreads[1], in_order(last[:, :]), -BIG, None, ALU.mult)
            v.sem_inc(flags_spread, 1)
            cp(src[:, SLOTS:SLOTS + 16], src[:, 0:16])
            slint = sltmp.bitcast(I32)
            cp(slint, src[:, 0:SLOTS])
            ts(slint, slint, 7, None, ALU.arith_shift_right)
            cp(src_a, slint)
            stt(src_b, src_a, -float(P), src[:, 0:SLOTS], ALU.mult, ALU.add)
            tt(src_a, src_a, gone[:, :], ALU.add)

            v.wait_ge(weights_in, 16 * len(weights))
            for q in (1, 3):
                tt(w1[q * C:(q + 1) * C, :], w1[q * C:(q + 1) * C, :], w1less[q * C:(q + 1) * C, :], ALU.subtract)
            ts(lastmask[:, :], lastmask[:, :], float(LAST), None, ALU.is_lt)
            tmp = o2[:, 0:HC]
            for l in range(LAYERS):
                stt(tmp, wcat[l][:, 0:HC], 0.2, attrow[l][:, :], ALU.mult, ALU.mult)
                link(v.tensor_reduce(wcat[l][:, HC:ZC], tmp.rearrange("p (h c) -> p h c", h=H), AX.X, ALU.add))
                tt(wsum[l][:, 0:HC], wsum[l][:, 0:HC], wcat[l][0:C, 0:HC], ALU.add)
                stt(tmp[0:C, :], wsum[l][:, 0:HC], 0.2, attrow[l][0:C, :], ALU.mult, ALU.mult)
                link(v.tensor_reduce(wsum[l][:, HC:ZC], tmp[0:C, :].rearrange("p (h c) -> p h c", h=H), AX.X, ALU.add))
                ts(attrow[l][:, :], attrow[l][:, :], 0.8, None, ALU.mult)
            cp(identb[:, :], ident[:, :])
            v.sem_inc(weights_made, 1)
            v.wait_ge(x_in, 32)
            give_table(X[:, :, :])
            v.wait_ge(flags_copied, 2 * SG // 4)
            for k, f in enumerate((newF, newR)):
                link(v.tensor_reduce(anyreset[:, k:k + 1], f[:, :, :], AX.XY, ALU.min))
            v.sem_inc(carry_asked, 1)
            v.wait_ge(carry_turned, 2)
            for k in range(2):
                cp(resetrow[0:1, k, :], ps[0:1, k, 0:P])
            v.sem_inc(carry_asked, 1)

            v.wait_ge(table_stored, 16)
            link(v.memset(acc[:, :, 0:HID + 1], 0.0))
            link(v.memset(h3[:, :, HID:HID + 1], 1.0))
            for b in range(2):
                v.tensor_copy(idx[:, b, :], src[:, 8 * b:8 * b + 8]).then_inc(idx_ready, 1)

            def front0(i, b):
                make_hot(i, b, hot)

            def back0(i, b):
                g = 2 * i + b
                v.wait_ge(h3_summed, g + 1)
                v.tensor_tensor(h3[:, :, 0:HID], ps[:, 7, :].rearrange("p (j c) -> p j c", j=8),
                                down(b3row[:, :], 8), ALU.add).then_inc(h3_biased, 1)
                v.wait_ge(h3_biased, g + 1)
                v.tensor_scalar(h3[:, :, 0:HID], h3[:, :, 0:HID], 0.0, None, ALU.max).then_inc(h3_made, 1)
                add_steps(0, i, b, [ps[:, 2, k * (HID + 1):(k + 1) * (HID + 1)] for k in range(4)], HID + 1)

            pipelined(v, lambda f, k: (front0(*f), back0(*k), stage(0, *f)),
                      lambda i, b: (front0(i, b), stage(0, i, b)), back0)
            v.wait_ge(acc_added, 4 * G + 1)
            v.sem_inc(small_asked, 1)
            count, most, inv, rs, dis, out_rs = (nodecol[:, k, :] for k in (0, 1, 3, 4, 5, 7))
            cp(count, acc[:, :, HID])
            ts(most, count, 1.0, None, ALU.max)
            link(v.reciprocal(inv, most))
            cp(rs, most)
            ts(empty[:, :], count, 0.0, -BIG, ALU.is_equal, ALU.mult)
            v.wait_ge(small_summed, 1)
            tt(T1[:, :, :], wide(count, C), down(b4row[:, :], W), ALU.mult)
            for w, o in out_parts():
                tt(T1[:, w, :], T1[:, w, :], o, ALU.add)
            tt(T1[:, :, :], T1[:, :, :], wide(inv, C), ALU.mult)
            tt(T1[:, :, :], T1[:, :, :], X[:, :, :], ALU.add)
            layernorm(T1[:, :, :])
            rsqrt()
            ts(dis, count, 0.0, None, ALU.is_gt)
            tt(dis, dis, rs, ALU.mult)

            def gcn(pas):
                def front(i, b):
                    if pas == 1:
                        sl = bass.ds(16 * i + 8 * b, 8)
                        v.tensor_tensor(srchot[:, b, :, 0:P], wide(src_b[:, sl], P), down(iota[:, :], 8), ALU.is_equal
                                        ).then_inc(srchot_made, 1)
                        v.tensor_tensor(srchot[:, b, :, P:P + W], wide(src_a[:, sl], W), down(iota[:, 0:W], 8),
                                        ALU.is_equal).then_inc(srchot_made, 1)
                    make_hot(i, b, hotb)
                    stage(pas, i, b)

                def back(i, b):
                    add_steps(pas, i, b, [ps[:, b, k * 3 * C:(k + 1) * 3 * C] for k in range(4)], 3 * C)
                link(v.memset(acc[:, :, 0:3 * C], 0.0))
                v.wait_ge(table_stored, 16 * (pas + 1))
                pipelined(v, lambda f, k: (front(*f), back(*k)), front, back)
                v.wait_ge(acc_added, 4 * G * (pas + 1) + 1)
                tt(T1[:, :, :], acc[:, :, 0:C], acc[:, :, C:2 * C], ALU.add)
                tt(acc[:, :, 0:C], T1[:, :, :], acc[:, :, 2 * C:3 * C], ALU.add)

            tt(T1[:, :, :], X[:, :, :], wide(dis, C), ALU.mult)
            give_table(T1[:, :, :])
            gcn(1)
            tt(T1[:, :, :], acc[:, :, 0:C], wide(dis, C), ALU.mult)
            tt(T1[:, :, :], T1[:, :, :], X[:, :, :], ALU.add)
            layernorm(T1[:, :, :])
            v.wait_ge(degree_summed, 1)
            ts(out_rs, ps[:, 7, 0:W], 1.0, None, ALU.max)
            rsqrt()

            tt(T1[:, :, :], X[:, :, :], wide(out_rs, C), ALU.mult)
            give_table(T1[:, :, :])
            gcn(2)
            tt(T1[:, :, :], acc[:, :, 0:C], wide(rs, C), ALU.mult)
            v.sem_inc(small_asked, 1)
            v.wait_ge(small_summed, 2)
            for w, o in out_parts():
                tt(T2[:, w, :], o, down(bgrow[:, :], w.stop - w.start), ALU.add)
            stt(T1[:, :, :], T2[:, :, :], 0.0, X[:, :, :], ALU.max, ALU.add)
            layernorm(T1[:, :, :])
            cp(X0[:, :, :], X[:, :, :])

            stretch = [(JB - 1) * H + h for h in range(H)]

            def scans(l):
                begin = newF[:, :, :].rearrange("p a b -> p (a b)")
                end = newR[:, :, :].rearrange("p a b -> p (a b)")
                L = SG * P

                def carries(k, column, resets):
                    cp(carrycol[:, 2 * k:2 * k + 1], column)
                    v.sem_inc(carry_asked, 1)
                    v.wait_ge(carry_turned, 2 + 4 * l + 2 * k + 1)
                    cp(carry[0:1, 2 * k, :], ps[0:1, 4, 0:P])
                    link(v.memset(carry[0:1, 2 * k + 1, :], -BIG))
                    got = carry[0:1, 2 * k, :].rearrange("p (j h) -> p h j", h=H)
                    res = resets.rearrange("p (j h) -> p h j", h=H)
                    to = carry[0:1, 2 * k + 1, :].rearrange("p (j h) -> p h j", h=H)
                    for h in range(H):
                        if k == 0:
                            o, a, c = to[:, h, 1:JB], res[:, h, 0:JB - 1], got[:, h, 0:JB - 1]
                        else:
                            o, a, c = to[:, h, JB - 2::-1], res[:, h, JB - 1:0:-1], got[:, h, JB - 1:0:-1]
                        link(v.tensor_tensor_scan(o, a, c, -BIG, ALU.add, ALU.max))
                    v.sem_inc(carry_asked, 1)
                    v.wait_ge(carry_turned, 2 + 4 * l + 2 * k + 2)
                    cp(carrycol[:, 2 * k + 1:2 * k + 2], ps[:, 5, 0:1])
                    return carrycol[:, 2 * k + 1:2 * k + 2]

                v.wait_ge(order_copied, (l + 1) * (SG // 4))
                link(v.tensor_tensor_scan(o2, begin, o1, -BIG, ALU.add, ALU.max))
                c = carries(0, o2[:, L - 1:L], resetrow[0:1, 0, :])
                link(v.tensor_tensor_scan(o2, begin, o1, c, ALU.add, ALU.max))
                link(v.tensor_tensor_scan(o1[:, ::-1], end[:, ::-1], o2[:, ::-1], -BIG, ALU.add, ALU.max))
                c = carries(1, o1[:, 0:1], resetrow[0:1, 1, :])
                link(v.tensor_tensor_scan(o1[:, ::-1], end[:, ::-1], o2[:, ::-1], c, ALU.add, ALU.max))
                v.sem_inc(back_asked, 1)
                for n in range(SG // 4):
                    v.wait_ge(back_turned, l * (SG // 4) + n + 1)
                    m = ps[:, n % 4, :].rearrange("p (g j h) -> p g j h", g=4, j=JB)
                    for k in range(4):
                        lg = logit[:, 4 * n + k::SG, :]
                        tt(lg, lg, m[:, k, :, :], ALU.subtract)
                        ins = v.tensor_tensor(endmax[:, 4 * n + k::SG, :], m[:, k, :, :],
                                              wide(last[:, 4 * n + k::SG], H), ALU.mult)
                        if k == 3:
                            ins.then_inc(back_copied, 1)
                        else:
                            link(ins)

            for l in range(LAYERS):
                give_table(X[:, :, :])
                v.sem_inc(small_asked, 1)
                for w in range(W):
                    v.wait_ge(zn_summed, l * W + w + 1)
                    stt(prodself[:, w, :], ps[:, w % 8, 0:HC], 0.0, attrow[l][:, :], ALU.max, ALU.mult)
                    v.tensor_copy(lself[:, w, :], ps[:, w % 8, HC:ZC]).then_inc(zn_read, 1)
                selfsum = selfcol[:, 0, :, :]
                v.wait_ge(table_stored, 16 * (l + 4))
                link(v.tensor_reduce(selfsum.rearrange("p w h -> p (w h)"),
                                     prodself.rearrange("p w (h c) -> p (w h) c", h=H), AX.X, ALU.add))
                v.wait_ge(zn_read, (l + 1) * W)
                tt(lself[:, :, :], lself[:, :, :], selfsum, ALU.add)

                def front(i, b):
                    stage(3 + l, i, b)

                def back(i, b):
                    g = l * G + 2 * i + b
                    for k in range(4):
                        v.wait_ge(lin_copied, 4 * g + k + 1)
                        v.scalar_tensor_tensor(prod[b][:, 2 * k:2 * k + 2, :], pair(b, k)[:, :, 0:HC], 0.0,
                                               down(attrow[l][:, :], 2), ALU.max, ALU.mult).then_inc(prod_made, 1)
                    v.wait_ge(prod_made, 4 * g + 7)
                    sums = zsum[:, b, :]
                    v.tensor_reduce(sums, prod[b].rearrange("p j (h c) -> p (j h) c", h=H), AX.X, ALU.add
                                    ).then_inc(prod_summed, 1)
                    v.wait_ge(prod_summed, 2 * g + 1)
                    v.tensor_tensor(sums, sums, lin[:, b, :, :].rearrange("p j h -> p (j h)"), ALU.add
                                    ).then_inc(prod_summed, 1)
                    v.wait_ge(prod_summed, 2 * g + 2)
                    sl = bass.ds(16 * i + 8 * b, 8)
                    v.tensor_tensor(logit[:, sl, :], sums.rearrange("p (j h) -> p j h", h=H), wide(gone[:, sl], H),
                                    ALU.add).then_inc(logit_made, 1)
                pipelined(v, lambda f, k: (back(*k), front(*f)), front, back)
                link(v.memset(acc[:, :, :], 0.0))
                scans(l)

                def front(i, b):
                    g = l * G + 2 * i + b
                    make_hot(i, b, hot)
                    v.wait_ge(p_made, 2 * g + 2)
                    v.wait_ge(xs_in[b], 16 * (l * HALF + i + 1))
                    weigh(v, b, 0, DVE_SLOTS).then_inc(px_made, 1)

                def back(i, b):
                    add_steps(3 + l, i, b, [ps[:, 4 * b + k, 0:HC + 2 * H] for k in range(4)], HC + 2 * H)
                pipelined(v, lambda f, k: (front(*f), back(*k)), front, back)
                v.wait_ge(acc_added, 4 * G * (4 + l) + 1)

                a, s0, s1, m = (selfcol[:, k, :, :] for k in (2, 0, 1, 3))
                tt(a, acc[:, :, HC + H:HC + 2 * H], wide(empty[:, :], H), ALU.add)
                tt(m, a, lself[:, :, :], ALU.max)
                tt(s0, a, m, ALU.subtract)
                tt(s1, lself[:, :, :], m, ALU.subtract)
                v.sem_inc(exp_asked, 1)
                v.wait_ge(exp_done, l + 1)
                tt(a, acc[:, :, HC:HC + H], s0, ALU.mult)
                tt(a, a, s1, ALU.add)
                link(v.reciprocal(m, a))
                stt(s0, m, 1.0 / H, s0, ALU.mult, ALU.mult)
                stt(s1, m, 1.0 / H, s1, ALU.mult, ALU.mult)
                y4 = ysum.rearrange("p w (h c) -> p w h c", h=H)
                z4 = yself.rearrange("p w (h c) -> p w h c", h=H)
                tt(y4, acc[:, :, 0:HC].rearrange("p w (h c) -> p w h c", h=H),
                   s0.unsqueeze(3).broadcast_to([P, W, H, C]), ALU.mult)
                tt(z4, X[:, :, :].unsqueeze(2).broadcast_to([P, W, H, C]),
                   s1.unsqueeze(3).broadcast_to([P, W, H, C]), ALU.mult)
                tt(ysum, ysum, yself, ALU.add)
                v.sem_inc(y_asked, 1)
                v.wait_ge(y_summed, l + 1)
                for w, o in out_parts():
                    tt(T1[:, w, :], o, down(brow[l][:, 0, :], w.stop - w.start), ALU.add)
                if l < LAYERS - 1:
                    stt(T1[:, :, :], T1[:, :, :], 0.01, T1[:, :, :], ALU.mult, ALU.max)
                tt(T1[:, :, :], T1[:, :, :], X[:, :, :], ALU.add)
                ts(T1[:, W - 1, :], T1[:, W - 1, :], lastmask[:, 0:1], None, ALU.mult)
                cp(rest[:, :, :], T1[:, :, :])
                v.sem_inc(bn_asked, 1)
                v.wait_ge(bn_summed, 2 * l + 1)
                ts(bn[:, 0, :], ps[:, 1, 0:C], 1.0 / N, None, ALU.mult)
                tt(T2[:, :, :], T1[:, :, :], down(bn[:, 0, :], W), ALU.subtract)
                ts(T2[:, W - 1, :], T2[:, W - 1, :], lastmask[:, 0:1], None, ALU.mult)
                tt(rest[:, :, :], T2[:, :, :], T2[:, :, :], ALU.mult)
                v.sem_inc(bn_asked, 1)
                v.wait_ge(bn_summed, 2 * l + 2)
                ts(bn[:, 1, :], ps[:, 2, 0:C], 1.0 / N, EPS, ALU.mult, ALU.add)
                rsqrt()
                tt(bn[:, 2, :], bn[:, 1, :], brow[l][:, 1, :], ALU.mult)
                tt(T2[:, :, :], T2[:, :, :], down(bn[:, 2, :], W), ALU.mult)
                tt(X[:, :, :], T2[:, :, :], down(brow[l][:, 2, :], W), ALU.add)

            tt(T1[:, :, :], X[:, :, :], X0[:, :, :], ALU.add)
            layernorm(T1[:, :, :])
            v.sem_inc(table_ready, 1)


def kernel(**inputs):
    import numpy as _np
    import concourse.bacc as _bacc
    from concourse import mybir as _mybir
    from concourse.bass_utils import run_bass_kernel_spmd as _run

    nc = _bacc.Bacc("TRN2", target_bir_lowering=False, num_devices=1)
    arrays = {}

    def given(name, a):
        a = _np.ascontiguousarray(a)
        arrays[f"in_{name}"] = a
        return nc.dram_tensor(f"in_{name}", a.shape, _mybir.dt.from_np(a.dtype), kind="ExternalInput").ap()

    src, dst = _np.asarray(inputs["src"]), _np.asarray(inputs["dst"])
    pad = BLOCKS * BLOCK - E
    none = _np.full(pad + 1, NO_NODE, dst.dtype)
    rows = [_np.concatenate([src, _np.zeros(pad, src.dtype)]), _np.concatenate([dst, none[1:]]),
            _np.concatenate([none[:1], dst, none[1:]])[:-1], _np.concatenate([dst[1:], none])]
    blocks = _np.stack([r.reshape(BLOCKS, BLOCK) for r in rows], axis=1).reshape(BLOCKS, ROWS * BLOCK)

    x = given("x", inputs["x"])
    edge_blocks = given("edge_blocks", blocks)
    L0 = [given(f"L0_{k}", inputs[f"L0_gnn_{k}"]) for k in ("W1", "b1", "W2", "b2", "W3", "b3", "W4", "b4")]
    W_gcn, b_gcn = given("W_gcn", inputs["L2_gnn_weight"]), given("b_gcn", inputs["L2_gnn_bias"])
    gat = [[given(f"{k}{l}", inputs[f"L3_gnn_{k}{l}"]) for k in ("Wl", "Wr", "att", "b", "g", "be")]
           for l in range(1, LAYERS + 1)]
    out = nc.dram_tensor("out_0", (N, C), _mybir.dt.from_np(_np.dtype("float32")), kind="ExternalOutput").ap()
    build(nc, x, edge_blocks, L0, W_gcn, b_gcn, gat, out)
    r = _run(nc, [arrays], core_ids=[0])
    return r.results[0]["out_0"]
```

```python
from contextlib import ExitStack

import numpy as np

import concourse.bass as bass
from concourse import mybir

ALU = mybir.AluOpType
ACT = mybir.ActivationFunctionType
AX = mybir.AxisListType
F32 = mybir.dt.float32
BF16 = mybir.dt.bfloat16
I32 = mybir.dt.int32

P = 128
N = 3125
C = 32
E = 100000
W = -(-N // P)
LAST = N - (W - 1) * P
BLOCK = 256
BLOCKS = -(-E // BLOCK)
STEPS = -(-(BLOCKS + W - 1) // 8) * 8
SLOTS = 2 * STEPS
G = SLOTS // 8
HALF = G // 2
ROWS = 4
NO_NODE = 8191
HID = 64
H = 8
HC = H * C
LAYERS = 3
JB = 16
SG = SLOTS // JB
BIG = 1e30
EPS = 1e-5
TAB = C + 3 * C // 2
ZC = HC + H
DVE_SLOTS = 3
NT = -(-(W * P) // 512)
YT = -(-2 * W // 4)
assert G % 4 == 0 and SLOTS % JB == 0 and SG % 4 == 0


def build(nc, x, edge_blocks, L0, W_gcn, b_gcn, gat, out):
    with ExitStack() as ctx:
        def sb(name, shape, dt=F32):
            return ctx.enter_context(nc.sbuf_tensor(name, shape, dt))

        def sem(name):
            return ctx.enter_context(nc.semaphore(name))

        ps = ctx.enter_context(nc.psum_tensor("ps", [P, 8, 512], F32))

        table = nc.dram_tensor("table", [W * P, TAB], F32).ap()
        turned_dram = nc.dram_tensor("turned_dram", [G, P, 8 * P], BF16).ap()
        xs_dram = nc.dram_tensor("xs_dram", [G, P, 8 * C], F32).ap()

        X = sb("X", [P, W, C])
        T1 = sb("T1", [P, W, C])
        T2 = sb("T2", [P, W, C])
        nodecol = sb("nodecol", [P, 12, W])
        acc = sb("acc", [P, W, 272])
        src = sb("src", [P, SLOTS + 16])
        dloc = sb("dloc", [P, SLOTS])
        gone = sb("gone", [P, SLOTS])
        last = sb("last", [P, SLOTS], BF16)
        logit = sb("logit", [P, SLOTS, H])
        order1 = sb("order1", [P, SG, P])
        order2 = sb("order2", [P, SG, P])
        newF = sb("newF", [P, SG, P], BF16)
        newR = sb("newR", [P, SG, P], BF16)
        packed = sb("packed", [1, G], I32)
        idx = sb("idx", [P, 2, 8], I32)
        rows = sb("rows", [P, 2, 8, TAB])
        xs = sb("xs", [P, 2, 8, C])
        lin = sb("lin", [P, 2, 8, H])
        hot = sb("hot", [P, 2, 8, P])
        turned = sb("turned", [P, 2, 8 * P], BF16)
        xwin = sb("xwin", [P, 2, 4, 3 * C], BF16)
        xT = sb("xT", [P, 2, 512])
        ident = sb("ident", [P, P])
        identb = sb("identb", [P, P], BF16)
        iota = sb("iota", [P, P])
        ones = sb("ones", [P, P])
        w1 = sb("w1", [P, P])
        w2 = sb("w2", [P, 2, P])
        w3 = sb("w3", [P, HID])
        w4 = sb("w4", [HID, C])
        bcol = sb("bcol", [P, 2])
        b3row = sb("b3row", [P, HID])
        b4row = sb("b4row", [P, C])
        wg = sb("wg", [C, C])
        bgrow = sb("bgrow", [P, C])
        wcat = [sb(f"wcat{l}", [P, 2, ZC]) for l in range(LAYERS)]
        wsum = [sb(f"wsum{l}", [C, ZC]) for l in range(LAYERS)]
        wstk = [sb(f"wstk{l}", [P, 2, C]) for l in range(LAYERS)]
        attrow = [sb(f"attrow{l}", [P, HC]) for l in range(LAYERS)]
        brow = [sb(f"brow{l}", [P, 3, C]) for l in range(LAYERS)]
        w1less = sb("w1less", [P, HID])
        zeros = sb("zeros", [P, P], BF16)
        lself = sb("lself", [P, W, H])
        bn = sb("bn", [P, 3, C])
        carry = sb("carry", [1, 4, P])
        carrycol = sb("carrycol", [P, 4])

        X0 = sb("X0", [P, W, C])
        zsum = sb("zsum", [P, 2, 8 * H])
        root = sb("root", [P, 2 * C])
        lastmask = sb("lastmask", [P, 1])
        empty = sb("empty", [P, W])
        block_no = sb("block_no", [P, 4], I32)
        win = sb("win", [P, 16, W + 1])
        win_i = sb("win_i", [P, 2, W + 1], I32)
        anyreset = sb("anyreset", [P, 2])
        resetrow = sb("resetrow", [1, 2, P])
        powers = [nodecol[:, 2, :], nodecol[:, 4, :], nodecol[:, 2, :], nodecol[:, 7, :], nodecol[:, 2, :]] \
            + [bn[:, 1, :]] * LAYERS + [nodecol[:, 2, :]]

        hotf = hot[:, :, :, :].rearrange("p b j n -> p (b j n)")
        selfcol = hotf[:, 0:4 * W * H].rearrange("p (k w h) -> p k w h", k=4, w=W)
        rest = hotf[:, 4 * W * H:4 * W * H + W * C].rearrange("p (w c) -> p w c", w=W)
        tabf = hotf[:, 0:W * TAB]
        tab = tabf.rearrange("p (w c) -> p w c", w=W)
        xsring = rows[:, :, :, :].rearrange("p b j c -> p (b j c)")[:, 0:4 * 8 * C].rearrange(
            "p (q j c) -> p q j c", q=4, j=8)
        tabparts = tabf.bitcast(BF16).rearrange("p (w c) -> p w c", w=W)
        accf = acc[:, :, :].rearrange("p w c -> p (w c)")
        dst_i = accf[:, 0:1024].bitcast(I32)
        dst_all = accf[:, 1024:2048]
        junk = accf[:, 2048:3072]
        step_no = accf[:, 3072:3072 + STEPS + 4]
        step_win = accf[:, 3500:3500 + STEPS + 4]
        step_blk = accf[:, 3930:3930 + STEPS + 4]
        step_tmp = accf[:, 4360:4360 + STEPS + 4]
        spreads = [t.rearrange("p (g j h) -> p g j h", g=SG, j=JB)
                   for t in (logit[:, :, :].rearrange("p s h -> p (s h)"), accf[:, 0:SLOTS * H])]
        staged = hotf[:, 0:1024].rearrange("p (k c) -> p k c", k=2)
        o1 = order1[:, :, :].rearrange("p a b -> p (a b)")
        o2 = order2[:, :, :].rearrange("p a b -> p (a b)")
        blocks_i = order1[:, :, :].rearrange("p a b -> p (a b)")[:, 0:4 * 1024].bitcast(I32) \
            .rearrange("p (g r) -> p g r", g=4)
        blocks_f = o2[:, 0:4 * 1024].rearrange("p (g r) -> p g r", g=4)
        dstf = hot[:, 0, :, :].rearrange("p j n -> p (j n)")[:, 0:SLOTS]
        prevf = hot[:, 1, :, :].rearrange("p j n -> p (j n)")[:, 0:SLOTS]
        nodeslots = o1[:, 4 * 1024:4 * 1024 + 2 * SLOTS].rearrange("p (k s) -> p k s", k=2)
        nextf = nodeslots[:, 0, :]
        valid = nodeslots[:, 1, :]
        src_a, src_b = nodeslots[:, 0, :], nodeslots[:, 1, :]
        srchot = o1[:, 0:8 * (P + W)].bitcast(BF16).rearrange("p (r j c) -> p r j c", r=2, j=8)
        sltmp = xT[:, :, :].rearrange("p a b -> p (a b)")[:, 0:SLOTS]
        nodeT = o2[0:HID, 0:W * P]
        h1 = o1[:, 0:512]
        h2 = o1[:, 512:1536]
        h3 = o1[:, 1536:1536 + 8 * (HID + 1)].rearrange("p (j c) -> p j c", j=8)
        prod = [o1[:, k * 2048:(k + 1) * 2048].rearrange("p (j c) -> p j c", j=8) for k in range(2)]
        prodself = o1[:, 0:W * HC].rearrange("p (w c) -> p w c", w=W)
        hotb = o1[:, 2560:3584].bitcast(BF16).rearrange("p (b j n) -> p b j n", b=2, j=8)
        rowparts = [rows[:, b, :, :].rearrange("p j c -> p (j c)").bitcast(BF16).rearrange("p (j c) -> p j c", j=8)
                    for b in range(2)]
        px = [o1[:, k * 2176:(k + 1) * 2176].rearrange("p (j c) -> p j c", j=8) for k in range(2)]
        endmax = order2[:, :, :].rearrange("p a b -> p (a b)").rearrange("p (s h) -> p s h", h=H)
        ysum = order2[:, :, :].rearrange("p a b -> p (a b)")[:, 0:W * HC].rearrange("p (w k) -> p w k", w=W)
        yself = order1[:, :, :].rearrange("p a b -> p (a b)")[:, 0:W * HC].rearrange("p (w k) -> p w k", w=W)
        yT = logit[:, :, :].rearrange("p s h -> p (s h)")

        x_in, x_zeroed, zeros_made = sem("x_in"), sem("x_zeroed"), sem("zeros_made")
        weighed, maxima_taken, acc_zeroed = sem("weighed"), sem("maxima_taken"), sem("acc_zeroed")
        exp_asked, exp_done = sem("exp_asked"), sem("exp_done")
        weights_in, weights_zeroed = sem("weights_in"), sem("weights_zeroed")
        edges_in = sem("edges_in")
        consts_made = sem("consts_made")
        weights_made = sem("weights_made")
        counts_made = sem("counts_made")
        counts_summed = sem("counts_summed")
        steps_made = sem("steps_made")
        blocks_in = sem("blocks_in")
        blocks_floated = sem("blocks_floated")
        slots_turned = sem("slots_turned")
        slots_copied = sem("slots_copied")
        flags_spread = sem("flags_spread")
        flags_turned = sem("flags_turned")
        flags_copied = sem("flags_copied")
        table_ready = sem("table_ready")
        table_stored = sem("table_stored")
        begun = sem("begun")
        idx_ready = sem("idx_ready")
        gathered = [sem(f"gathered{b}") for b in range(2)]
        hot_made, hotb_made, halves_made = sem("hot_made"), sem("hotb_made"), sem("halves_made")
        px_made_pool = sem("px_made_pool")
        hot_turned = sem("hot_turned")
        turned_made = sem("turned_made")
        turned_stored = [sem(f"turned_stored{b}") for b in range(2)]
        turned_in = [sem(f"turned_in{b}") for b in range(2)]
        xwin_in = [sem(f"xwin_in{b}") for b in range(2)]
        xd_summed = sem("xd_summed")
        xs_copied = sem("xs_copied")
        lin_copied, prod_made, prod_summed = sem("lin_copied"), sem("prod_made"), sem("prod_summed")
        x_turned = sem("x_turned")
        xT_copied = sem("xT_copied")
        h1_summed, h1_made = sem("h1_summed"), sem("h1_made")
        h2_summed, h2_made = sem("h2_summed"), sem("h2_made")
        h3_summed, h3_made = sem("h3_summed"), sem("h3_made")
        agg_summed = sem("agg_summed")
        acc_added = sem("acc_added")
        srchot_made, degree_summed = sem("srchot_made"), sem("degree_summed")
        z_summed, logit_made = sem("z_summed"), sem("logit_made")
        xs_stored = [sem(f"xs_stored{b}") for b in range(2)]
        xs_in = [sem(f"xs_in{q}") for q in range(4)]
        px_made, p_made = sem("px_made"), sem("p_made")
        root_asked, root_done = sem("root_asked"), sem("root_done")
        order_staged = sem("order_staged")
        order_turned, order_copied = sem("order_turned"), sem("order_copied")
        back_asked, back_turned, back_copied = sem("back_asked"), sem("back_turned"), sem("back_copied")
        carry_asked, carry_turned = sem("carry_asked"), sem("carry_turned")
        small_asked, small_turned, small_copied = sem("small_asked"), sem("small_turned"), sem("small_copied")
        small_summed = sem("small_summed")
        zn_summed, zn_read = sem("zn_summed"), sem("zn_read")
        y_asked, y_turned, y_copied, y_summed = sem("y_asked"), sem("y_turned"), sem("y_copied"), sem("y_summed")
        bn_asked, bn_summed = sem("bn_asked"), sem("bn_summed")
        h3_biased, linked = sem("h3_biased"), sem("linked")
        out_stored = sem("out_stored")

        block = ctx.enter_context(nc.Block())

        def pipelined(eng, both, front, back):
            front(0, 0)
            with eng.Fori(0, HALF - 1) as i:
                both((i, 1), (i, 0))
                both((i + 1, 0), (i, 1))
            both((HALF - 1, 1), (HALF - 1, 0))
            back(HALF - 1, 1)

        def pipelined_by_three(eng, steps):
            end = HALF - 1
            steps((0, 0), None, None, None)
            steps((0, 1), (0, 0), None, None)
            steps((1, 0), (0, 1), (0, 0), None)
            with eng.Fori(0, HALF - 2) as i:
                steps((i + 1, 1), (i + 1, 0), (i, 1), (i, 0))
                steps((i + 2, 0), (i + 1, 1), (i + 1, 0), (i, 1))
            steps((end, 1), (end, 0), (end - 1, 1), (end - 1, 0))
            steps(None, (end, 1), (end, 0), (end - 1, 1))
            steps(None, None, (end, 1), (end, 0))
            steps(None, None, None, (end, 1))

        n_gat = {3 + l: l for l in range(LAYERS)}

        def pool_gathers(pool, pas):
            def group(i, b):
                done = pas * G + 2 * i + b
                pool.wait_ge(table_stored, 16 * (pas + 1))
                pool.wait_ge(idx_ready, done + 1)
                if pas == 0:
                    pool.wait_ge(x_turned, 2 * i + b + 1)
                elif pas < 3:
                    pool.wait_ge(agg_summed, done - 1)
                else:
                    pool.wait_ge(x_turned, (pas - 2) * G + 2 * i + b + 1)
                    pool.wait_ge(xs_copied, (pas - 3) * G + 2 * i + b + 1)
                pool.sem_inc(begun, 1)
                for j in range(8):
                    pool.indirect_dma_start(
                        rows[:, b, j, :], None, table,
                        bass.IndirectOffsetOnAxis(ap=idx[:, b, j:j + 1], axis=0)).then_inc(gathered[b], 16)
            with pool.Fori(0, HALF) as i:
                group(i, 0)
                group(i, 1)

        def weigh(eng, i, q, lo, hi):
            return eng.tensor_tensor(
                px[q % 2][:, lo:hi, 0:HC].rearrange("p j (h c) -> p j h c", h=H),
                logit[:, bass.ds(32 * i + 8 * q + lo, hi - lo), :].unsqueeze(3).broadcast_to([P, hi - lo, H, C]),
                xsring[:, q, lo:hi, :].unsqueeze(2).broadcast_to([P, hi - lo, H, C]), ALU.mult)

        def pool_weighs(pool, l):
            pool.wait_ge(weighed, l + 1)
            def group(i, q):
                pool.wait_ge(agg_summed, (3 + l) * G + 4 * i + q - 1)
                pool.wait_ge(xs_in[q], 16 * (l * (G // 4) + i + 1))
                weigh(pool, i, q, DVE_SLOTS, 8)
                sl = bass.ds(32 * i + 8 * q, 8)
                pool.tensor_tensor(px[q % 2][:, :, HC + H:HC + 2 * H], endmax[:, sl, :],
                                   last[:, sl].unsqueeze(2).broadcast_to([P, 8, H]), ALU.mult
                                   ).then_inc(px_made_pool, 1)
            with pool.Fori(0, G // 4) as i:
                for q in range(4):
                    group(i, q)

        @block.gpsimd
        def _(pool):
            pool.iota(iota[:, :], [[1, P]], 0, 0, allow_small_or_imprecise_dtypes=True).then_inc(consts_made, 1)
            pool.memset(ones[:, :], 1.0).then_inc(consts_made, 1)
            pool.wait_ge(consts_made, 2)
            pool.affine_select(ident[:, :], ones[:, :], [[-1, P]], ALU.is_equal, 0.0, 0, 1).then_inc(consts_made, 1)
            pool.iota(step_no[:, 0:STEPS], [[1, STEPS]], 0, 0, allow_small_or_imprecise_dtypes=True).then_inc(consts_made, 1)
            pool.iota(step_no[:, STEPS:STEPS + 4], [[P, 4]], 0, 1, allow_small_or_imprecise_dtypes=True
                      ).then_inc(consts_made, 1)
            pool.iota(lastmask[:, :], [[0, 1]], 0, 1, allow_small_or_imprecise_dtypes=True).then_inc(consts_made, 1)
            pool.wait_ge(steps_made, 1)
            for g in range(4):
                pool.indirect_dma_start(
                    blocks_i[:, g, :], None, edge_blocks,
                    bass.IndirectOffsetOnAxis(ap=block_no[:, g:g + 1], axis=0)).then_inc(blocks_in, 16)
            pool_gathers(pool, 0)
            pool_gathers(pool, 1)
            pool_gathers(pool, 2)
            for l in range(LAYERS):
                pool_gathers(pool, 3 + l)
                pool.memset(acc[:, :, :], 0.0).then_inc(acc_zeroed, 1)
                pool_weighs(pool, l)

        def window_of(eng, code, k):
            return nc.s_assert_within(eng.snap((code >> (5 * k)) & 31), 0, W - 1,
                                      skip_runtime_bounds_check_because="DVE clamps the windows that it packs")

        def load_windows(sp, which, i, b):
            done = which * G + 2 * i + b
            sp.wait_ge(xd_summed, done + 1)
            code = sp.value_load(packed[0:1, bass.ds(2 * i + b, 1)], min_val=0, max_val=(1 << 20) - 1)
            for k in range(4):
                w = window_of(sp, code, k)
                sp.dma_start(xwin[:, b, k, :], table[bass.ds(w * P, P), C:TAB].bitcast(BF16)
                             ).then_inc(xwin_in[b], 16)

        def sp_pass0(sp):
            sp.wait_ge(table_stored, 16)

            def front(i, b):
                load_windows(sp, 0, i, b)

            def back(i, b):
                sp.wait_ge(turned_made, 2 * i + b + 1)
                sp.dma_start(turned_dram[bass.ds(2 * i + b, 1), :, :].rearrange("a p c -> (a p) c"),
                             turned[:, b, :]).then_inc(turned_stored[b], 16)
            pipelined(sp, lambda f, k: (front(*f), back(*k)), front, back)
            for b in range(2):
                sp.wait_ge(turned_stored[b], 16 * (HALF + 1))

        def sp_gather_side(sp, l):
            sp.wait_ge(table_stored, 16 * (l + 4))

            def front(i, b):
                load_windows(sp, l + 1, i, b)
                sp.dma_start(turned[:, b, :], turned_dram[bass.ds(2 * i + b, 1), :, :].rearrange("a p c -> (a p) c")
                             ).then_inc(turned_in[b], 16)

            def back(i, b):
                sp.wait_ge(xs_copied, l * G + 2 * i + b + 3)
                sp.dma_start(xs_dram[bass.ds(2 * i + b, 1), :, :].rearrange("a p c -> (a p) c"),
                             xs[:, b, :, :].rearrange("p j c -> p (j c)")).then_inc(xs_stored[b], 16)
            pipelined(sp, lambda f, k: (front(*f), back(*k)), front, back)
            for b in range(2):
                sp.wait_ge(xs_stored[b], 16 * ((l + 1) * HALF + 1))

        def sp_sum_side(sp, l):
            sp.wait_ge(x_turned, (l + 2) * G + 2)
            def group(i, q):
                sp.wait_ge(px_made, l * G + 4 * i + q + 1)
                sp.wait_ge(px_made_pool, l * G + 4 * i + q + 1)
                sp.dma_start(xsring[:, q, :, :].rearrange("p j c -> p (j c)"),
                             xs_dram[bass.ds(4 * i + q, 1), :, :].rearrange("a p c -> (a p) c")
                             ).then_inc(xs_in[q], 16)
            with sp.Fori(0, G // 4) as i:
                for q in range(4):
                    group(i, q)

        def store_table(sp, n):
            sp.wait_ge(table_ready, n + 1)
            sp.dma_start(table.rearrange("(w p) c -> p w c", p=P), tab[:, :, :]).then_inc(table_stored, 16)

        @block.sync
        def _(sp):
            full = BLOCKS // P
            sp.dma_start(dst_i[:, 0:full * BLOCK].rearrange("p (g r) -> p g r", g=full),
                         edge_blocks[0:full * P, BLOCK:2 * BLOCK].rearrange("(p g) r -> p g r", g=full)
                         ).then_inc(edges_in, 16)
            sp.wait_ge(x_zeroed, 2)
            sp.dma_start(dst_i[0:BLOCKS - full * P, full * BLOCK:(full + 1) * BLOCK],
                         edge_blocks[full * P:BLOCKS, BLOCK:2 * BLOCK]).then_inc(edges_in, 16)
            sp.dma_start(X[:, 0:W - 1, :], x[0:(W - 1) * P, :].rearrange("(w p) c -> p w c", p=P)).then_inc(x_in, 16)
            sp.dma_start(X[0:LAST, W - 1, :], x[(W - 1) * P:N, :]).then_inc(x_in, 16)
            store_table(sp, 0)
            sp_pass0(sp)
            store_table(sp, 1)
            store_table(sp, 2)
            for l in range(LAYERS):
                store_table(sp, 3 + l)
                sp_gather_side(sp, l)
                sp_sum_side(sp, l)
            sp.wait_ge(table_ready, 4 + LAYERS)
            sp.dma_start(out[0:(W - 1) * P, :].rearrange("(w p) c -> p w c", p=P), X[:, 0:W - 1, :]).then_inc(out_stored, 16)
            sp.dma_start(out[(W - 1) * P:N, :], X[0:LAST, W - 1, :]).then_inc(out_stored, 16)
            sp.wait_ge(out_stored, 32)

        weights = [
            (w1[0:C, 0:HID], L0[0][C:2 * C, :]), (w1[2 * C:3 * C, HID:P], L0[0][C:2 * C, :]),
            (w1[C:2 * C, 0:HID], L0[0][0:C, :]), (w1[3 * C:4 * C, HID:P], L0[0][0:C, :]),
            (w1less[C:2 * C, :], L0[0][C:2 * C, :]), (w1less[3 * C:4 * C, :], L0[0][C:2 * C, :]),
            (w2[0:HID, 0, :], L0[2]), (w2[HID:P, 1, :], L0[2]), (w3[:, :], L0[4]), (w4[:, :], L0[6]),
            (bcol[0:HID, 0:1], L0[1].rearrange("(p a) -> p a", a=1)),
            (bcol[HID:P, 0:1], L0[1].rearrange("(p a) -> p a", a=1)),
            (bcol[:, 1:2], L0[3].rearrange("(p a) -> p a", a=1)),
            (b3row[:, :], L0[5].partition_broadcast(P)), (b4row[:, :], L0[7].partition_broadcast(P)),
            (wg[:, :], W_gcn), (bgrow[:, :], b_gcn.partition_broadcast(P)),
        ]
        for l, (Wl, Wr, att, bias, gamma, beta) in enumerate(gat):
            flat = att.rearrange("h c -> (h c)")
            weights += [(wcat[l][k * C:(k + 1) * C, k // 2, 0:HC], (Wl, Wr)[k % 2]) for k in range(4)]
            weights += [(wsum[l][:, 0:HC], Wr), (attrow[l][:, :], flat.partition_broadcast(P))]
            weights += [(brow[l][:, k, :], v.partition_broadcast(P)) for k, v in enumerate((bias, gamma, beta))]
            weights += [(wstk[l][q * C:(q + 1) * C, t, :], Wl[:, (4 * t + q) * C:(4 * t + q + 1) * C])
                        for q in range(4) for t in range(2)]

        def act_pass0(act):
            def front(i, b):
                g = 2 * i + b
                act.wait_ge(hot_turned, g + 1)
                act.wait_ge(turned_stored[b], 16 * (i + 1))
                act.activation(turned[:, b, :], ps[:, 0:2, :].rearrange("p k c -> p (k c)"), ACT.Copy
                               ).then_inc(turned_made, 1)

            def front2(i, b):
                act.wait_ge(x_turned, 2 * i + b + 3)
                act.activation(xT[:, b, :], ps[:, 3, :], ACT.Copy).then_inc(xT_copied, 1)

            def back(i, b):
                g = 2 * i + b
                act.wait_ge(h1_summed, g + 1)
                act.activation(h1, ps[:, 4, :], ACT.Relu, bias=bcol[:, 0:1]).then_inc(h1_made, 1)

            def back2(i, b):
                g = 2 * i + b
                act.wait_ge(h2_summed, g + 1)
                act.activation(h2, ps[:, 5:7, :].rearrange("p k c -> p (k c)"), ACT.Relu, bias=bcol[:, 1:2]
                               ).then_inc(h2_made, 1)

            def steps(ahead, f, k, behind):
                if k:
                    back(*k)
                    back2(*k)
                if f:
                    front2(*f)
                if ahead:
                    front(*ahead)
            pipelined_by_three(act, steps)

        def pair(b, k):
            n = 2 + 2 * ((4 * b + k) % 3)
            return ps[:, n:n + 2, :]

        def act_gather_side(act, l):
            base = (l + 1) * G

            def front(i, b):
                g = 2 * i + b
                act.wait_ge(gathered[b], 128 * ((3 + l) * HALF + i + 1))
                act.wait_ge(xs_stored[b], 16 * (l * HALF + i + 1))
                act.activation(xs[:, b, :, :], rows[:, b, :, 0:C], ACT.Copy).then_inc(xs_copied, 1)
                act.wait_ge(x_turned, base + g + 3)
                act.activation(xT[:, b, :], ps[:, b, :], ACT.Copy).then_inc(xT_copied, 1)

            def back(i, b):
                for k in range(4):
                    act.wait_ge(z_summed, l * 4 * G + 8 * i + 4 * b + k + 1)
                    act.activation(lin[:, b, 2 * k:2 * k + 2, :], pair(b, k)[:, :, HC:ZC], ACT.Copy
                                   ).then_inc(lin_copied, 1)

            def both(f, k):
                back(*k)
                front(*f)
            pipelined(act, both, front, back)

        def act_sum_side(act, l):
            act.wait_ge(maxima_taken, (l + 1) * (SG // 4))
            act.activation(logit[:, :, :], logit[:, :, :], ACT.Exp).then_inc(weighed, 1)
            act.wait_ge(weighed, l + 1)
            def group(i, b):
                act.wait_ge(agg_summed, (3 + l) * G + 2 * i + b - 1)
                sl = bass.ds(16 * i + 8 * b, 8)
                act.activation(px[b][:, :, HC:HC + H], logit[:, sl, :], ACT.Copy).then_inc(p_made, 1)
            with act.Fori(0, HALF) as i:
                group(i, 0)
                group(i, 1)

        def act_small(act, n, rows_):
            act.wait_ge(small_turned, n + 1)
            for k in range(NT):
                c = min(512, W * P - 512 * k)
                act.activation(nodeT[0:rows_, 512 * k:512 * k + c], ps[0:rows_, k, 0:c], ACT.Copy
                               ).then_inc(small_copied, 1)

        def act_root(act, n):
            act.wait_ge(root_asked, n + 1)
            act.activation(root[:, 0:powers[n].shape[1]], powers[n], ACT.Sqrt).then_inc(root_done, 1)

        @block.scalar
        def _(act):
            act.wait_ge(weights_zeroed, 2 + LAYERS)
            for dst, srcw in weights:
                act.dma_start(dst, srcw).then_inc(weights_in, 16)
            for n in range(2 * SG // 4):
                act.wait_ge(flags_turned, n + 1)
                tile = (newF, newR)[n // (SG // 4)]
                k = n % (SG // 4)
                act.activation(tile[:, 4 * k:4 * k + 4, :].rearrange("p g e -> p (g e)"), ps[:, n % 8, :], ACT.Copy
                               ).then_inc(flags_copied, 1)
            act_pass0(act)
            act_small(act, 0, HID)
            for n in range(4):
                act_root(act, n)
            act_small(act, 1, C)
            act_root(act, 4)
            for l in range(LAYERS):
                act_small(act, 2 + l, C)
                act_gather_side(act, l)
                for n in range(SG // 4):
                    act.wait_ge(order_turned, l * (SG // 4) + n + 1)
                    act.activation(order1[:, 4 * n:4 * n + 4, :].rearrange("p g e -> p (g e)"), ps[:, n % 4, :],
                                   ACT.Copy).then_inc(order_copied, 1)
                for n in range(SG // 4):
                    act.wait_ge(back_turned, l * (SG // 4) + n + 1)
                    act.activation(endmax.rearrange("p (j g) h -> p g j h", j=JB)[:, 4 * n:4 * n + 4, :, :],
                                   ps[:, n % 4, :].rearrange("p (g j h) -> p g j h", g=4, j=JB),
                                   ACT.Copy).then_inc(back_copied, 1)
                act_sum_side(act, l)
                act.wait_ge(exp_asked, l + 1)
                act.activation(selfcol[:, 0:2, :, :], selfcol[:, 0:2, :, :], ACT.Exp).then_inc(exp_done, 1)
                for n in range(YT):
                    c = min(4, 2 * W - 4 * n) * P
                    act.wait_ge(y_turned, l * YT + n + 1)
                    act.activation(yT[:, 512 * n:512 * n + c], ps[:, 1 + n % 6, 0:c], ACT.Copy).then_inc(y_copied, 1)
                act_root(act, 5 + l)
            act_root(act, 5 + LAYERS)

        def pe_dst_rows(pe, b, bank):
            for j in range(8):
                q = 64 * (j % 2) + C
                for s in range(3):
                    mm = pe.matmul(ps[q:q + C, bank, (j // 2) * P:(j // 2 + 1) * P],
                                   xwin[:, b, j // 2, s * C:(s + 1) * C], turned[:, b, j * P:(j + 1) * P],
                                   start=(s == 0), stop=(s == 2))
            mm.then_inc(xd_summed, 1)

        def pe_src_rows(pe, b, bank):
            for j in range(8):
                q = 64 * (j % 2)
                for s in range(3):
                    mm = pe.matmul(ps[q:q + C, bank, (j // 2) * P:(j // 2 + 1) * P],
                                   rowparts[b][:, j, 2 * C + s * C:2 * C + (s + 1) * C], identb[:, :],
                                   start=(s == 0), stop=(s == 2))
            mm.then_inc(x_turned, 1)

        def pe_pass0(pe):
            def front_a(i, b):
                pe.wait_ge(hotb_made, 2 * i + b + 1)
                for j in range(8):
                    mm = pe.matmul(ps[:, j // 4, (j % 4) * P:(j % 4 + 1) * P], hotb[:, b, j, :], identb[:, :],
                                   start=True, stop=True)
                mm.then_inc(hot_turned, 1)

            def front_b(i, b):
                pe.wait_ge(turned_made, 2 * i + b + 1)
                pe.wait_ge(xwin_in[b], 64 * (i + 1))
                pe_dst_rows(pe, b, 3)

            def front_c(i, b):
                pe.wait_ge(gathered[b], 128 * (i + 1))
                pe_src_rows(pe, b, 3)

            def back_a(i, b):
                g = 2 * i + b
                pe.wait_ge(xT_copied, g + 1)
                pe.matmul(ps[:, 4, :], w1[:, :], xT[:, b, :], start=True, stop=True).then_inc(h1_summed, 1)

            def back_b(i, b):
                pe.wait_ge(h1_made, 2 * i + b + 1)
                for q in range(2):
                    mm = pe.matmul(ps[:, 5 + q, :], w2[:, q, :], h1, start=True, stop=True)
                mm.then_inc(h2_summed, 1)

            def back_c(i, b):
                pe.wait_ge(h2_made, 2 * i + b + 1)
                for j in range(8):
                    at = (j % 2) * 512 + (j // 2) * P
                    mm = pe.matmul(ps[:, 7, j * HID:(j + 1) * HID], h2[:, at:at + P], w3[:, :], start=True, stop=True)
                mm.then_inc(h3_summed, 1)

            def back_d(i, b):
                pe.wait_ge(h3_made, 2 * i + b + 1)
                pe.wait_ge(hot_made, 2 * i + b + 1)
                pe.wait_ge(acc_added, 8 * i + 4 * b + 1)
                for j in range(8):
                    k = j // 2
                    mm = pe.matmul(ps[:, 2, k * (HID + 1):(k + 1) * (HID + 1)], hot[:, b, j, :], h3[:, j, :],
                                   start=(j % 2 == 0), stop=(j % 2 == 1))
                mm.then_inc(agg_summed, 1)

            def steps(ahead, f, k, behind):
                for step, group in ((back_a, k), (front_b, f), (back_d, behind), (back_b, k), (front_c, f),
                                    (front_a, ahead), (back_c, k)):
                    if group:
                        step(*group)
            pipelined_by_three(pe, steps)

        def pe_gcn(pe, pas):
            base = pas * G

            def group(i, b):
                g = base + 2 * i + b
                if pas == 1:
                    pe.wait_ge(srchot_made, 4 * i + 2 * b + 2)
                    for j in range(8):
                        pe.matmul(ps[:, 7, 0:W], srchot[:, b, j, 0:P], srchot[:, b, j, P:P + W],
                                  start=False, stop=False, skip_group_check=True)
                pe.wait_ge(hot_made, g + 1)
                pe.wait_ge(gathered[b], 128 * (pas * HALF + i + 1))
                pe.wait_ge(acc_added, 4 * g - 3)
                for j in range(8):
                    k = j // 2
                    mm = pe.matmul(ps[:, b, k * 3 * C:(k + 1) * 3 * C], hotb[:, b, j, :],
                                   rowparts[b][:, j, 2 * C:5 * C],
                                   start=(j % 2 == 0), stop=(j % 2 == 1))
                mm.then_inc(agg_summed, 1)
            if pas == 1:
                pe.wait_ge(zeros_made, 1)
                pe.wait_ge(srchot_made, 2)
                pe.matmul(ps[:, 7, 0:W], zeros[:, 0:P], zeros[:, 0:W], start=True, stop=False, skip_group_check=True)
            with pe.Fori(0, HALF) as i:
                group(i, 0)
                group(i, 1)
            if pas == 1:
                pe.matmul(ps[:, 7, 0:W], zeros[:, 0:P], zeros[:, 0:W], start=False, stop=True,
                          skip_group_check=True).then_inc(degree_summed, 1)

        def pe_gather_side(pe, l):
            base = (l + 1) * G

            def front_a(i, b):
                pe.wait_ge(turned_in[b], 16 * (l * HALF + i + 1))
                pe.wait_ge(xwin_in[b], 64 * ((l + 1) * HALF + i + 1))
                pe_dst_rows(pe, b, b)

            def front_b(i, b):
                pe.wait_ge(gathered[b], 128 * ((3 + l) * HALF + i + 1))
                pe_src_rows(pe, b, b)

            def back(i, b):
                pe.wait_ge(xT_copied, base + 2 * i + b + 1)
                for k in range(4):
                    n = l * 4 * G + 8 * i + 4 * b + k
                    pe.wait_ge(prod_made, n + 1 + (b == 0 and k < 2))
                    for q in range(2):
                        mm = pe.matmul(pair(b, k)[:, q, 0:ZC], xT[:, b, k * P:(k + 1) * P], wcat[l][:, q, :],
                                       start=True, stop=True)
                    mm.then_inc(z_summed, 1)

            def both(f, k):
                front_a(*f)
                back(*k)
                front_b(*f)
            pe.wait_ge(zn_read, (l + 1) * W)
            pipelined(pe, both, lambda i, b: (front_a(i, b), front_b(i, b)), back)

        def pe_order(pe, l):
            for n in range(SG // 4):
                if n >= 4:
                    pe.wait_ge(order_copied, l * (SG // 4) + n - 3)
                pe.wait_ge(order_staged, l * (SG // 4) + n + 1)
                for k in range(4):
                    mm = pe.transpose(ps[:, n % 4, k * P:(k + 1) * P], staged[:, n % 2, k * P:(k + 1) * P], ident[:, :])
                mm.then_inc(order_turned, 1)
            for k in range(2):
                pe.wait_ge(carry_asked, 4 * l + 2 * k + 1 + 2)
                pe.transpose(ps[0:1, 4, 0:P], carrycol[:, 2 * k:2 * k + 1], ident[:, :]).then_inc(carry_turned, 1)
                pe.wait_ge(carry_asked, 4 * l + 2 * k + 2 + 2)
                pe.transpose(ps[:, 5, 0:1], carry[0:1, 2 * k + 1, :], ident[0:1, 0:1]).then_inc(carry_turned, 1)
            pe.wait_ge(back_asked, l + 1)
            for n in range(SG // 4):
                if n >= 4:
                    pe.wait_ge(back_copied, l * (SG // 4) + n - 3)
                for k in range(4):
                    mm = pe.transpose(ps[:, n % 4, k * P:(k + 1) * P], order1[:, 4 * n + k, :], ident[:, :])
                mm.then_inc(back_turned, 1)

        def pe_sum_side(pe, l):
            def group(i, b):
                g = l * G + 2 * i + b
                pe.wait_ge(halves_made, 2 * g + 2)
                pe.wait_ge(p_made, g + 1)
                pe.wait_ge(px_made, g + 5)
                pe.wait_ge(px_made_pool, g + 5)
                pe.wait_ge(acc_added, 12 * G + 4 * g - 3)
                for j in range(8):
                    mm = pe.matmul(ps[:, 4 * b + j // 2, 0:HC + 2 * H], hot[:, b, j, :], px[b][:, j, :],
                                   start=(j % 2 == 0), stop=(j % 2 == 1))
                mm.then_inc(agg_summed, 1)
            with pe.Fori(0, HALF) as i:
                group(i, 0)
                group(i, 1)

        def pe_small(pe, n, src_, cols, weight):
            pe.wait_ge(small_asked, n + 1)
            for w in range(W):
                mm = pe.transpose(ps[0:cols, w // 4, (w % 4) * P:(w % 4 + 1) * P], src_[:, w, 0:cols], ident[:, :])
            mm.then_inc(small_turned, 1)
            pe.wait_ge(small_copied, NT * (n + 1))
            if weight is not None:
                for w in range(W):
                    mm = pe.matmul(out_at(w), nodeT[0:cols, w * P:(w + 1) * P], weight, start=True, stop=True)
                mm.then_inc(small_summed, 1)

        def out_at(w):
            return ps[:, 7, w * C:(w + 1) * C] if w < 16 else ps[:, 0, (w - 16) * C:(w - 15) * C]

        def pe_self_sums(pe, l):
            for w in range(W):
                if w >= 8:
                    pe.wait_ge(zn_read, l * W + w - 7)
                pe.matmul(ps[:, w % 8, 0:ZC], nodeT[0:C, w * P:(w + 1) * P], wsum[l][:, :],
                          start=True, stop=True).then_inc(zn_summed, 1)

        def pe_attention_out(pe, l):
            pe.wait_ge(y_asked, l + 1)
            for n in range(YT):
                if n >= 6:
                    pe.wait_ge(y_copied, l * YT + n - 5)
                for k in range(4 * n, min(4 * n + 4, 2 * W)):
                    w, t = k // 2, k % 2
                    mm = pe.transpose(ps[:, 1 + n % 6, (k % 4) * P:(k % 4 + 1) * P], ysum[:, w, t * P:(t + 1) * P],
                                      ident[:, :])
                mm.then_inc(y_turned, 1)
            pe.wait_ge(y_copied, (l + 1) * YT)
            for w in range(W):
                for t in range(2):
                    mm = pe.matmul(out_at(w), yT[:, (2 * w + t) * P:(2 * w + t + 1) * P], wstk[l][:, t, :],
                                   start=(t == 0), stop=(t == 1))
            mm.then_inc(y_summed, 1)
            for s in range(2):
                pe.wait_ge(bn_asked, 2 * l + s + 1)
                pe.matmul(ps[:, 1 + s, 0:C], ones[:, :], bn[:, 0, :], start=True, stop=True).then_inc(bn_summed, 1)

        @block.tensor
        def _(pe):
            pe.sem_inc(xd_summed, 2)
            pe.sem_inc(x_turned, 2)
            for b in range(2):
                pe.sem_inc(turned_stored[b], 16)
                pe.sem_inc(xs_stored[b], 16)
            pe.sem_inc(xs_copied, 2)
            pe.sem_inc(prod_made, 3)
            pe.sem_inc(acc_added, 1)
            pe.wait_ge(consts_made, 6)
            pe.wait_ge(counts_made, 1)
            pe.matmul(ps[:, 0, 0:W - 1], ones[:, :], win[:, 0, 1:W], start=True, stop=True).then_inc(counts_summed, 1)
            pe.wait_ge(blocks_floated, 1)
            for g in range(4):
                for rp in range(2):
                    for k in range(4):
                        r, hf = 2 * rp + k // 2, k % 2
                        at = r * BLOCK + hf * P
                        mm = pe.transpose(ps[:, 2 * g + rp, k * P:(k + 1) * P], blocks_f[:, g, at:at + P], ident[:, :])
                    mm.then_inc(slots_turned, 1)
            pe.wait_ge(flags_spread, 1)
            for n in range(2 * SG // 4):
                spread = spreads[n // (SG // 4)].rearrange("p g j h -> p g (j h)")
                if n >= 8:
                    pe.wait_ge(flags_copied, n - 7)
                for k in range(4):
                    mm = pe.transpose(ps[:, n % 8, k * P:(k + 1) * P], spread[:, 4 * (n % (SG // 4)) + k, :], ident[:, :])
                mm.then_inc(flags_turned, 1)
            pe.wait_ge(flags_copied, 2 * SG // 4)
            pe.wait_ge(weights_made, 1)
            pe_pass0(pe)
            pe_small(pe, 0, acc, HID, w4[:, :])
            pe_gcn(pe, 1)
            pe.wait_ge(carry_asked, 1)
            for k in range(2):
                pe.transpose(ps[0:1, k, 0:P], anyreset[:, k:k + 1], ident[:, :]).then_inc(carry_turned, 1)
            pe.wait_ge(carry_asked, 2)
            pe_gcn(pe, 2)
            pe_small(pe, 1, T1, C, wg[:, :])
            for l in range(LAYERS):
                pe_small(pe, 2 + l, X, C, None)
                pe_self_sums(pe, l)
                pe_gather_side(pe, l)
                pe_order(pe, l)
                pe_sum_side(pe, l)
                pe_attention_out(pe, l)

        def wide(ap, cols):
            return ap.unsqueeze(2).broadcast_to([ap.shape[0], ap.shape[1], cols])

        def down(ap, k):
            return ap.unsqueeze(1).broadcast_to([ap.shape[0], k, ap.shape[1]])

        @block.vector
        def _(v):
            chain = [0]

            def link(ins):
                chain[0] += 1
                ins.then_inc(linked, 1)
                v.wait_ge(linked, chain[0])

            def tt(o, a, b, op):
                link(v.tensor_tensor(o, a, b, op))

            def ts(o, a, s1, s2, op0, op1=ALU.bypass):
                link(v.tensor_scalar(o, a, s1, s2, op0, op1))

            def stt(o, a, s_, b, op0, op1):
                link(v.scalar_tensor_tensor(o, a, s_, b, op0, op1))

            def cp(o, a):
                link(v.tensor_copy(o, a))

            asked = [0]

            def rsqrt():
                x_ = powers[asked[0]]
                asked[0] += 1
                v.sem_inc(root_asked, 1)
                v.wait_ge(root_done, asked[0])
                r_, t_ = root[:, 0:x_.shape[1]], root[:, C:C + x_.shape[1]]
                link(v.reciprocal(r_, r_))
                tt(t_, x_, r_, ALU.mult)
                tt(t_, t_, r_, ALU.mult)
                ts(t_, t_, -0.5, 1.5, ALU.mult, ALU.add)
                tt(x_, r_, t_, ALU.mult)

            def layernorm(of):
                mean, var = nodecol[:, 1, :], nodecol[:, 2, :]
                link(v.tensor_reduce(mean, of, AX.X, ALU.add))
                ts(mean, mean, 1.0 / C, None, ALU.mult)
                tt(T2[:, :, :], of, wide(mean, C), ALU.subtract)
                tt(rest[:, :, :], T2[:, :, :], T2[:, :, :], ALU.mult)
                link(v.tensor_reduce(var, rest[:, :, :], AX.X, ALU.add))
                ts(var, var, 1.0 / C, EPS, ALU.mult, ALU.add)
                rsqrt()
                tt(X[:, :, :], T2[:, :, :], wide(var, C), ALU.mult)

            def give_table(of):
                hi, mid, lo = (tabparts[:, :, (2 + k) * C:(3 + k) * C] for k in range(3))
                cp(tab[:, :, 0:C], of)
                cp(hi, of)
                tt(T2[:, :, :], of, hi, ALU.subtract)
                cp(mid, T2[:, :, :])
                tt(T2[:, :, :], T2[:, :, :], mid, ALU.subtract)
                cp(lo, T2[:, :, :])
                v.sem_inc(table_ready, 1)

            def out_parts():
                return [(slice(0, 16), ps[:, 7, :].rearrange("p (w c) -> p w c", c=C)),
                        (slice(16, W), ps[:, 0, 0:(W - 16) * C].rearrange("p (w c) -> p w c", c=C))]

            def make_hot(i, b, to, made):
                v.tensor_tensor(to[:, b, :, :], wide(dloc[:, bass.ds(16 * i + 8 * b, 8)], P),
                                down(iota[:, :], 8), ALU.is_equal).then_inc(made, 1)

            def stage(pas, i, b):
                v.wait_ge(gathered[b], 128 * (pas * HALF + i + 1))
                v.tensor_copy(idx[:, b, :], src[:, bass.ds(16 * i + 8 * b + 16, 8)]).then_inc(idx_ready, 1)

            def add_steps(pas, i, b, banks, cols, between=()):
                g = pas * G + 2 * i + b
                code = v.value_load(packed[0:1, bass.ds(2 * i + b, 1)], min_val=0, max_val=(1 << 20) - 1)
                windows = [window_of(v, code, k) for k in range(4)]
                v.wait_ge(agg_summed, g + 1)
                for k, w in enumerate(windows):
                    at = acc[:, bass.ds(w, 1), 0:cols].rearrange("p a c -> p (a c)")
                    v.wait_ge(acc_added, 4 * g + k + 1)
                    v.tensor_tensor(at, at, banks[k], ALU.add).then_inc(acc_added, 1)
                    if k < len(between):
                        between[k]()

            for t in [w1[:, :], w2[:, :, :]] + [w[:, :, :] for w in wcat]:
                v.memset(t, 0.0).then_inc(weights_zeroed, 1)

            v.sem_inc(px_made_pool, 4)
            v.sem_inc(px_made, 4)
            v.memset(dst_i[:, (BLOCKS // P) * BLOCK:], NO_NODE).then_inc(x_zeroed, 1)
            v.memset(X[:, W - 1, :], 0.0).then_inc(x_zeroed, 1)
            v.memset(zeros[:, :], 0.0).then_inc(zeros_made, 1)
            v.wait_ge(edges_in, 32)
            v.wait_ge(x_zeroed, 2)
            cp(dst_all, dst_i)
            for w in range(1, W):
                link(v.tensor_scalar(junk, dst_all, float(P * w), 0.0, ALU.is_lt, ALU.add, accum_out=win[:, 0, w:w + 1]))
            v.sem_inc(counts_made, 1)
            before, blk0, blk1, steps, some = (win[:, k, :] for k in range(1, 6))
            ends, starts, shift, incr = (win[:, k, :] for k in range(6, 10))
            link(v.memset(before[:, 0:1], 0.0))
            link(v.memset(before[:, W:W + 1], float(E)))
            v.wait_ge(counts_summed, 1)
            cp(before[:, 1:W], ps[:, 0, 0:W - 1])
            cp(win_i[:, 0, :], before)
            ts(win_i[:, 0, :], win_i[:, 0, :], 8, None, ALU.arith_shift_right)
            cp(blk0, win_i[:, 0, :])
            ts(win_i[:, 1, :], before, float(BLOCK - 1), None, ALU.add)
            ts(win_i[:, 1, :], win_i[:, 1, :], 8, None, ALU.arith_shift_right)
            cp(blk1, win_i[:, 1, :])
            tt(steps[:, 0:W], blk1[:, 1:W + 1], blk0[:, 0:W], ALU.subtract)
            tt(some[:, 0:W], before[:, 1:W + 1], before[:, 0:W], ALU.is_gt)
            tt(steps[:, 0:W], steps[:, 0:W], some[:, 0:W], ALU.mult)
            v.wait_ge(consts_made, 6)
            link(v.tensor_tensor_scan(ends[:, 0:W], ones[:, 0:W], steps[:, 0:W], 0.0, ALU.mult, ALU.add))
            link(v.memset(starts[:, 0:1], 0.0))
            cp(starts[:, 1:W + 1], ends[:, 0:W])
            tt(shift, blk0, starts, ALU.subtract)
            tt(incr[:, 0:W], shift[:, 1:W + 1], shift[:, 0:W], ALU.subtract)
            link(v.memset(step_win, 0.0))
            cp(step_blk, step_no)
            for w in range(W):
                ts(step_tmp, step_no, ends[:, w:w + 1], None, ALU.is_ge)
                tt(step_win, step_win, step_tmp, ALU.add)
                stt(step_blk, step_tmp, incr[:, w:w + 1], step_blk, ALU.mult, ALU.add)
            ts(step_blk, step_blk, float(BLOCKS - 1), 0.0, ALU.min, ALU.max)
            cp(block_no[:, :], step_blk[:, STEPS:STEPS + 4])
            v.sem_inc(steps_made, 1)
            ts(step_tmp, step_win, float(W - 1), None, ALU.min)
            quad = step_tmp[0:1, 0:STEPS].rearrange("p (g k) -> p g k", k=4)
            code = win[0:1, :, :].rearrange("p a b -> p (a b)")[:, 0:G]
            stt(code, quad[:, :, 3], 32.0, quad[:, :, 2], ALU.mult, ALU.add)
            stt(code, code, 32.0, quad[:, :, 1], ALU.mult, ALU.add)
            stt(code, code, 32.0, quad[:, :, 0], ALU.mult, ALU.add)
            cp(packed[:, :], code)

            v.wait_ge(blocks_in, 64)
            for g in range(4):
                cp(blocks_f[:, g, :], blocks_i[:, g, :])
            v.sem_inc(blocks_floated, 1)
            for g in range(4):
                ns = min(P, STEPS - P * g)
                for r, to in enumerate((src[:, 0:SLOTS], dstf, prevf, nextf)):
                    v.wait_ge(slots_turned, 2 * g + r // 2 + 1)
                    for hf in range(2):
                        k = (r % 2) * 2 + hf
                        cp(to.rearrange("p (s f) -> p s f", f=2)[:, P * g:P * g + ns, hf],
                           ps[:, 2 * g + r // 2, k * P:k * P + ns])
            stt(dloc[:, :].rearrange("p (s f) -> p s f", f=2), wide(step_win[:, 0:STEPS], 2), -float(P),
                dstf.rearrange("p (s f) -> p s f", f=2), ALU.mult, ALU.add)
            ts(sltmp, dloc[:, :], 0.0, None, ALU.is_ge)
            stt(valid, dloc[:, :], float(P - 1), sltmp, ALU.is_le, ALU.mult)
            ts(gone[:, :], valid, 1.0, BIG, ALU.subtract, ALU.mult)
            tt(sltmp, dstf, prevf, ALU.not_equal)
            stt(prevf, sltmp, -BIG, valid, ALU.mult, ALU.mult)
            tt(sltmp, dstf, nextf, ALU.not_equal)
            tt(last[:, :], sltmp, valid, ALU.mult)
            def in_order(ap):
                return ap.rearrange("p (j g) -> p g j", j=JB).unsqueeze(3).broadcast_to([P, SG, JB, H])
            cp(spreads[0], in_order(prevf))
            ts(spreads[1], in_order(last[:, :]), -BIG, None, ALU.mult)
            v.sem_inc(flags_spread, 1)
            cp(src[:, SLOTS:SLOTS + 16], src[:, 0:16])
            slint = sltmp.bitcast(I32)
            cp(slint, src[:, 0:SLOTS])
            ts(slint, slint, 7, None, ALU.arith_shift_right)
            cp(src_a, slint)
            stt(src_b, src_a, -float(P), src[:, 0:SLOTS], ALU.mult, ALU.add)
            tt(src_a, src_a, gone[:, :], ALU.add)

            v.wait_ge(weights_in, 16 * len(weights))
            for q in (1, 3):
                at = w1[q * C:(q + 1) * C, (q // 2) * HID:(q // 2 + 1) * HID]
                tt(at, at, w1less[q * C:(q + 1) * C, :], ALU.subtract)
            ts(lastmask[:, :], lastmask[:, :], float(LAST), None, ALU.is_lt)
            cp(identb[:, :], ident[:, :])
            v.sem_inc(weights_made, 1)
            v.wait_ge(x_in, 32)
            give_table(X[:, :, :])
            v.wait_ge(table_stored, 16)
            v.wait_ge(flags_copied, 2 * SG // 4)
            link(v.memset(acc[:, :, 0:HID + 1], 0.0))
            link(v.memset(h3[:, :, HID:HID + 1], 1.0))
            for b in range(2):
                v.tensor_copy(idx[:, b, :], src[:, 8 * b:8 * b + 8]).then_inc(idx_ready, 1)

            def bias0(i, b):
                g = 2 * i + b
                v.wait_ge(h3_summed, g + 1)
                v.tensor_tensor(h3[:, :, 0:HID], ps[:, 7, :].rearrange("p (j c) -> p j c", j=8),
                                down(b3row[:, :], 8), ALU.add).then_inc(h3_biased, 1)
                v.wait_ge(h3_biased, g + 1)
                v.tensor_scalar(h3[:, :, 0:HID], h3[:, :, 0:HID], 0.0, None, ALU.max).then_inc(h3_made, 1)

            def steps0(ahead, f, k, behind):
                if ahead:
                    if k:
                        v.wait_ge(hot_turned, 2 * ahead[0] + ahead[1] - 1)
                    make_hot(*ahead, hotb, hotb_made)
                if behind:
                    add0(*behind)
                if f:
                    make_hot(*f, hot, hot_made)
                    stage(0, *f)
                if k:
                    bias0(*k)

            def add0(i, b):
                add_steps(0, i, b, [ps[:, 2, k * (HID + 1):(k + 1) * (HID + 1)] for k in range(4)], HID + 1)

            pipelined_by_three(v, steps0)
            v.wait_ge(acc_added, 4 * G + 1)
            v.sem_inc(small_asked, 1)
            count, most, inv, rs, dis, out_rs = (nodecol[:, k, :] for k in (0, 1, 3, 4, 5, 7))
            cp(count, acc[:, :, HID])
            ts(most, count, 1.0, None, ALU.max)
            link(v.reciprocal(inv, most))
            cp(rs, most)
            ts(empty[:, :], count, 0.0, -BIG, ALU.is_equal, ALU.mult)
            v.wait_ge(small_summed, 1)
            tt(T1[:, :, :], wide(count, C), down(b4row[:, :], W), ALU.mult)
            for w, o in out_parts():
                tt(T1[:, w, :], T1[:, w, :], o, ALU.add)
            tt(T1[:, :, :], T1[:, :, :], wide(inv, C), ALU.mult)
            tt(T1[:, :, :], T1[:, :, :], X[:, :, :], ALU.add)
            layernorm(T1[:, :, :])
            rsqrt()
            ts(dis, count, 0.0, None, ALU.is_gt)
            tt(dis, dis, rs, ALU.mult)

            def gcn(pas):
                def front(i, b):
                    if pas == 1:
                        sl = bass.ds(16 * i + 8 * b, 8)
                        v.tensor_tensor(srchot[:, b, :, 0:P], wide(src_b[:, sl], P), down(iota[:, :], 8), ALU.is_equal
                                        ).then_inc(srchot_made, 1)
                        v.tensor_tensor(srchot[:, b, :, P:P + W], wide(src_a[:, sl], W), down(iota[:, 0:W], 8),
                                        ALU.is_equal).then_inc(srchot_made, 1)
                    make_hot(i, b, hotb, hot_made)
                    stage(pas, i, b)

                def back(i, b):
                    add_steps(pas, i, b, [ps[:, b, k * 3 * C:(k + 1) * 3 * C] for k in range(4)], 3 * C)
                link(v.memset(acc[:, :, 0:3 * C], 0.0))
                v.wait_ge(table_stored, 16 * (pas + 1))
                pipelined(v, lambda f, k: (front(*f), back(*k)), front, back)
                v.wait_ge(acc_added, 4 * G * (pas + 1) + 1)
                tt(T1[:, :, :], acc[:, :, 0:C], acc[:, :, C:2 * C], ALU.add)
                tt(acc[:, :, 0:C], T1[:, :, :], acc[:, :, 2 * C:3 * C], ALU.add)

            tt(T1[:, :, :], X[:, :, :], wide(dis, C), ALU.mult)
            give_table(T1[:, :, :])
            tmp2 = o2[:, 0:2 * HC].rearrange("p (k c) -> p k c", k=2)
            tmp = o2[0:C, 0:HC]
            for l in range(LAYERS):
                stt(tmp2, wcat[l][:, :, 0:HC], 0.2, down(attrow[l][:, :], 2), ALU.mult, ALU.mult)
                for k in range(2):
                    link(v.tensor_reduce(wcat[l][:, k, HC:ZC], tmp2[:, k, :].rearrange("p (h c) -> p h c", h=H),
                                         AX.X, ALU.add))
                tt(wsum[l][:, 0:HC], wsum[l][:, 0:HC], wcat[l][0:C, 0, 0:HC], ALU.add)
                stt(tmp, wsum[l][:, 0:HC], 0.2, attrow[l][0:C, :], ALU.mult, ALU.mult)
                link(v.tensor_reduce(wsum[l][:, HC:ZC], tmp.rearrange("p (h c) -> p h c", h=H), AX.X, ALU.add))
                ts(attrow[l][:, :], attrow[l][:, :], 0.8, None, ALU.mult)
            gcn(1)
            tt(T1[:, :, :], acc[:, :, 0:C], wide(dis, C), ALU.mult)
            tt(T1[:, :, :], T1[:, :, :], X[:, :, :], ALU.add)
            layernorm(T1[:, :, :])
            v.wait_ge(degree_summed, 1)
            ts(out_rs, ps[:, 7, 0:W], 1.0, None, ALU.max)
            rsqrt()

            tt(T1[:, :, :], X[:, :, :], wide(out_rs, C), ALU.mult)
            give_table(T1[:, :, :])
            v.wait_ge(flags_copied, 2 * SG // 4)
            for k, f in enumerate((newF, newR)):
                link(v.tensor_reduce(anyreset[:, k:k + 1], f[:, :, :], AX.XY, ALU.min))
            v.sem_inc(carry_asked, 1)
            v.wait_ge(carry_turned, 2)
            for k in range(2):
                cp(resetrow[0:1, k, :], ps[0:1, k, 0:P])
            v.sem_inc(carry_asked, 1)

            gcn(2)
            tt(T1[:, :, :], acc[:, :, 0:C], wide(rs, C), ALU.mult)
            v.sem_inc(small_asked, 1)
            v.wait_ge(small_summed, 2)
            for w, o in out_parts():
                tt(T2[:, w, :], o, down(bgrow[:, :], w.stop - w.start), ALU.add)
            stt(T1[:, :, :], T2[:, :, :], 0.0, X[:, :, :], ALU.max, ALU.add)
            layernorm(T1[:, :, :])
            cp(X0[:, :, :], X[:, :, :])

            stretch = [(JB - 1) * H + h for h in range(H)]

            def scans(l):
                begin = newF[:, :, :].rearrange("p a b -> p (a b)")
                end = newR[:, :, :].rearrange("p a b -> p (a b)")
                L = SG * P

                def carries(k, column, resets):
                    cp(carrycol[:, 2 * k:2 * k + 1], column)
                    v.sem_inc(carry_asked, 1)
                    v.wait_ge(carry_turned, 2 + 4 * l + 2 * k + 1)
                    cp(carry[0:1, 2 * k, :], ps[0:1, 4, 0:P])
                    link(v.memset(carry[0:1, 2 * k + 1, :], -BIG))
                    got = carry[0:1, 2 * k, :].rearrange("p (j h) -> p h j", h=H)
                    res = resets.rearrange("p (j h) -> p h j", h=H)
                    to = carry[0:1, 2 * k + 1, :].rearrange("p (j h) -> p h j", h=H)
                    for h in range(H):
                        if k == 0:
                            o, a, c = to[:, h, 1:JB], res[:, h, 0:JB - 1], got[:, h, 0:JB - 1]
                        else:
                            o, a, c = to[:, h, JB - 2::-1], res[:, h, JB - 1:0:-1], got[:, h, JB - 1:0:-1]
                        link(v.tensor_tensor_scan(o, a, c, -BIG, ALU.add, ALU.max))
                    v.sem_inc(carry_asked, 1)
                    v.wait_ge(carry_turned, 2 + 4 * l + 2 * k + 2)
                    cp(carrycol[:, 2 * k + 1:2 * k + 2], ps[:, 5, 0:1])
                    return carrycol[:, 2 * k + 1:2 * k + 2]

                v.wait_ge(order_copied, (l + 1) * (SG // 4))
                link(v.tensor_tensor_scan(o2, begin, o1, -BIG, ALU.add, ALU.max))
                c = carries(0, o2[:, L - 1:L], resetrow[0:1, 0, :])
                link(v.tensor_tensor_scan(o2, begin, o1, c, ALU.add, ALU.max))
                link(v.tensor_tensor_scan(o1[:, ::-1], end[:, ::-1], o2[:, ::-1], -BIG, ALU.add, ALU.max))
                c = carries(1, o1[:, 0:1], resetrow[0:1, 1, :])
                link(v.tensor_tensor_scan(o1[:, ::-1], end[:, ::-1], o2[:, ::-1], c, ALU.add, ALU.max))
                v.sem_inc(back_asked, 1)
                by_stretch = [t.rearrange("p s h -> p (s h)").rearrange("p (j x) -> p j x", j=JB)
                              for t in (logit[:, :, :], endmax)]
                for n in range(SG // 4):
                    v.wait_ge(back_copied, l * (SG // 4) + n + 1)
                    lg, m = (t[:, :, 4 * n * H:4 * (n + 1) * H] for t in by_stretch)
                    v.tensor_tensor(lg, lg, m, ALU.subtract).then_inc(maxima_taken, 1)

            def stage_orders(l):
                view = logit[:, :, :].rearrange("p (j g) h -> p g j h", j=JB)
                v.wait_ge(logit_made, (l + 1) * G)
                for n in range(SG // 4):
                    if n >= 2:
                        v.wait_ge(order_turned, l * (SG // 4) + n - 1)
                    v.tensor_copy(staged[:, n % 2, :].rearrange("p (g j h) -> p g j h", g=4, j=JB),
                                  view[:, 4 * n:4 * n + 4, :, :]).then_inc(order_staged, 1)

            for l in range(LAYERS):
                give_table(X[:, :, :])
                v.sem_inc(small_asked, 1)
                for w in range(W):
                    if w == 8:
                        stage(3 + l, 0, 0)
                    v.wait_ge(zn_summed, l * W + w + 1)
                    stt(prodself[:, w, :], ps[:, w % 8, 0:HC], 0.0, attrow[l][:, :], ALU.max, ALU.mult)
                    v.tensor_copy(lself[:, w, :], ps[:, w % 8, HC:ZC]).then_inc(zn_read, 1)
                selfsum = selfcol[:, 0, :, :]
                v.wait_ge(table_stored, 16 * (l + 4))
                link(v.tensor_reduce(selfsum.rearrange("p w h -> p (w h)"),
                                     prodself.rearrange("p w (h c) -> p (w h) c", h=H), AX.X, ALU.add))
                v.wait_ge(zn_read, (l + 1) * W)
                tt(lself[:, :, :], lself[:, :, :], selfsum, ALU.add)

                def back(i, b):
                    g = l * G + 2 * i + b
                    for k in range(4):
                        v.wait_ge(lin_copied, 4 * g + k + 1)
                        v.scalar_tensor_tensor(prod[b][:, 2 * k:2 * k + 2, :], pair(b, k)[:, :, 0:HC], 0.0,
                                               down(attrow[l][:, :], 2), ALU.max, ALU.mult).then_inc(prod_made, 1)
                    v.wait_ge(prod_made, 4 * g + 7)
                    sums = zsum[:, b, :]
                    v.tensor_reduce(sums, prod[b].rearrange("p j (h c) -> p (j h) c", h=H), AX.X, ALU.add
                                    ).then_inc(prod_summed, 1)
                    v.wait_ge(prod_summed, 2 * g + 1)
                    v.tensor_tensor(sums, sums, lin[:, b, :, :].rearrange("p j h -> p (j h)"), ALU.add
                                    ).then_inc(prod_summed, 1)
                    v.wait_ge(prod_summed, 2 * g + 2)
                    sl = bass.ds(16 * i + 8 * b, 8)
                    v.tensor_tensor(logit[:, sl, :], sums.rearrange("p (j h) -> p j h", h=H), wide(gone[:, sl], H),
                                    ALU.add).then_inc(logit_made, 1)
                pipelined(v, lambda f, k: (back(*k), stage(3 + l, *f)), lambda i, b: None, back)
                stage_orders(l)
                scans(l)

                def match(i, q, half):
                    v.tensor_tensor(hot[:, q % 2, 4 * half:4 * half + 4, :],
                                    wide(dloc[:, bass.ds(32 * i + 8 * q + 4 * half, 4)], P), down(iota[:, :], 4),
                                    ALU.is_equal).then_inc(halves_made, 1)

                def weigh_rows(i, q):
                    v.wait_ge(xs_in[q], 16 * (l * (G // 4) + i + 1))
                    weigh(v, i, q, 0, DVE_SLOTS).then_inc(px_made, 1)

                def step(add, make):
                    work = () if make is None else (lambda: match(*make, 0), lambda: match(*make, 1),
                                                    lambda: weigh_rows(*make))
                    if add is None:
                        for w in work:
                            w()
                    else:
                        i, q = add
                        add_steps(3 + l, 2 * i + q // 2, q % 2,
                                  [ps[:, 4 * (q % 2) + k, 0:HC + 2 * H] for k in range(4)], HC + 2 * H, work)

                v.wait_ge(weighed, l + 1)
                v.wait_ge(acc_zeroed, l + 1)
                step(None, (0, 0))
                step(None, (0, 1))
                with v.Fori(0, G // 4 - 1) as i:
                    step((i, 0), (i, 2))
                    step((i, 1), (i, 3))
                    step((i, 2), (i + 1, 0))
                    step((i, 3), (i + 1, 1))
                end = G // 4 - 1
                step((end, 0), (end, 2))
                step((end, 1), (end, 3))
                step((end, 2), None)
                step((end, 3), None)
                v.wait_ge(acc_added, 4 * G * (4 + l) + 1)

                a, s0, s1, m = (selfcol[:, k, :, :] for k in (2, 0, 1, 3))
                tt(a, acc[:, :, HC + H:HC + 2 * H], wide(empty[:, :], H), ALU.add)
                tt(m, a, lself[:, :, :], ALU.max)
                tt(s0, a, m, ALU.subtract)
                tt(s1, lself[:, :, :], m, ALU.subtract)
                v.sem_inc(exp_asked, 1)
                v.wait_ge(exp_done, l + 1)
                tt(a, acc[:, :, HC:HC + H], s0, ALU.mult)
                tt(a, a, s1, ALU.add)
                link(v.reciprocal(m, a))
                stt(s0, m, 1.0 / H, s0, ALU.mult, ALU.mult)
                stt(s1, m, 1.0 / H, s1, ALU.mult, ALU.mult)
                y4 = ysum.rearrange("p w (h c) -> p w h c", h=H)
                z4 = yself.rearrange("p w (h c) -> p w h c", h=H)
                tt(y4, acc[:, :, 0:HC].rearrange("p w (h c) -> p w h c", h=H),
                   s0.unsqueeze(3).broadcast_to([P, W, H, C]), ALU.mult)
                tt(z4, X[:, :, :].unsqueeze(2).broadcast_to([P, W, H, C]),
                   s1.unsqueeze(3).broadcast_to([P, W, H, C]), ALU.mult)
                tt(ysum, ysum, yself, ALU.add)
                v.sem_inc(y_asked, 1)
                v.wait_ge(y_summed, l + 1)
                for w, o in out_parts():
                    tt(T1[:, w, :], o, down(brow[l][:, 0, :], w.stop - w.start), ALU.add)
                if l < LAYERS - 1:
                    stt(T1[:, :, :], T1[:, :, :], 0.01, T1[:, :, :], ALU.mult, ALU.max)
                tt(T1[:, :, :], T1[:, :, :], X[:, :, :], ALU.add)
                ts(T1[:, W - 1, :], T1[:, W - 1, :], lastmask[:, 0:1], None, ALU.mult)
                link(v.tensor_reduce(bn[:, 0, :], T1[:, :, :].rearrange("p w c -> p c w"), AX.X, ALU.add))
                v.sem_inc(bn_asked, 1)
                v.wait_ge(bn_summed, 2 * l + 1)
                ts(bn[:, 0, :], ps[:, 1, 0:C], 1.0 / N, None, ALU.mult)
                tt(T2[:, :, :], T1[:, :, :], down(bn[:, 0, :], W), ALU.subtract)
                ts(T2[:, W - 1, :], T2[:, W - 1, :], lastmask[:, 0:1], None, ALU.mult)
                tt(rest[:, :, :], T2[:, :, :], T2[:, :, :], ALU.mult)
                link(v.tensor_reduce(bn[:, 0, :], rest[:, :, :].rearrange("p w c -> p c w"), AX.X, ALU.add))
                v.sem_inc(bn_asked, 1)
                v.wait_ge(bn_summed, 2 * l + 2)
                ts(bn[:, 1, :], ps[:, 2, 0:C], 1.0 / N, EPS, ALU.mult, ALU.add)
                rsqrt()
                tt(bn[:, 2, :], bn[:, 1, :], brow[l][:, 1, :], ALU.mult)
                tt(T2[:, :, :], T2[:, :, :], down(bn[:, 2, :], W), ALU.mult)
                tt(X[:, :, :], T2[:, :, :], down(brow[l][:, 2, :], W), ALU.add)

            tt(T1[:, :, :], X[:, :, :], X0[:, :, :], ALU.add)
            layernorm(T1[:, :, :])
            v.sem_inc(table_ready, 1)


def kernel(**inputs):
    import numpy as _np
    import concourse.bacc as _bacc
    from concourse import mybir as _mybir
    from concourse.bass_utils import run_bass_kernel_spmd as _run

    nc = _bacc.Bacc("TRN2", target_bir_lowering=False, num_devices=1)
    arrays = {}

    def given(name, a):
        a = _np.ascontiguousarray(a)
        arrays[f"in_{name}"] = a
        return nc.dram_tensor(f"in_{name}", a.shape, _mybir.dt.from_np(a.dtype), kind="ExternalInput").ap()

    src, dst = _np.asarray(inputs["src"]), _np.asarray(inputs["dst"])
    pad = BLOCKS * BLOCK - E
    none = _np.full(pad + 1, NO_NODE, dst.dtype)
    rows = [_np.concatenate([src, _np.zeros(pad, src.dtype)]), _np.concatenate([dst, none[1:]]),
            _np.concatenate([none[:1], dst, none[1:]])[:-1], _np.concatenate([dst[1:], none])]
    blocks = _np.stack([r.reshape(BLOCKS, BLOCK) for r in rows], axis=1).reshape(BLOCKS, ROWS * BLOCK)

    x = given("x", inputs["x"])
    edge_blocks = given("edge_blocks", blocks)
    L0 = [given(f"L0_{k}", inputs[f"L0_gnn_{k}"]) for k in ("W1", "b1", "W2", "b2", "W3", "b3", "W4", "b4")]
    W_gcn, b_gcn = given("W_gcn", inputs["L2_gnn_weight"]), given("b_gcn", inputs["L2_gnn_bias"])
    gat = [[given(f"{k}{l}", inputs[f"L3_gnn_{k}{l}"]) for k in ("Wl", "Wr", "att", "b", "g", "be")]
           for l in range(1, LAYERS + 1)]
    out = nc.dram_tensor("out_0", (N, C), _mybir.dt.from_np(_np.dtype("float32")), kind="ExternalOutput").ap()
    build(nc, x, edge_blocks, L0, W_gcn, b_gcn, gat, out)
    r = _run(nc, [arrays], core_ids=[0])
    return r.results[0]["out_0"]
```
